# Optimizing a Trainium2 kernel written in Bass

```python
import numpy as np
import jax
import jax.numpy as jnp

def _softmax(x, axis=-1):
    return jax.nn.softmax(x, axis=axis)

def _gelu(x):
    return jax.nn.gelu(x, approximate=True)

def _silu(x):
    return jax.nn.silu(x)

def _sigmoid(x):
    return jax.nn.sigmoid(x)

def _layernorm(x, axis=-1, eps=1e-05):
    m = jnp.mean(x, axis=axis, keepdims=True)
    v = jnp.var(x, axis=axis, keepdims=True)
    return (x - m) / jnp.sqrt(v + eps)

def _scatter_add(tgt, idx, src, axis=0):
    return tgt.at[idx].add(src)

def _segment_sum(src, seg, n):
    return jax.ops.segment_sum(src, seg, n)
kernel_name = 'mk_adaln_ffn_d2_seqx_r8_7d9d22'

def setup_inputs(seed: int=0):
    np.random.seed(seed)
    _w = jnp.asarray

    def _rec_inputs():
        import jax
        import jax.numpy as jnp
        _rk = jax.random.key(seed)
        x = 0.0001734 + 0.8201 * jax.random.normal(jax.random.fold_in(_rk, 1), (64, 32, 512), jnp.float32)
        _lenS = 32 - jax.random.randint(jax.random.fold_in(_rk, 7), (64,), 0, max(1, 32 // 4) + 1, jnp.int32)
        _lenS2 = 32 - jax.random.randint(jax.random.fold_in(_rk, 8), (64,), 0, max(1, 32 // 4) + 1, jnp.int32)
        itok_B_0_7 = jax.random.randint(jax.random.fold_in(_rk, 11), (64,), 0, 8, jnp.int32)
        itok_B_2182_4065 = jax.random.randint(jax.random.fold_in(_rk, 13), (64,), 2182, 4066, jnp.int32)
        itok_B_6_15 = jax.random.randint(jax.random.fold_in(_rk, 14), (64,), 6, 16, jnp.int32)
        return (x, itok_B_0_7, itok_B_2182_4065, itok_B_6_15, _lenS)
    x, itok_B_0_7, itok_B_2182_4065, itok_B_6_15, _lenS = _rec_inputs()

    def _L0_cond_setup():
        import jax, jax.numpy as jnp
        import numpy as np
        SESSION_CHANNELS = [128, 160, 192, 224, 240, 248, 252, 32]
        N_SESS = len(SESSION_CHANNELS)
        B, MAX_C, MAX_T = (16, 32, 512)
        HID, N_SRC = (64, 32)
        key = jax.random.key(seed)
        ks = jax.random.split(key, 7)
        session_ids = jax.random.randint(ks[0], (B,), 0, N_SESS)
        chan_table = jnp.asarray(SESSION_CHANNELS)
        channel_counts = chan_table[session_ids]
        seq_lens = jax.random.randint(ks[1], (B,), MAX_T // 2, MAX_T + 1)
        x = jax.random.normal(ks[2], (B, MAX_C, MAX_T), jnp.float32)
        cmask = (jnp.arange(MAX_C)[None, :] < channel_counts[:, None]).astype(x.dtype)
        tmask = (jnp.arange(MAX_T)[None, :] < seq_lens[:, None]).astype(x.dtype)
        x = x * cmask[:, :, None] * tmask[:, None, :]
        lim1 = 1.0 / np.sqrt(MAX_C)
        W_sess = jax.random.uniform(ks[3], (N_SESS, MAX_C, HID), jnp.float32, -lim1, lim1)
        b_sess = jax.random.uniform(ks[4], (N_SESS, HID), jnp.float32, -lim1, lim1)
        lim2 = 1.0 / np.sqrt(HID)
        W2 = jax.random.uniform(ks[5], (HID, N_SRC), jnp.float32, -lim2, lim2)
        b2 = jax.random.uniform(ks[6], (N_SRC,), jnp.float32, -lim2, lim2)
        return dict(x=x, session_ids=session_ids, channel_counts=channel_counts, seq_lens=seq_lens, W_sess=W_sess, b_sess=b_sess, W2=W2, b2=b2)
    _L0_cond_all = _L0_cond_setup()
    _L0_cond_in = {k: v for k, v in _L0_cond_all.items() if k in ('W_sess', 'b_sess', 'W2', 'b2')}
    del _L0_cond_all

    def _L0_ffn_setup():
        import jax, jax.numpy as jnp
        import numpy as np
        GROUP_SIZE = 128

        def dequantize(qweight, qzeros, scales):
            shifts = jnp.arange(8, dtype=jnp.int32) * 4
            out_features = qweight.shape[1]
            q = qweight[:, None, :] >> shifts[None, :, None] & 15
            q = q.reshape(-1, out_features)
            z = qzeros[:, :, None] >> shifts[None, None, :] & 15
            z = z.reshape(qzeros.shape[0], -1)
            G = scales.shape[0]
            W = (q.reshape(G, GROUP_SIZE, out_features).astype(jnp.float16) - z[:, None, :].astype(jnp.float16)) * scales[:, None, :]
            return W.reshape(-1, out_features)
        key = jax.random.key(seed)
        k1, k2, k3, k4, k5 = jax.random.split(key, 5)
        B, S, IN, OUT, G = (4, 256, 512, 512, 512 // GROUP_SIZE)
        x = jax.random.normal(k1, (B, S, IN), dtype=jnp.float16)
        qweight = jax.random.randint(k2, (IN // 8, OUT), 0, 2147483647, dtype=jnp.int32)
        qzeros = jax.random.randint(k3, (G, OUT // 8), 0, 2147483647, dtype=jnp.int32)
        scales = (jax.random.uniform(k4, (G, OUT), dtype=jnp.float32) * 0.01 + 0.001).astype(jnp.float16)
        bias = (jax.random.normal(k5, (OUT,), dtype=jnp.float32) * 0.02).astype(jnp.float16)
        return {'x': x, 'qweight': qweight, 'qzeros': qzeros, 'scales': scales, 'bias': bias}
    _L0_ffn_all = _L0_ffn_setup()
    _L0_ffn_in = {k: v for k, v in _L0_ffn_all.items() if k in ('qweight', 'qzeros', 'scales', 'bias')}
    del _L0_ffn_all

    def _L1_cond_setup():
        import jax, jax.numpy as jnp
        import numpy as np
        B, S, D_IN, D_OUT = (4, 256, 512, 512)
        RANK, MAX_LORAS = (16, 32)
        key = jax.random.key(seed)
        ks = jax.random.split(key, 6)
        x = jax.random.normal(ks[0], (B, S, D_IN), dtype=jnp.float32)
        adapter_ids = jax.random.randint(ks[1], (B,), 0, MAX_LORAS)
        base_weight = jax.random.normal(ks[2], (D_OUT, D_IN), dtype=jnp.float32) * D_IN ** (-0.5)
        base_bias = jax.random.normal(ks[3], (D_OUT,), dtype=jnp.float32) * 0.01
        lora_A_w = jax.random.normal(ks[4], (MAX_LORAS, RANK, D_IN), dtype=jnp.float32) * D_IN ** (-0.5)
        lora_B_w = jax.random.normal(ks[5], (MAX_LORAS, D_OUT, RANK), dtype=jnp.float32) * RANK ** (-0.5)
        return {'x': x, 'adapter_ids': adapter_ids, 'base_weight': base_weight, 'base_bias': base_bias, 'lora_A_w': lora_A_w, 'lora_B_w': lora_B_w}
    _L1_cond_all = _L1_cond_setup()
    _L1_cond_in = {k: v for k, v in _L1_cond_all.items() if k in ('base_weight', 'base_bias', 'lora_A_w', 'lora_B_w')}
    del _L1_cond_all

    def _L1_ffn_setup():
        import jax, jax.numpy as jnp
        import numpy as np
        NUM_EXPERTS = 8
        RANK = 32
        ALPHA = 16.0
        TOP_K = 2
        TEMPERATURE = 1.0
        GAMMA = 0.5
        SOFT_TOPK_TEMP = 0.5
        N_GRAM = 2
        EPS = 1e-06
        key = jax.random.key(seed)
        ks = jax.random.split(key, 6)
        d_in, d_out = (512, 512)
        Bsz, T = (4, 256)
        x = jax.random.normal(ks[0], (Bsz, T, d_in), dtype=jnp.float32)
        W = jax.random.normal(ks[1], (d_out, d_in), dtype=jnp.float32) / np.sqrt(d_in)
        b = jax.random.normal(ks[2], (d_out,), dtype=jnp.float32) * 0.01
        A = jax.random.normal(ks[3], (d_in, RANK), dtype=jnp.float32) / np.sqrt(d_in)
        Bmat = jax.random.normal(ks[4], (RANK, d_out), dtype=jnp.float32) * 0.01
        LiMEs = jax.random.normal(ks[5], (NUM_EXPERTS, RANK), dtype=jnp.float32) * 0.1
        return {'x': x, 'W': W, 'b': b, 'A': A, 'Bmat': Bmat, 'LiMEs': LiMEs}
    _L1_ffn_all = _L1_ffn_setup()
    _L1_ffn_in = {k: v for k, v in _L1_ffn_all.items() if k in ('W', 'b', 'A', 'Bmat', 'LiMEs')}
    del _L1_ffn_all
    return {'x': x, 'itok_B_0_7': itok_B_0_7, 'itok_B_2182_4065': itok_B_2182_4065, 'itok_B_6_15': itok_B_6_15, '_lenS': _lenS, 'L0_cond_W_sess': _L0_cond_in['W_sess'], 'L0_cond_b_sess': _L0_cond_in['b_sess'], 'L0_cond_W2': _L0_cond_in['W2'], 'L0_cond_b2': _L0_cond_in['b2'], 'L0_ffn_qweight': _L0_ffn_in['qweight'], 'L0_ffn_qzeros': _L0_ffn_in['qzeros'], 'L0_ffn_scales': _L0_ffn_in['scales'], 'L0_ffn_bias': _L0_ffn_in['bias'], 'L1_cond_base_weight': _L1_cond_in['base_weight'], 'L1_cond_base_bias': _L1_cond_in['base_bias'], 'L1_cond_lora_A_w': _L1_cond_in['lora_A_w'], 'L1_cond_lora_B_w': _L1_cond_in['lora_B_w'], 'L1_ffn_W': _L1_ffn_in['W'], 'L1_ffn_b': _L1_ffn_in['b'], 'L1_ffn_A': _L1_ffn_in['A'], 'L1_ffn_Bmat': _L1_ffn_in['Bmat'], 'L1_ffn_LiMEs': _L1_ffn_in['LiMEs']}

def reference(x, itok_B_0_7, itok_B_2182_4065, itok_B_6_15, _lenS, L0_cond_W_sess, L0_cond_b_sess, L0_cond_W2, L0_cond_b2, L0_ffn_qweight, L0_ffn_qzeros, L0_ffn_scales, L0_ffn_bias, L1_cond_base_weight, L1_cond_base_bias, L1_cond_lora_A_w, L1_cond_lora_B_w, L1_ffn_W, L1_ffn_b, L1_ffn_A, L1_ffn_Bmat, L1_ffn_LiMEs):
    import jax
    import jax.numpy as jnp

    def _L0_cond_ref(x, session_ids, channel_counts, seq_lens, W_sess, b_sess, W2, b2):
        import jax, jax.numpy as jnp
        import numpy as np
        SESSION_CHANNELS = [128, 160, 192, 224, 240, 248, 252, 32]
        N_SESS = len(SESSION_CHANNELS)
        B, MAX_C, MAX_T = (16, 32, 512)
        HID, N_SRC = (64, 32)
        cmask = (jnp.arange(x.shape[1])[None, :] < channel_counts[:, None]).astype(x.dtype)
        xm = x * cmask[:, :, None]
        W = W_sess[session_ids]
        b = b_sess[session_ids]
        h = jnp.einsum('bct,bch->bht', xm, W) + b[:, :, None]
        h = jax.nn.gelu(h, approximate=False)
        out = jnp.einsum('bht,hs->bst', h, W2) + b2[None, :, None]
        tmask = (jnp.arange(x.shape[2])[None, :] < seq_lens[:, None]).astype(x.dtype)
        return out * tmask[:, None, :]

    def _L0_ffn_ref(x, qweight, qzeros, scales, bias):
        import jax, jax.numpy as jnp
        import numpy as np
        GROUP_SIZE = 128

        def dequantize(qweight, qzeros, scales):
            shifts = jnp.arange(8, dtype=jnp.int32) * 4
            out_features = qweight.shape[1]
            q = qweight[:, None, :] >> shifts[None, :, None] & 15
            q = q.reshape(-1, out_features)
            z = qzeros[:, :, None] >> shifts[None, None, :] & 15
            z = z.reshape(qzeros.shape[0], -1)
            G = scales.shape[0]
            W = (q.reshape(G, GROUP_SIZE, out_features).astype(jnp.float16) - z[:, None, :].astype(jnp.float16)) * scales[:, None, :]
            return W.reshape(-1, out_features)
        W = dequantize(qweight, qzeros, scales)
        out = jnp.einsum('bsi,io->bso', x.astype(jnp.float16), W)
        return out + bias

    def _L1_cond_ref(x, adapter_ids, base_weight, base_bias, lora_A_w, lora_B_w):
        import jax, jax.numpy as jnp
        import numpy as np
        B, S, D_IN, D_OUT = (4, 256, 512, 512)
        RANK, MAX_LORAS = (16, 32)
        result = jnp.einsum('bsd,od->bso', x, base_weight) + base_bias
        A = lora_A_w[adapter_ids]
        Bw = lora_B_w[adapter_ids]
        h = jnp.einsum('bsd,brd->bsr', x, A)
        lora_out = jnp.einsum('bsr,bor->bso', h, Bw)
        result = result + lora_out
        return result.astype(x.dtype)

    def _L1_ffn_ref(x, W, b, A, Bmat, LiMEs):
        import jax, jax.numpy as jnp
        import numpy as np
        NUM_EXPERTS = 8
        RANK = 32
        ALPHA = 16.0
        TOP_K = 2
        TEMPERATURE = 1.0
        GAMMA = 0.5
        SOFT_TOPK_TEMP = 0.5
        N_GRAM = 2
        EPS = 1e-06
        Bsz, T, d_in = x.shape
        E = LiMEs.shape[0]
        scaling = ALPHA / RANK
        H = jnp.einsum('btd,od->bto', x, W) + b
        z = jnp.einsum('btd,dr->btr', x, A)
        anchors = jnp.arange(N_GRAM - 1, T, N_GRAM)
        H_slice = H[:, anchors, :E]
        delta_slice = jnp.einsum('bar,er->bae', z[:, anchors], LiMEs)
        H_scale = jnp.maximum(jnp.max(jnp.abs(H_slice)), EPS)
        d_scale = jnp.maximum(jnp.max(jnp.abs(delta_slice)), EPS)
        logits = ((1.0 - GAMMA) * (H_slice / H_scale) + GAMMA * (delta_slice / d_scale)) / TEMPERATURE
        probs = jax.nn.softmax(logits, axis=-1)
        topk_vals, _ = jax.lax.top_k(probs, TOP_K)
        thresh = topk_vals[..., -1:]
        mask = jax.nn.sigmoid((probs - thresh) / SOFT_TOPK_TEMP)
        weights = probs * mask
        weights = weights / (jnp.sum(weights, axis=-1, keepdims=True) + 1e-09)
        weights_full = jnp.repeat(weights, N_GRAM, axis=1)
        p_mix = jnp.einsum('bte,er->btr', weights_full, LiMEs)
        delta = jnp.einsum('btr,ro->bto', z * p_mix, Bmat) * scaling
        return H + delta
    x = x + _L0_ffn_ref(_L0_cond_ref(x, itok_B_0_7, _lenS, itok_B_2182_4065, L0_cond_W_sess, L0_cond_b_sess, L0_cond_W2, L0_cond_b2), L0_ffn_qweight, L0_ffn_qzeros, L0_ffn_scales, L0_ffn_bias)
    x = x + _L1_ffn_ref(_L1_cond_ref(x, itok_B_6_15, L1_cond_base_weight, L1_cond_base_bias, L1_cond_lora_A_w, L1_cond_lora_B_w), L1_ffn_W, L1_ffn_b, L1_ffn_A, L1_ffn_Bmat, L1_ffn_LiMEs)
    return x

_drawn_inputs = setup_inputs


def setup_inputs(seed=0):
    import zlib

    import numpy as np

    out = dict(_drawn_inputs(seed))
    spreads = {}
    factors = {'L0_ffn_bias': 3.291,
     'L1_cond_base_bias': 8.0,
     'L1_ffn_b': 8.0,
     'L1_ffn_A': 8.0,
     'L1_ffn_Bmat': 8.0,
     'L1_ffn_LiMEs': 8.0}
    for name, (base, spread) in spreads.items():
        noise = np.random.default_rng([zlib.crc32(name.encode()), seed]).standard_normal(out[name].shape)
        drawn = base * np.exp(spread * noise) if base else spread * noise
        out[name] = jnp.asarray(drawn.astype(out[name].dtype))
    for name, factor in factors.items():
        out[name] = (out[name] * factor).astype(out[name].dtype)
    return out
```

```python
from contextlib import ExitStack

import concourse.bass as bass
from concourse import mybir

F32 = mybir.dt.float32
F32R = mybir.dt.float32r
F16 = mybir.dt.float16
I32 = mybir.dt.int32
ALU = mybir.AluOpType
ACT = mybir.ActivationFunctionType
AX = mybir.AxisListType

P = 128


def adaln_ffn_program(nc, x, sess_ids, seq_lens, lora_ids, chan_counts, W_sess, b_sess, W2, b2,
                      qweight, qzeros, scales, bias16_in, Wb, bb, lora_A, lora_B, W, b, A, Bmat, LiMEs, out):
    NB, C, D = x.shape
    NT = NB * C // P
    BT = P // C
    NS, _, HID = W_sess.shape
    NA, RK, _ = lora_A.shape
    KC = D // P
    R32, NE = A.shape[1], LiMEs.shape[0]
    RH = BT * RK
    NZ = 2 * NE + R32
    AZW = RH + NZ
    NX = 2 * KC + 1
    EPS, WEPS = 1e-6, 1e-9
    DEPTH = 3

    x_rows = x.rearrange("b c t -> (b c) t")
    out_rows = out.rearrange("b c t -> (b c) t")
    L_hi_dram = nc.dram_tensor("L_hi_dram", [NA * RK, D], F32).ap()
    L_lo_dram = nc.dram_tensor("L_lo_dram", [NA * RK, D], F32).ap()
    L_z_dram = nc.dram_tensor("L_z_dram", [NA * RK, 2 * NZ], F32).ap()

    with ExitStack() as ctx:
        def sb(name, shape, dt):
            return ctx.enter_context(nc.sbuf_tensor(name, shape, dt))

        def sem(name):
            return ctx.enter_context(nc.semaphore(name))

        x_all = sb("x_all", [P, NT, D], F32)
        xT_all = sb("xT_all", [P, NT, NX, P], F32R)
        ATG = sb("ATG", [P, 2, KC, D], F32R)
        WT = sb("WT", [P, 2, KC, D], F32R)
        Wbs = sb("Wbs", [P, 2, KC, D], F32R)
        xT = sb("xT", [P, 2, NX, P], F32R)
        az = sb("az", [P, 2048], F32R)
        gel = sb("gel", [P, 2, D], F32)
        x1s = sb("x1s", [P, 2, D], F32)
        W16 = sb("W16", [P, KC, D], F16)
        c16 = sb("c16", [P, D], F16)
        cT16 = sb("cT16", [P, D], F16)
        f16 = sb("f16", [P, D], F16)
        mask16 = sb("mask16", [P, D], F16)
        iota16 = sb("iota16", [P, D], F16)
        bias16 = sb("bias16", [P, D], F16)
        wsel = sb("wsel", [P, 2, HID], F32)
        wbd = sb("wbd", [P, 2, BT, HID], F32)
        lz = sb("lz", [P, 2, 2 * NZ], F32R)
        crow = sb("crow", [P, D], F32)
        cz = sb("cz", [P, NZ], F32)
        zall = sb("zall", [P, NT, NZ], F32)
        Bstk = sb("Bstk", [P, D], F32R)
        Rz = sb("Rz", [P, 2, KC, NZ], F32R)
        ident = sb("ident", [P, P], F32)
        ident16 = sb("ident16", [P, P], F16)
        ids_i = sb("ids_i", [P, 4, NB], I32)
        ids_f = sb("ids_f", [P, 4, NB], F32)
        m32 = sb("m32", [P, BT], F32)
        m16 = sb("m16", [P, 2, BT], F32)
        hmask = sb("hmask", [P, BT, RK], F32)
        blk = sb("blk", [P, NT, NE], F32)
        sel = sb("sel", [P, 5, NT], F32)
        idx_w = sb("idx_w", [P, NT], I32)
        idx_l = sb("idx_l", [P, NT], I32)
        idxw = sb("idxw", [P, 2], I32)
        idxl = sb("idxl", [P, 2], I32)
        pid_i = sb("pid_i", [P, 4], I32)
        pid_f = sb("pid_f", [P, 4], F32)
        mch = sb("mch", [P, NT, BT], F32)
        bsess = sb("bsess", [P, NT * 2], F32)
        W2bd = sb("W2bd", [P, 2, C], F32)
        b2col = sb("b2col", [P, 1], F32)
        fA = sb("fA", [P, KC, R32], F32)
        liT = sb("liT", [R32, NE], F32)
        bb_raw = sb("bb_raw", [P, KC], F32)
        bz = sb("bz", [P, NE], F32)
        hmf = sb("hmf", [P, RH], F32)
        hs = sb("hs", [P, 2, P], F32)
        zT = sb("zT", [P, 2, P], F32R)
        small = sb("small", [P, 16], F32)
        oddp = sb("oddp", [P, 1], F32)
        ones2 = sb("ones2", [2, P], F32)

        W_raw = x_all[:, 8:12, :]
        Wb_raw = x_all[:, 8:12, :]
        lA_raw = x_all[:, 12:16, :]
        lB_raw = x_all[:, 4:8, :].rearrange("p s (a j r) -> p (s a) j r", j=KC, r=RK)
        xT_flat = xT_all[:, :, :, :].rearrange("p t k c -> p (t k c)")
        lBs = xT_flat[:, 12 * NX * P:12 * NX * P + 2 * KC * D].rearrange("p (s j n) -> p s j n", s=2, j=KC)
        bbB = xT_flat[:, 11 * NX * P:11 * NX * P + 2 * KC * P].rearrange("p (s j n) -> p s j n", s=2, j=KC)
        q_i = gel[:, 0, :].bitcast(I32)
        q_nib = gel[:, 1, :].bitcast(I32)
        zero16, scale16, qz16 = c16, cT16, f16
        L_st = xT[:, :, :, :].rearrange("p s k c -> p s (k c)")
        azv = az[:, 0:2 * 2 * KC * AZW].rearrange("p (b s k w) -> p b s k w", b=2, s=2, k=KC)
        L_hi = az[:, 0:2 * D].rearrange("p (b n) -> p b n", b=2)
        L_lo = az[:, 2 * D:4 * D].rearrange("p (b n) -> p b n", b=2)
        BD = gel[:, 0, :]
        zw = gel[:, 1, :].rearrange("p (t r) -> p t r", t=NT)
        rt = x1s[:, :, :].rearrange("p a (b n) -> p (a b) n", n=NT * NE)
        lrow = sb("lrow", [P, R32], F32)
        bm_raw = x1s[:, 0, :]
        onehot, b_raw = hs[0:NS, 0, 0:NB], hs[0:NS, 1, 0:HID]
        li_raw = hmf[0:NE, 0:R32]
        qz_i = x1s[:, 1, 0:D // 8].bitcast(I32)
        fAT = x1s[0:R32, 1, :].rearrange("r (j p) -> r j p", j=KC)

        ps = [ctx.enter_context(nc.psum_tensor(f"ps{i}", [P, D], F32)) for i in range(7)]
        ps_ct = ctx.enter_context(nc.psum_tensor("ps_ct", [P, 2 * D], F16))
        ps_hid, ps_c, ps_f, ps_x, ps_z = ps[0:2], ps[2], ps[3], ps[4], ps[5]
        ps_s = ps[6]

        names_dma = ["ids", "w2", "bsess_in", "W", "fA", "li", "q", "qz", "sc", "bias", "lA", "lB", "Wb", "bb",
                     "crow_in", "bz_in", "Bm", "lrow", "x0", "x1", "x2", "x3"]
        dma = {n: sem("dma_" + n) for n in names_dma}
        s_L_st = [sem("L_stored0"), sem("L_stored1")]
        s_const, s_ids, s_deq, s_setup_ps, s_setup_hi, s_setup_lo = (sem(n) for n in (
            "const_ready", "ids_ready", "dequant_done", "setup_psum", "setup_hi", "setup_lo"))
        s_lB_hi, s_lB_lo, s_Wb_hi, s_Wb_lo = (sem(n) for n in ("lB_hi", "lB_lo", "Wb_hi", "Wb_lo"))
        s_sp, s_sv = sem("small_psum"), sem("small_evac")
        s_chain = sem("dve_chain")
        s_bbB = sem("bbB_ready")
        s_bst = sem("Bmat_split")
        s_pool = sem("pool_chain")
        s_lzp = sem("L_z_psum")
        s_gate = sem("gather_gate")
        s_wg = [sem("wsel_in0"), sem("wsel_in1")]
        s_lzd = [sem("lz_in0"), sem("lz_in1")]
        s_idxw, s_idxl, s_wbd, s_az = sem("idxw_ready"), sem("idxl_ready"), sem("wbd_ready"), sem("az_ready")
        s_hid, s_gelu, s_cond, s_mask, s_c16, s_ctp, s_cT, s_ffn, s_f16, s_b16, s_x1, s_xTp, s_hi, s_lo = (
            sem(n) for n in ("hid_psum", "gelu_done", "cond_psum", "tmask", "c16_ready", "ct_psum", "cT_ready",
                             "ffn_psum", "f16_ready", "f16_biased", "x1_ready", "x1T_psum", "x1T_hi", "x1T_lo"))
        s_hz, s_hm, s_hh, s_hs, s_hTp, s_hT, s_l48, s_zh = (
            sem(n) for n in ("hz_psum", "h_masked", "h_hi", "hs_ready", "hT_psum", "hT_ready", "z_psum", "z_ready"))
        s_x1st = [sem("x1_stored0"), sem("x1_stored1")]
        s_xTst = [sem("xT_stored0"), sem("xT_stored1")]
        s_rp, s_ra, s_rv = sem("routing_psum"), sem("routing_act"), sem("routing_dve")
        s_Gp, s_Ghi, s_Glo = sem("G_psum"), sem("G_hi"), sem("G_lo")
        s_li, s_lhd, s_lld = sem("L_idx"), [sem("L_hi_in0"), sem("L_hi_in1")], [sem("L_lo_in0"), sem("L_lo_in1")]
        s_xc, s_xb, s_zph, s_zs, s_zTp, s_zTs, s_main, s_out_r = (
            sem(n) for n in ("xT_copied", "x1_biased", "zp_hi", "zp_split", "zT_psum", "zT_ready", "main_psum", "out_ready"))
        s_out = sem("out_stored")
        block = ctx.enter_context(nc.Block())

        BSESS, LIT, D2, GZ, CZ, CROW = 1, 2, 3, 4, 5, 6
        R_MAX, R_SCALE, R_LOGITS, R_DIFF, R_W, R_WT = 1, 2, 3, 4, 5, 6

        class Step:

            def __init__(self, k, c):
                self.k, self.c = k, c

            def on(self, s):
                return not isinstance(self.k, int) or 0 <= self.c - s < NT

            def tile(self, s, plus=0):
                return 2 * self.k + (self.c - s + plus)

            def half(self, s, plus=0):
                return self.k + ((self.c - s) // 2 + plus)

            def par(self, s):
                return (self.c - s) % 2

            def past(self, s, back):
                return not isinstance(self.k, int) or self.c - s - back >= 0

        FIRST = DEPTH
        LAST = NT - 1

        def run_phase_a(eng, body):
            for n in range(FIRST):
                body(Step(0, n))
            with eng.Fori(0, (LAST - FIRST) // 2) as k:
                body(Step(k, FIRST))
                body(Step(k, FIRST + 1))
            for n in range(LAST, NT + DEPTH):
                body(Step(0, n))

        @block.sync
        def _(sp):
            for i, ids in enumerate((sess_ids, seq_lens, lora_ids, chan_counts)):
                sp.dma_start(ids_i[:, i, :], ids.rearrange("(a n) -> a n", a=1).to_broadcast([P, NB])).then_inc(dma["ids"], 16)
            sp.dma_start(W_raw, W.rearrange("(m p) o -> p m o", p=P)).then_inc(dma["W"], 16)
            for h in range(2):
                sp.dma_start(q_i[64 * h:64 * h + 64, :], qweight).then_inc(dma["q"], 16)
                for g in range(KC):
                    at = 64 * h + 16 * g
                    sp.dma_start(qz_i[at:at + 16, :], qzeros[g:g + 1, :].to_broadcast([16, D // 8])).then_inc(dma["qz"], 16)
                    sp.dma_start(scale16[at:at + 16, :], scales[g:g + 1, :].to_broadcast([16, D])).then_inc(dma["sc"], 16)
            sp.dma_start(x_all[:, 0:4, :], x_rows[0:4 * P, :].rearrange("(a p) t -> p a t", p=P)).then_inc(dma["x0"], 16)
            sp.dma_start(bias16[:, :], bias16_in.rearrange("(a n) -> a n", a=1).to_broadcast([P, D])).then_inc(dma["bias"], 16)
            sp.dma_start(lA_raw, lora_A.rearrange("a r d -> (a r) d").rearrange("(m p) d -> p m d", p=P)).then_inc(dma["lA"], 16)
            sp.dma_start(lB_raw.rearrange("p a j r -> p a (j r)"),
                         lora_B.rearrange("a (p j) r -> p a (j r)", j=KC)).then_inc(dma["lB"], 16)
            sp.wait_ge(s_setup_ps, KC)
            sp.dma_start(Wb_raw, Wb.rearrange("(p j) d -> p j d", j=KC)).then_inc(dma["Wb"], 16)
            sp.wait_ge(s_setup_ps, 2 * KC)
            sp.dma_start(x_all[:, 12:16, :], x_rows[12 * P:16 * P, :].rearrange("(a p) t -> p a t", p=P)).then_inc(dma["x3"], 16)
            sp.wait_ge(s_lB_lo, KC)
            sp.dma_start(x_all[:, 4:8, :], x_rows[4 * P:8 * P, :].rearrange("(a p) t -> p a t", p=P)).then_inc(dma["x1"], 16)
            sp.wait_ge(s_Wb_lo, KC)
            sp.dma_start(x_all[:, 8:12, :], x_rows[8 * P:12 * P, :].rearrange("(a p) t -> p a t", p=P)).then_inc(dma["x2"], 16)
            for m in range(KC):
                rows = slice(m * P, (m + 1) * P)
                sp.wait_ge(s_setup_lo, 2 * KC + m + 1)
                st = L_st[:, m % 2, :].bitcast(F32)
                sp.dma_start(L_z_dram[rows, :], st[:, 2 * D:2 * D + 2 * NZ]).then_inc(s_L_st[m % 2], 16)
                sp.dma_start(L_hi_dram[rows, :], st[:, 0:D]).then_inc(s_L_st[m % 2], 16)
                sp.dma_start(L_lo_dram[rows, :], st[:, D:2 * D]).then_inc(s_L_st[m % 2], 16)

            def stores(n):
                if n.on(2):
                    sp.wait_ge(s_x1, n.tile(2, 1))
                    sp.dma_start(x_all[:, n.tile(2), :], x1s[:, n.par(2), :]).then_inc(s_x1st[n.par(2)], 16)
                if n.on(3):
                    sp.wait_ge(s_hT, n.tile(3, 1))
                    sp.dma_start(xT_all[:, n.tile(3), :, :].bitcast(F32), xT[:, n.par(3), :, :].bitcast(F32)).then_inc(s_xTst[n.par(3)], 16)
            run_phase_a(sp, stores)

            with sp.Fori(0, NT) as t:
                sp.wait_ge(s_out_r, t + 1)
                sp.dma_start(out_rows[bass.ts(t, P), :], x_all[:, t, :]).then_inc(s_out, 16)
            sp.wait_ge(s_out, 16 * NT)

        @block.gpsimd
        def _(pool):
            count = [0]

            def link(ins):
                count[0] += 1
                ins.then_inc(s_pool, 1)
                pool.wait_ge(s_pool, count[0])

            def band(ap, pattern, width, mult=1, base=0):
                link(nc.gpsimd.affine_select(out=ap, in_=ap, compare_op=ALU.is_ge, fill=0.0, base=base,
                                             pattern=pattern, channel_multiplier=mult))
                link(nc.gpsimd.affine_select(out=ap, in_=ap, compare_op=ALU.is_ge, fill=0.0, base=width - 1 - base,
                                             pattern=[[-s, c] for s, c in pattern], channel_multiplier=-mult))

            link(nc.gpsimd.iota(pid_i[:, 0:1], pattern=[[0, 1]], base=0, channel_multiplier=1))
            link(nc.gpsimd.memset(m32[:, :], 1.0))
            band(m32[:, :], [[-C, BT]], C)
            link(nc.gpsimd.memset(m16[:, :, :], 1.0))
            band(m16[:, :, :], [[-P // 2, 2], [-RK, BT]], RK)
            link(nc.gpsimd.memset(ident[:, :], 0.0))
            link(nc.gpsimd.affine_select(out=ident[:, :], in_=ident[:, :], compare_op=ALU.not_equal, fill=1.0, base=0,
                                         pattern=[[-1, P]], channel_multiplier=1))
            link(nc.gpsimd.memset(W2bd[:, :, :], 0.0))
            link(nc.gpsimd.iota(iota16[:, :], pattern=[[1, D]], base=0, channel_multiplier=0,
                                allow_small_or_imprecise_dtypes=True))
            link(nc.gpsimd.memset(hmask[:, :, :], 1.0))
            band(hmask[:, :, :], [[-C, BT], [0, RK]], C)
            link(nc.gpsimd.memset(blk[:, :, :], 1.0))
            band(blk[:, :, :], [[-NE, NT], [0, NE]], NE)
            nc.gpsimd.memset(ones2[:, :], 1.0).then_inc(s_const, 1)
            for h in range(2):
                pool.dma_start(W2bd[HID * h:HID * h + HID, h, :], W2).then_inc(dma["w2"], 16)
            for j in range(BT):
                pool.dma_start(b2col[C * j:C * j + C, :], b2.rearrange("(n a) -> n a", a=1)).then_inc(dma["w2"], 16)
            pool.dma_start(b_raw[:, :], b_sess).then_inc(dma["bsess_in"], 16)
            pool.dma_start(fA[:, :, :], A.rearrange("(p j) r -> p j r", j=KC)).then_inc(dma["fA"], 16)
            pool.dma_start(li_raw[:, :], LiMEs).then_inc(dma["li"], 16)
            pool.dma_start(bb_raw[:, :], bb.rearrange("(p j) -> p j", j=KC)).then_inc(dma["bb"], 16)
            pool.dma_start(bz[:, :], b.rearrange("(a n) -> a n", a=1)[:, 0:NE].to_broadcast([P, NE])).then_inc(dma["bz_in"], 16)
            pool.dma_start(crow[:, :], b.rearrange("(a n) -> a n", a=1).to_broadcast([P, D])).then_inc(dma["crow_in"], 16)
            for j in range(BT):
                pool.dma_start(bm_raw[R32 * j:R32 * j + R32, :], Bmat).then_inc(dma["Bm"], 16)
            for j in range(BT):
                for e in range(C // NE):
                    at = C * j + NE * e
                    pool.dma_start(lrow[at:at + NE, :], LiMEs).then_inc(dma["lrow"], 16)

            def gather_w(n, s):
                t, par = n.tile(s), n.par(s)
                if n.past(s, 2):
                    pool.wait_ge(s_wg[par], 16 * n.half(s))
                    pool.wait_ge(s_wbd, n.tile(s, -1))
                nc.gpsimd.tensor_copy(idxw[:, par:par + 1], idx_w[:, bass.ds(t, 1)]).then_inc(s_idxw, 1)
                pool.wait_ge(s_idxw, n.tile(s, 1))
                pool.sem_inc(s_gate, 1)
                nc.gpsimd.indirect_dma_start(
                    wsel[:, par, :], None, W_sess.rearrange("s c h -> (s c) h"),
                    bass.IndirectOffsetOnAxis(idxw[:, par:par + 1], 0)).then_inc(s_wg[par], 16)

            def make_wbd(n, s):
                t, par = n.tile(s), n.par(s)
                pool.wait_ge(s_wg[par], 16 * n.half(s, 1))
                if n.past(s, 2):
                    pool.wait_ge(s_hid, 2 * n.tile(s, -1))
                nc.gpsimd.tensor_tensor(
                    wbd[:, par, :, :], wsel[:, par, :].unsqueeze(1).to_broadcast([P, BT, HID]),
                    mch[:, t, :].unsqueeze(2).to_broadcast([P, BT, HID]), ALU.mult).then_inc(s_wbd, 1)

            def gather_a(n, s):
                t, par = n.tile(s), n.par(s)
                if n.past(s, 2):
                    pool.wait_ge(s_hz, n.tile(s, -1))
                for j in range(BT):
                    a = pool.value_load(ids_i[0:1, 2, bass.ds(4 * t + j, 1)], min_val=0, max_val=NA - 1)
                    last = nc.gpsimd.tensor_copy(
                        azv[:, par, :, :, RK * j:RK * j + RK].rearrange("p s k w -> p (s k) w"),
                        ATG[:, :, :, bass.ds(a * RK, RK)].rearrange("p s k w -> p (s k) w"))
                    if j < BT - 1:
                        last.then_inc(s_pool, 1)
                last.then_inc(s_az, 1)

            def gather_lz(n, s):
                t, par = n.tile(s), n.par(s)
                if n.past(s, 2):
                    pool.wait_ge(s_lzd[par], 16 * n.half(s))
                    pool.wait_ge(s_l48, n.tile(s, -1))
                nc.gpsimd.tensor_copy(idxl[:, par:par + 1], idx_l[:, bass.ds(t, 1)]).then_inc(s_idxl, 1)
                pool.wait_ge(s_idxl, n.tile(s, 1))
                pool.sem_inc(s_gate, 1)
                nc.gpsimd.indirect_dma_start(
                    lz[:, par, :].bitcast(F32), None, L_z_dram,
                    bass.IndirectOffsetOnAxis(idxl[:, par:par + 1], 0)).then_inc(s_lzd[par], 16)

            pool.wait_ge(s_ids, 1)
            gather_w(Step(0, 0), 0)
            make_wbd(Step(0, 0), 0)

            def gathers(n):
                if n.on(-1):
                    gather_w(n, -1)
                if isinstance(n.k, int) and n.c == 2:
                    pool.wait_ge(s_setup_lo, 2 * KC)
                    pool.wait_ge(s_sv, GZ)
                    for m in range(2):
                        pool.wait_ge(s_L_st[m], 16 * 3 * 2)
                if n.on(2):
                    gather_lz(n, 2)
                    gather_a(n, 2)
                if n.on(-1):
                    make_wbd(n, -1)
            run_phase_a(pool, gathers)

            for par in range(2):
                pool.wait_ge(s_x1st[par], 16 * NT // 2)
                pool.wait_ge(s_lzd[par], 16 * NT // 2)
            pool.wait_ge(s_hz, NT)
            with pool.Fori(0, NT // 2) as k:
                for u in range(2):
                    t = 2 * k + u
                    if True:
                        pool.wait_ge(s_main, t)
                    nc.gpsimd.tensor_copy(idxl[:, u:u + 1], idx_l[:, bass.ds(t, 1)]).then_inc(s_li, 1)
                    pool.wait_ge(s_li, t + 1)
                    pool.sem_inc(s_gate, 1)
                    nc.gpsimd.indirect_dma_start(L_hi[:, u, :].bitcast(F32), None, L_hi_dram,
                                                 bass.IndirectOffsetOnAxis(idxl[:, u:u + 1], 0)).then_inc(s_lhd[u], 16)
                    nc.gpsimd.indirect_dma_start(L_lo[0:RH, u, :].bitcast(F32), None, L_lo_dram,
                                                 bass.IndirectOffsetOnAxis(idxl[0:RH, u:u + 1], 0)).then_inc(s_lld[u], 16)
                    nc.gpsimd.tensor_tensor(x_all[:, t, :], x_all[:, t, :], crow[:, :], ALU.add).then_inc(s_xb, 1)
                    pool.wait_ge(s_lhd[u], 16 * k + 16)
                    pool.wait_ge(s_lld[u], 16 * k + 16)

        @block.scalar
        def _(act):
            def copy(dst, src):
                return nc.scalar.activation(dst, src, ACT.Copy)

            def setup_hi(k, dst, src):
                act.wait_ge(s_setup_ps, k + 1)
                copy(dst, src).then_inc(s_setup_hi, 1)

            for j in range(KC):
                setup_hi(j, WT[:, 0, j, :], ps[j % 4][:, :])
            act.wait_ge(dma["lB"], 16)
            for j in range(KC):
                copy(lBs[:, 0, j, :].rearrange("p (a r) -> p a r", r=RK), lB_raw[:, :, j, :]).then_inc(s_lB_hi, 1)
            for j in range(KC):
                setup_hi(KC + j, ATG[:, 0, j, :], ps[j % 4][:, :])
            act.wait_ge(dma["Wb"], 16)
            for j in range(KC):
                copy(Wbs[:, 0, j, :], Wb_raw[:, j, :]).then_inc(s_Wb_hi, 1)
            for m in range(KC):
                if m >= 2:
                    act.wait_ge(s_L_st[m % 2], 48)
                act.wait_ge(s_setup_ps, 2 * KC + m + 1)
                copy(L_st[:, m % 2, 0:D], ps[m % 4][:, :]).then_inc(s_setup_hi, 1)

            def stages(n):
                if n.on(2):
                    act.wait_ge(s_ffn, n.tile(2, 1))
                    if n.past(2, 1):
                        act.wait_ge(s_x1, n.tile(2))
                    copy(f16[:, :], ps_f[:, :]).then_inc(s_f16, 1)
                if n.on(3):
                    act.wait_ge(s_hTp, n.tile(3, 1))
                    copy(xT[:, n.par(3), NX - 1, :], ps_x[:, 0:P]).then_inc(s_hT, 1)
                for p in range(2):
                    if n.on(0):
                        act.wait_ge(s_hid, 2 * n.tile(0) + p + 1)
                        if isinstance(n.k, int) and n.c == 0 and p == 0:
                            act.wait_ge(s_deq, 1)
                            act.wait_ge(s_sv, BSESS)
                        if n.past(0, 1):
                            act.wait_ge(s_cond, n.tile(0))
                        nc.scalar.activation(gel[:, p, :], ps_hid[p][:, :], ACT.Gelu,
                                             bias=bsess[:, bass.ds(2 * n.tile(0) + p, 1)]).then_inc(s_gelu, 1)
                    if p == 0 and n.on(2):
                        act.wait_ge(s_xTp, n.tile(2, 1))
                        if isinstance(n.k, int) and n.c == 2:
                            for m in range(2):
                                act.wait_ge(s_L_st[m], 48 * KC // 2)
                        if n.past(2, 2):
                            act.wait_ge(s_xTst[n.par(2)], 16 * n.half(2))
                            act.wait_ge(s_l48, n.tile(2, -1))
                        copy(xT[:, n.par(2), 0:KC, :].rearrange("p k c -> p (k c)"), ps_x[:, :]).then_inc(s_hi, 1)
            run_phase_a(act, stages)

            act.wait_ge(s_rv, R_LOGITS)
            nc.scalar.activation(rt[:, 1, :], rt[:, 0, :], ACT.Exp).then_inc(s_ra, 1)
            for k in range(2):
                act.wait_ge(s_Gp, k + 1)
                if k == 0:
                    act.wait_ge(s_az, NT)
                copy(ATG[:, 0, k, :], ps[k % 2][:, :]).then_inc(s_Ghi, 1)
            act.wait_ge(s_rv, R_DIFF)
            nc.scalar.activation(rt[:, 3, :], rt[:, 4, :], ACT.Exp, scale=-2.0).then_inc(s_ra, 1)
            for k in range(2, KC):
                act.wait_ge(s_Gp, k + 1)
                copy(ATG[:, 0, k, :], ps[k % 2][:, :]).then_inc(s_Ghi, 1)
            with act.Fori(0, NT // 2) as k:
                for u in range(2):
                    t = 2 * k + u
                    act.wait_ge(s_zTp, t + 1)
                    act.wait_ge(s_main, t)
                    copy(zT[:, u, :], ps_z[:, 0:P]).then_inc(s_zTs, 1)

        @block.vector
        def _(dve):
            count = [0]

            def link(ins):
                count[0] += 1
                ins.then_inc(s_chain, 1)
                dve.wait_ge(s_chain, count[0])

            def tt(o, a, bb_, op):
                return nc.vector.tensor_tensor(o, a, bb_, op)

            def ts_(o, a, s1, s2, op0, op1=None):
                return nc.vector.tensor_scalar(o, a, s1, s2, op0, op1) if op1 is not None else \
                    nc.vector.tensor_scalar(o, a, s1, None, op0)

            def stt(o, a, s, c, op0, op1):
                return nc.vector.scalar_tensor_tensor(out=o, in0=a, scalar=s, in1=c, op0=op0, op1=op1)

            def lo_of(dst, src, hi):
                return tt(dst, src, hi.bitcast(F32), ALU.subtract)

            dve.wait_ge(s_const, 1)
            nc.vector.tensor_copy(ident16[:, :], ident[:, :]).then_inc(s_const, 1)
            link(ts_(pid_i[:, 1:2], pid_i[:, 0:1], C - 1, None, ALU.bitwise_and))
            link(ts_(pid_i[:, 2:3], pid_i[:, 0:1], RK - 1, None, ALU.bitwise_and))
            link(ts_(pid_i[:, 3:4], pid_i[:, 0:1], 1, None, ALU.bitwise_and))
            link(nc.vector.tensor_copy(pid_f[:, :], pid_i[:, :]))
            link(nc.vector.tensor_copy(oddp[:, :], pid_f[:, 3:4]))
            link(tt(m16[:, 0, :], m16[:, 0, :], m16[:, 1, :], ALU.add))
            dve.wait_ge(dma["ids"], 64)
            link(nc.vector.tensor_copy(ids_f[:, :, :], ids_i[:, :, :]))
            for i, m in enumerate((m32, m32, m16[:, 0, :], m32)):
                ids = ids_f[:, i, :].rearrange("p (t j) -> p t j", j=BT)
                link(ts_(sel[:, i, :], ids[:, :, 0], m[:, 0:1], None, ALU.mult))
                for j in range(1, BT):
                    link(stt(sel[:, i, :], ids[:, :, j], m[:, j:j + 1], sel[:, i, :], ALU.mult, ALU.add))
            link(ts_(sel[:, 4, :], sel[:, 0, :], float(C), pid_f[:, 1:2], ALU.mult, ALU.add))
            link(nc.vector.tensor_copy(idx_w[:, :], sel[:, 4, :]))
            link(ts_(sel[:, 4, :], sel[:, 2, :], float(RK), pid_f[:, 2:3], ALU.mult, ALU.add))
            link(nc.vector.tensor_copy(idx_l[:, :], sel[:, 4, :]))
            link(ts_(sel[:, 4, :], sel[:, 3, :], pid_f[:, 1:2], None, ALU.is_gt))
            tt(mch[:, :, :], sel[:, 4, :].unsqueeze(2).to_broadcast([P, NT, BT]),
               m32[:, :].unsqueeze(1).to_broadcast([P, NT, BT]), ALU.mult).then_inc(s_ids, 1)
            ts_(onehot[:, :], ids_f[0:NS, 0, :], pid_f[0:NS, 0:1], None, ALU.is_equal).then_inc(s_ids, 1)
            dve.wait_ge(s_sp, 1)
            nc.vector.tensor_copy(bsess[:, :], ps_s[:, 0:2 * NT]).then_inc(s_sv, 1)

            def setup_lo(k, dst, src, hi, eng_sem=s_setup_lo):
                dve.wait_ge(s_setup_hi, k + 1)
                lo_of(dst, src, hi).then_inc(eng_sem, 1)

            for j in range(KC):
                setup_lo(j, WT[:, 1, j, :], ps[j % 4][:, :], WT[:, 0, j, :])

            dve.wait_ge(dma["qz"], 16 * 2 * KC)
            qzi = mask16[:, 0:2 * (D // 8)].bitcast(I32)
            for e in range(8):
                link(ts_(qzi, qz_i[:, :], 4 * e, 15, ALU.logical_shift_right, ALU.bitwise_and))
                link(nc.vector.tensor_copy(zero16[:, :].rearrange("p (m e) -> p m e", e=8)[:, :, e], qzi))
            dve.wait_ge(dma["q"], 32)
            link(ts_(q_i[64:P, :], q_i[64:P, :], 4, None, ALU.logical_shift_right))
            dve.wait_ge(dma["sc"], 16 * 2 * KC)
            for c in range(KC):
                link(ts_(q_nib, q_i, 8 * c, 15, ALU.logical_shift_right, ALU.bitwise_and))
                link(tt(f16[:, :], q_nib, zero16[:, :], ALU.subtract))
                w = tt(W16[:, c, :], f16[:, :], scale16[:, :], ALU.mult)
                if c < KC - 1:
                    link(w)
                else:
                    w.then_inc(s_deq, 1)

            for j in range(KC):
                dve.wait_ge(s_lB_hi, j + 1)
                lo_of(lBs[:, 1, j, :].rearrange("p (a r) -> p a r", r=RK), lB_raw[:, :, j, :],
                      lBs[:, 0, j, :].rearrange("p (a r) -> p a r", r=RK)).then_inc(s_lB_lo, 1)
            for j in range(KC):
                setup_lo(KC + j, ATG[:, 1, j, :], ps[j % 4][:, :], ATG[:, 0, j, :])
            dve.wait_ge(s_sp, 2)
            link(nc.vector.tensor_copy(liT[:, :], ps_z[0:R32, 0:NE]))
            nc.vector.tensor_copy(fAT[:, :, :].rearrange("r j p -> r (j p)"), ps_s[0:R32, :]).then_inc(s_sv, 1)
            for s in range(2):
                nc.vector.tensor_copy(Rz[:, s, :, 0:NE], WT[:, s, :, 0:NE].bitcast(F32))
            link(nc.vector.tensor_copy(Rz[:, 0, :, 2 * NE:NZ], fA[:, :, :]))
            link(lo_of(Rz[:, 1, :, 2 * NE:NZ], fA[:, :, :], Rz[:, 0, :, 2 * NE:NZ]))
            dve.wait_ge(s_sp, 3)
            d2 = ps_s[:, 0:KC * NE].rearrange("p (j e) -> p j e", e=NE)
            link(nc.vector.tensor_copy(Rz[:, 0, :, NE:2 * NE], d2))
            lo_of(Rz[:, 1, :, NE:2 * NE], d2, Rz[:, 0, :, NE:2 * NE]).then_inc(s_sv, 1)
            dve.wait_ge(dma["bb"], 16)
            bbw = bb_raw[:, :].unsqueeze(2).to_broadcast([P, KC, P])
            link(nc.vector.tensor_copy(bbB[:, 0, :, :], bbw))
            tt(bbB[:, 1, :, :], bbw, bbB[:, 0, :, :].bitcast(F32), ALU.subtract).then_inc(s_bbB, 1)
            for j in range(KC):
                dve.wait_ge(s_Wb_hi, j + 1)
                lo_of(Wbs[:, 1, j, :], Wb_raw[:, j, :], Wbs[:, 0, j, :]).then_inc(s_Wb_lo, 1)
            dve.wait_ge(s_sp, GZ)
            gz = ps_s[:, 0:KC * NZ].rearrange("p (k w) -> p k w", w=NZ)
            for par in range(2):
                link(nc.vector.tensor_copy(azv[:, par, 0, :, RH:AZW], gz))
                g = lo_of(azv[:, par, 1, :, RH:AZW], gz, azv[:, par, 0, :, RH:AZW])
                if par == 0:
                    link(g)
                else:
                    g.then_inc(s_sv, 1)
            dve.wait_ge(s_sv, GZ)
            dve.wait_ge(s_lzp, 1)
            for m in range(KC):
                dve.wait_ge(s_setup_hi, 2 * KC + m + 1)
                lo_of(L_st[:, m % 2, D:2 * D], ps[m % 4][:, :], L_st[:, m % 2, 0:D]).then_inc(s_chain, 1)
                count[0] += 1
                lzp = ps_x[:, m * 64:m * 64 + NZ]
                link(nc.vector.tensor_copy(L_st[:, m % 2, 2 * D:2 * D + NZ], lzp))
                lo_of(L_st[:, m % 2, 2 * D + NZ:2 * D + 2 * NZ], lzp,
                      L_st[:, m % 2, 2 * D:2 * D + NZ]).then_inc(s_setup_lo, 1)
            dve.wait_ge(dma["Bm"], 16 * BT)
            link(ts_(bm_raw[:, :], bm_raw[:, :], 0.5, None, ALU.mult))
            link(nc.vector.tensor_copy(Bstk[:, :], bm_raw[:, :]))
            lo_of(Bstk[P // 2:P, :], bm_raw[P // 2:P, :], Bstk[P // 2:P, :]).then_inc(s_bst, 1)
            dve.wait_ge(s_sp, CZ)
            dve.wait_ge(dma["bz_in"], 16)
            link(nc.vector.tensor_copy(cz[:, :], ps_s[:, 0:NZ]))
            tt(cz[:, 0:NE], cz[:, 0:NE], bz[:, :], ALU.add).then_inc(s_sv, 1)
            dve.wait_ge(s_sp, CROW)
            dve.wait_ge(dma["crow_in"], 16)
            tt(crow[:, :], crow[:, :], ps_f[:, :], ALU.add).then_inc(s_sv, 1)
            dve.wait_ge(s_sv, CROW)
            dve.wait_ge(dma["w2"], 16 * 6)
            dve.wait_ge(dma["bias"], 16)

            def stages(n):
                if n.on(3):
                    t = n.tile(3)
                    dve.wait_ge(s_hz, n.tile(3, 1))
                    tt(hmf[:, :].rearrange("p (j r) -> p j r", r=RK), ps_z[:, 0:RH].rearrange("p (j r) -> p j r", r=RK),
                       hmask[:, :, :], ALU.mult).then_inc(s_hm, 1)
                    dve.wait_ge(s_hm, n.tile(3, 1))
                    if n.past(3, 1):
                        dve.wait_ge(s_hTp, t)
                    nc.vector.tensor_copy(hs[:, 0, 0:RH].bitcast(F32R), hmf[:, :]).then_inc(s_hh, 1)
                    dve.wait_ge(s_hh, n.tile(3, 1))
                    tt(hs[:, 0, RH:2 * RH], hmf[:, :], hs[:, 0, 0:RH], ALU.subtract).then_inc(s_hs, 1)
                if n.on(2):
                    t, par = n.tile(2), n.par(2)
                    dve.wait_ge(s_f16, n.tile(2, 1))
                    tt(f16[:, :], f16[:, :], bias16[:, :], ALU.add).then_inc(s_b16, 1)
                    dve.wait_ge(s_b16, n.tile(2, 1))
                    if n.past(2, 2):
                        dve.wait_ge(s_x1st[par], 16 * n.half(2))
                        dve.wait_ge(s_xTp, n.tile(2, -1))
                    tt(x1s[:, par, :], x_all[:, t, :], f16[:, :], ALU.add).then_inc(s_x1, 1)
                if n.on(1):
                    t = n.tile(1)
                    ts_(mask16[:, :], iota16[:, :], sel[:, 1, bass.ds(t, 1)], None, ALU.is_lt).then_inc(s_mask, 1)
                    dve.wait_ge(s_mask, n.tile(1, 1))
                    dve.wait_ge(s_cond, n.tile(1, 1))
                    if n.past(1, 1):
                        dve.wait_ge(s_ctp, t)
                    stt(c16[:, :].rearrange("p (e w) -> p w e", e=8), ps_c[:, :].rearrange("p (w e) -> p w e", e=8),
                        b2col[:, :], mask16[:, :].rearrange("p (w e) -> p w e", e=8), ALU.add, ALU.mult).then_inc(s_c16, 1)
                    dve.wait_ge(s_ctp, n.tile(1, 1))
                    if n.past(1, 1):
                        dve.wait_ge(s_ffn, t)
                    nc.vector.tensor_copy(cT16[:, :], ps_ct[:, 0:D]).then_inc(s_cT, 1)
                if n.on(2):
                    par = n.par(2)
                    dve.wait_ge(s_hi, n.tile(2, 1))
                    lo_of(xT[:, par, KC:2 * KC, :].rearrange("p k c -> p (k c)"), ps_x[:, :],
                          xT[:, par, 0:KC, :].rearrange("p k c -> p (k c)")).then_inc(s_lo, 1)
                if n.on(3):
                    dve.wait_ge(s_l48, n.tile(3, 1))
                    tt(zall[:, n.tile(3), :], ps_z[:, RH:AZW], cz[:, :], ALU.add).then_inc(s_zh, 1)
            run_phase_a(dve, stages)

            dve.wait_ge(s_zh, NT)
            for par in range(2):
                dve.wait_ge(s_x1st[par], 16 * NT // 2)
            steps = [0]

            def signal(ins):
                steps[0] += 1
                ins.then_inc(s_rv, 1)
                dve.wait_ge(s_rv, steps[0])

            ne3 = [P, NT, NE]

            def v(i):
                return rt[:, i, :].rearrange("p (t e) -> p t e", e=NE)

            def col(i):
                return rt[:, 7, i * NT:(i + 1) * NT]

            def bc(ap):
                return ap.unsqueeze(2).to_broadcast(ne3)

            Hs, dl = zall[:, :, 0:NE], zall[:, :, NE:2 * NE]
            for i, src in enumerate((Hs, dl)):
                link(ts_(v(i), src, oddp[:, 0:1], None, ALU.mult))
            link(nc.vector.tensor_reduce(small[:, 0:1], v(0), AX.XY, ALU.max, apply_absolute_value=True))
            signal(nc.vector.tensor_reduce(small[:, 1:2], v(1), AX.XY, ALU.max, apply_absolute_value=True))
            dve.wait_ge(s_rp, 1)
            link(nc.vector.tensor_reduce(small[0:2, 2:3], ps_s[0:2, 0:P], AX.X, ALU.max))
            link(ts_(small[0:2, 3:4], small[0:2, 2:3], EPS, None, ALU.max))
            link(nc.vector.reciprocal(small[0:2, 4:5], small[0:2, 3:4]))
            signal(ts_(small[0:2, 6:8], ident[0:2, 0:2], small[0:2, 4:5], 0.5, ALU.mult, ALU.mult))
            dve.wait_ge(s_rp, 2)
            link(nc.vector.tensor_copy(small[:, 8:10], ps_s[:, 0:2]))
            link(ts_(v(0), Hs, small[:, 8:9], None, ALU.mult))
            link(stt(v(0), dl, small[:, 9:10], v(0), ALU.mult, ALU.add))
            link(nc.vector.tensor_reduce(col(0), v(0), AX.X, ALU.max))
            signal(tt(v(0), v(0), bc(col(0)), ALU.subtract))
            dve.wait_ge(s_ra, 1)
            link(nc.vector.tensor_reduce(col(1), v(1), AX.X, ALU.add))
            link(nc.vector.reciprocal(col(2), col(1)))
            link(tt(v(2), v(1), bc(col(2)), ALU.mult))
            link(nc.vector.tensor_reduce(col(3), v(2), AX.X, ALU.max))
            link(tt(v(5), v(2), bc(col(3)), ALU.is_equal))
            link(nc.vector.tensor_reduce(col(4), v(5), AX.X, ALU.add))
            link(stt(v(6), v(5), -2.0, v(2), ALU.mult, ALU.add))
            link(nc.vector.tensor_reduce(col(5), v(6), AX.X, ALU.max))
            link(stt(col(6), col(4), 2.0, col(3), ALU.is_ge, ALU.mult))
            link(tt(col(7), col(5), col(6), ALU.max))
            signal(tt(v(4), v(2), bc(col(7)), ALU.subtract))
            for k in range(2):
                dve.wait_ge(s_Ghi, k + 1)
                lo_of(ATG[:, 1, k, :], ps[k % 2][:, :], ATG[:, 0, k, :]).then_inc(s_Glo, 1)
            dve.wait_ge(dma["lrow"], 16 * P // NE)
            link(tt(BD.rearrange("p (t r) -> p t r", t=NT), blk[:, :, 0:1].to_broadcast([P, NT, R32]),
                    lrow[:, :].unsqueeze(1).to_broadcast([P, NT, R32]), ALU.mult))
            dve.wait_ge(s_ra, 2)
            link(ts_(v(3), v(3), 1.0, None, ALU.add))
            link(nc.vector.reciprocal(v(4), v(3)))
            link(tt(v(2), v(2), v(4), ALU.mult))
            link(nc.vector.tensor_reduce(col(0), v(2), AX.X, ALU.add))
            link(ts_(col(1), col(0), WEPS, None, ALU.add))
            link(nc.vector.reciprocal(col(2), col(1)))
            signal(tt(v(2), v(2), bc(col(2)), ALU.mult))
            dve.wait_ge(s_rp, 3)
            signal(nc.vector.tensor_copy(rt[:, 5, :].rearrange("p (n a) -> p n a", a=2),
                                         ps_s[:, 0:P].rearrange("p (n a) -> p n a", a=2)[:, :, 1:2].to_broadcast([P, P // 2, 2])))
            dve.wait_ge(s_rp, 4)
            link(tt(zw, zall[:, :, 2 * NE:NZ], ps_z[:, :].rearrange("p (t r) -> p t r", t=NT), ALU.mult))
            for k in range(2, KC):
                dve.wait_ge(s_Ghi, k + 1)
                lo_of(ATG[:, 1, k, :], ps[k % 2][:, :], ATG[:, 0, k, :]).then_inc(s_Glo, 1)

            for par in range(2):
                dve.wait_ge(s_xTst[par], 16 * NT // 2)

            def prepare(t, par, reader=None):
                if reader is not None:
                    dve.wait_ge(s_main, reader)
                nc.vector.tensor_copy(xT[:, par, :, :].rearrange("p k c -> p (k c)"),
                                      xT_all[:, t, :, :].rearrange("p k c -> p (k c)").bitcast(F32)).then_inc(s_xc, 1)
                parts = hs[:, par, :].rearrange("p (s a r) -> p s a r", s=2, a=2)
                z3 = zw[:, t, :].unsqueeze(1).to_broadcast([P, 2, R32])
                nc.vector.tensor_copy(parts[:, :, 0, :].bitcast(F32R), z3).then_inc(s_zph, 1)
                dve.wait_ge(s_zph, t + 1)
                tt(parts[:, :, 1, :], z3, parts[:, :, 0, :], ALU.subtract).then_inc(s_zs, 1)

            prepare(0, 0)
            prepare(1, 1)
            with dve.Fori(0, NT // 2 - 1) as k:
                for u in range(2):
                    t = 2 * k + u
                    dve.wait_ge(s_main, t + 1)
                    dve.wait_ge(s_xb, t + 1)
                    tt(x_all[:, t, :], x_all[:, t, :], ps[2 * u + 1][:, :], ALU.add).then_inc(s_out_r, 1)
                    prepare(t + 2, u)
            for t in range(NT - 2, NT):
                dve.wait_ge(s_main, t + 1)
                dve.wait_ge(s_xb, t + 1)
                tt(x_all[:, t, :], x_all[:, t, :], ps[2 * (t % 2) + 1][:, :], ALU.add).then_inc(s_out_r, 1)

        @block.tensor
        def _(pe):
            mm = nc.tensor.matmul

            def split_product(dst, lhs, rhs, start=True, stop=True):
                n = 0
                for j in range(KC):
                    for a, c in ((0, 0), (0, 1), (1, 0)):
                        last = mm(dst, lhs(a, j), rhs(c, j), start=start and n == 0, stop=stop and n == 3 * KC - 1)
                        n += 1
                return last

            pe.wait_ge(s_const, 2)
            pe.wait_ge(s_ids, 2)
            pe.wait_ge(dma["bsess_in"], 16)
            oh = onehot[:, :].rearrange("s (n a) -> s a n", a=2)
            for a in range(2):
                last = mm(ps_s[HID * a:HID * a + HID, 0:2 * NT], b_raw[:, :], oh[:, a, :], start=True, stop=True)
            last.then_inc(s_sp, 1)
            pe.wait_ge(dma["W"], 16)
            for j in range(KC):
                for m in range(KC):
                    last = nc.tensor.transpose(ps[j][:, m * P:(m + 1) * P],
                                               W_raw[:, m, :].rearrange("p (c j) -> p j c", j=KC)[:, j, :], ident[:, :])
                last.then_inc(s_setup_ps, 1)
            pe.wait_ge(dma["lA"], 16)
            for k in range(KC):
                pe.wait_ge(s_setup_lo, k + 1)
                for m in range(KC):
                    last = nc.tensor.transpose(ps[k][:, m * P:(m + 1) * P], lA_raw[:, m, k * P:(k + 1) * P], ident[:, :])
                last.then_inc(s_setup_ps, 1)
            pe.wait_ge(dma["li"], 16)
            pe.wait_ge(dma["fA"], 16)
            pe.wait_ge(s_sv, BSESS)
            nc.tensor.transpose(ps_z[0:R32, 0:NE], li_raw[:, :], ident[0:NE, 0:NE])
            for j in range(KC):
                last = nc.tensor.transpose(ps_s[0:R32, j * P:(j + 1) * P], fA[:, j, :], ident[:, :])
            last.then_inc(s_sp, 1)
            pe.wait_ge(s_sv, LIT)
            for j in range(KC):
                last = mm(ps_s[:, j * NE:(j + 1) * NE], fAT[:, j, :], liT[:, :], start=j == 0, stop=j == KC - 1,
                          skip_group_check=True)
            last.then_inc(s_sp, 1)
            pe.wait_ge(s_sv, D2)
            pe.wait_ge(s_Wb_lo, KC)
            for k in range(KC):
                last = split_product(ps_s[:, k * NZ:(k + 1) * NZ], lambda a, j: Wbs[:, a, j, k * P:(k + 1) * P],
                                     lambda a, j: Rz[:, a, j, :])
            last.then_inc(s_sp, 1)
            pe.wait_ge(s_lB_lo, KC)
            for m in range(KC):
                rows = slice(m * P, (m + 1) * P)
                last = split_product(ps_x[:, m * 64:m * 64 + NZ], lambda a, j: lBs[:, a, j, rows], lambda a, j: Rz[:, a, j, :])
            last.then_inc(s_lzp, 1)
            for m in range(KC):
                pe.wait_ge(s_setup_lo, KC + m + 1)
                rows = slice(m * P, (m + 1) * P)
                last = split_product(ps[m % 4][:, :], lambda a, j: lBs[:, a, j, rows], lambda a, j: WT[:, a, j, :])
                last.then_inc(s_setup_ps, 1)
            pe.wait_ge(s_bbB, 1)
            pe.wait_ge(s_sv, GZ)
            last = split_product(ps_s[:, 0:NZ], lambda a, j: bbB[:, a, j, :], lambda a, j: Rz[:, a, j, :])
            last.then_inc(s_sp, 1)
            pe.wait_ge(s_setup_lo, 3 * KC)
            last = split_product(ps_f[:, :], lambda a, j: bbB[:, a, j, :], lambda a, j: WT[:, a, j, :])
            last.then_inc(s_sp, 1)
            pe.wait_ge(s_sv, CROW)
            pe.wait_ge(dma["w2"], 16 * 6)
            pe.wait_ge(dma["x0"], 16)
            pe.wait_ge(s_deq, 1)

            def hidden(n, p):
                t = n.tile(0)
                if p == 0:
                    pe.wait_ge(s_wbd, n.tile(0, 1))
                if n.past(0, 1):
                    pe.wait_ge(s_gelu, 2 * t + (p - 1))
                mm(ps_hid[p][:, :], wbd[:, n.par(0), 2 * p:2 * p + 2, :].rearrange("p a h -> p (a h)"),
                   x_all[:, t, :], start=True, stop=True).then_inc(s_hid, 1)

            def stages(n):
                if isinstance(n.k, int) and n.c == FIRST - 1:
                    for g in ("x1", "x2", "x3"):
                        pe.wait_ge(dma[g], 16)
                if n.on(3):
                    t, par = n.tile(3), n.par(3)
                    pe.wait_ge(s_lo, n.tile(3, 1))
                    pe.wait_ge(s_az, n.tile(3, 1))
                    if n.past(3, 1):
                        pe.wait_ge(s_zh, t)
                    q = 0
                    for a, c in ((0, 0), (0, 1), (1, 0)):
                        for k in range(KC):
                            last = mm(ps_z[:, 0:AZW], xT[:, par, a * KC + k, :], azv[:, par, c, k, :],
                                      start=q == 0, stop=q == 3 * KC - 1)
                            q += 1
                    last.then_inc(s_hz, 1)
                if n.on(1):
                    t = n.tile(1)
                    pe.wait_ge(s_gelu, 2 * t + 2)
                    if n.past(1, 1):
                        pe.wait_ge(s_c16, t)
                    for p in range(2):
                        last = mm(ps_c[2 * C * p:2 * C * p + 2 * C, :], W2bd[:, :, :].rearrange("p a s -> p (a s)"),
                                  gel[:, p, :], start=True, stop=True)
                    last.then_inc(s_cond, 1)
                if n.on(3):
                    pe.wait_ge(s_hs, n.tile(3, 1))
                    nc.tensor.transpose(ps_x[:, 0:P], hs[:, 0, :], ident[:, :]).then_inc(s_hTp, 1)
                if n.on(0):
                    hidden(n, 0)
                if n.on(2):
                    t, par = n.tile(2), n.par(2)
                    pe.wait_ge(s_x1, n.tile(2, 1))
                    if n.past(2, 1):
                        pe.wait_ge(s_hT, t)
                    for k in range(KC):
                        last = nc.tensor.transpose(ps_x[:, k * P:(k + 1) * P], x1s[:, par, k * P:(k + 1) * P], ident[:, :])
                    last.then_inc(s_xTp, 1)
                if n.on(1):
                    t = n.tile(1)
                    pe.wait_ge(s_c16, n.tile(1, 1))
                    if n.past(1, 1):
                        pe.wait_ge(s_cT, t)
                    for c in range(KC):
                        last = nc.tensor.transpose(ps_ct[:, c * P:(c + 1) * P], c16[:, c * P:(c + 1) * P], ident16[:, :])
                    last.then_inc(s_ctp, 1)
                if n.on(0):
                    hidden(n, 1)
                if n.on(3):
                    par = n.par(3)
                    pe.wait_ge(s_hT, n.tile(3, 1))
                    pe.wait_ge(s_lzd[par], 16 * n.half(3, 1))
                    for c in range(2):
                        last = mm(ps_z[:, RH:AZW], xT[:, par, NX - 1, :], lz[:, par, c * NZ:(c + 1) * NZ],
                                  start=False, stop=c == 1, skip_group_check=True)
                    last.then_inc(s_l48, 1)
                if n.on(1):
                    t = n.tile(1)
                    pe.wait_ge(s_cT, n.tile(1, 1))
                    if n.past(1, 1):
                        pe.wait_ge(s_f16, t)
                    for c in range(KC):
                        last = mm(ps_f[:, :], cT16[:, c * P:(c + 1) * P], W16[:, c, :], start=c == 0, stop=c == KC - 1)
                    last.then_inc(s_ffn, 1)
            run_phase_a(pe, stages)

            def G_rows(k):
                if k >= 2:
                    pe.wait_ge(s_Glo, k - 1)
                split_product(ps[k % 2][:, :], lambda a, j: Wbs[:, a, j, k * P:(k + 1) * P],
                              lambda a, j: WT[:, a, j, :]).then_inc(s_Gp, 1)

            G_rows(0)
            pe.wait_ge(s_rv, R_MAX)
            mm(ps_s[0:2, 0:P], small[:, 0:2], ident[:, :], start=True, stop=True).then_inc(s_rp, 1)
            pe.wait_ge(s_rv, R_SCALE)
            mm(ps_s[:, 0:2], ones2[:, :], small[0:2, 6:8], start=True, stop=True).then_inc(s_rp, 1)
            G_rows(1)
            G_rows(2)
            G_rows(3)
            pe.wait_ge(s_rv, R_W)
            nc.tensor.transpose(ps_s[:, 0:P], rt[:, 2, :], ident[:, :]).then_inc(s_rp, 1)
            pe.wait_ge(s_rv, R_WT)
            mm(ps_z[:, :], rt[:, 5, :], BD, start=True, stop=True).then_inc(s_rp, 1)
            pe.wait_ge(s_rp, 4)
            pe.wait_ge(s_Glo, KC)
            pe.wait_ge(s_bst, 1)

            def z_transpose(t, par):
                pe.wait_ge(s_zs, t + 1)
                nc.tensor.transpose(ps_z[:, 0:P], hs[:, par, :], ident[:, :]).then_inc(s_zTp, 1)

            z_transpose(0, 0)

            def main(t, k, u, reuse):
                dst = ps[2 * u + 1][:, :]
                pe.wait_ge(s_xc, t + 1)
                if reuse:
                    pe.wait_ge(s_out_r, t - 1)
                q = 0
                for a, c in ((0, 0), (0, 1), (1, 0)):
                    for j in range(KC):
                        mm(dst, xT[:, u, a * KC + j, :], ATG[:, c, j, :], start=q == 0, stop=False)
                        q += 1
                pe.wait_ge(s_lhd[u], 16 * k + 16)
                mm(dst, xT[:, u, NX - 1, :], L_hi[:, u, :], start=False, stop=False)
                pe.wait_ge(s_lld[u], 16 * k + 16)
                mm(dst, xT[0:RH, u, NX - 1, :], L_lo[0:RH, u, :], start=False, stop=False)
                pe.wait_ge(s_zTs, t + 1)
                mm(dst, zT[:, u, :], Bstk[:, :], start=False, stop=True).then_inc(s_main, 1)

            def pair(k, first, last):
                for u in range(2):
                    t = 2 * k + u
                    if not (last and u == 1):
                        pe.wait_ge(s_zTs, t + 1)
                        z_transpose(t + 1, 1 - u)
                    main(t, k, u, not first)
            pair(0, True, False)
            with pe.Fori(1, NT // 2 - 1) as k:
                pair(k, False, False)
            pair(NT // 2 - 1, False, True)


INPUTS = ['x', 'itok_B_0_7', 'itok_B_2182_4065', 'itok_B_6_15', '_lenS',
          'L0_cond_W_sess', 'L0_cond_b_sess', 'L0_cond_W2', 'L0_cond_b2',
          'L0_ffn_qweight', 'L0_ffn_qzeros', 'L0_ffn_scales', 'L0_ffn_bias',
          'L1_cond_base_weight', 'L1_cond_base_bias', 'L1_cond_lora_A_w', 'L1_cond_lora_B_w',
          'L1_ffn_W', 'L1_ffn_b', 'L1_ffn_A', 'L1_ffn_Bmat', 'L1_ffn_LiMEs']


def kernel(**inputs):
    import numpy as np
    import concourse.bacc as bacc
    from concourse.bass_utils import run_bass_kernel_spmd as run

    nc = bacc.Bacc("TRN2", target_bir_lowering=False, num_devices=1)
    arrays, args = {}, []
    for name in INPUTS:
        a = np.ascontiguousarray(inputs[name])
        arrays["in_" + name] = a
        args.append(nc.dram_tensor("in_" + name, a.shape, mybir.dt.from_np(a.dtype), kind="ExternalInput").ap())
    args.append(nc.dram_tensor("out_0", inputs["x"].shape, mybir.dt.float32, kind="ExternalOutput").ap())
    adaln_ffn_program(nc, *args)
    return run(nc, [arrays], core_ids=[0]).results[0]["out_0"]
```

```python
from contextlib import ExitStack

import concourse.bass as bass
from concourse import mybir

F32 = mybir.dt.float32
F32R = mybir.dt.float32r
F16 = mybir.dt.float16
I32 = mybir.dt.int32
ALU = mybir.AluOpType
ACT = mybir.ActivationFunctionType
AX = mybir.AxisListType

P = 128


def adaln_ffn_program(nc, x, sess_ids, seq_lens, lora_ids, chan_counts, W_sess, b_sess, W2, b2,
                      qweight, qzeros, scales, bias16_in, Wb, bb, lora_A, lora_B, W, b, A, Bmat, LiMEs, out):
    NB, C, D = x.shape
    NT = NB * C // P
    BT = P // C
    NS, _, HID = W_sess.shape
    NA, RK, _ = lora_A.shape
    KC = D // P
    R32, NE = A.shape[1], LiMEs.shape[0]
    RH = BT * RK
    NZ = 2 * NE + R32
    ZW = 64
    AZW = RH + ZW
    NX = 2 * KC + 1
    EPS, WEPS = 1e-6, 1e-9
    DEPTH = 3

    x_rows = x.rearrange("b c t -> (b c) t")
    out_rows = out.rearrange("b c t -> (b c) t")
    L_hi_dram = nc.dram_tensor("L_hi_dram", [NA * RK, D], F32).ap()
    L_lo_dram = nc.dram_tensor("L_lo_dram", [NA * RK, D], F32).ap()
    L_z_dram = nc.dram_tensor("L_z_dram", [NA * RK, 2 * ZW], F32).ap()

    with ExitStack() as ctx:
        def sb(name, shape, dt):
            return ctx.enter_context(nc.sbuf_tensor(name, shape, dt))

        def sem(name):
            return ctx.enter_context(nc.semaphore(name))

        x_all = sb("x_all", [P, NT, D], F32)
        xT_all = sb("xT_all", [P, NT, NX, P], F32R)
        ATG = sb("ATG", [P, 2, KC, D], F32R)
        WT = sb("WT", [P, 2, KC, D], F32R)
        Wbs = sb("Wbs", [P, 2, KC, D], F32R)
        xT = sb("xT", [P, 2, NX, P], F32R)
        az = sb("az", [P, 2 * KC * 2 * AZW], F32R)
        gel = sb("gel", [P, 2, D], F32)
        x1s = sb("x1s", [P, 2, D], F32)
        W16 = sb("W16", [P, KC, D], F16)
        c16 = sb("c16", [P, D], F16)
        cT16 = sb("cT16", [P, D], F16)
        f16 = sb("f16", [P, D], F16)
        mask16 = sb("mask16", [P, D], F16)
        iota16 = sb("iota16", [P, D], F16)
        bias16 = sb("bias16", [P, D], F16)
        wsel = sb("wsel", [P, 2, HID], F32)
        wbd = sb("wbd", [P, 2, BT, HID], F32)
        lz = sb("lz", [P, 2, 2 * ZW], F32R)
        cz = sb("cz", [P, NZ], F32)
        zall = sb("zall", [P, NT, NZ], F32)
        Bstk = sb("Bstk", [P, D], F32R)
        Rz = sb("Rz", [P, 2, KC, ZW], F32R)
        ident = sb("ident", [P, P], F32)
        ident16 = sb("ident16", [P, P], F16)
        ids_i = sb("ids_i", [P, 4, NB], I32)
        ids_f = sb("ids_f", [P, 4, NB], F32)
        m32 = sb("m32", [P, BT], F32)
        m16 = sb("m16", [P, 2, BT], F32)
        hmask = sb("hmask", [P, BT, RK], F32)
        blk = sb("blk", [P, NT, NE], F32)
        sel = sb("sel", [P, 5, NT], F32)
        idx_w = sb("idx_w", [P, NT], I32)
        idx_l = sb("idx_l", [P, NT], I32)
        idxw = sb("idxw", [P, 2], I32)
        idxl = sb("idxl", [P, 4], I32)
        pid_i = sb("pid_i", [P, 4], I32)
        pid_f = sb("pid_f", [P, 4], F32)
        mch = sb("mch", [P, NT, BT], F32)
        bsess = sb("bsess", [P, NT * 2], F32)
        W2bd = sb("W2bd", [P, 2, C], F32)
        b2col = sb("b2col", [P, 1], F32)
        fA = sb("fA", [P, KC, R32], F32)
        liT = sb("liT", [R32, NE], F32)
        bb_raw = sb("bb_raw", [P, KC], F32)
        bz = sb("bz", [P, NE], F32)
        hmf = sb("hmf", [P, RH], F32)
        hs = sb("hs", [P, 2, P], F32)
        small = sb("small", [P, 16], F32)
        zTu = sb("zTu", [P, 2, P], F32R)
        oddp = sb("oddp", [P, 1], F32)
        ones2 = sb("ones2", [2, P], F32)

        W_raw = x_all[:, 8:12, :]
        Wb_raw = x_all[:, 8:12, :]
        lA_raw = x_all[:, 12:16, :]
        lB_raw = x_all[:, 4:8, :].rearrange("p s (a j r) -> p (s a) j r", j=KC, r=RK)
        xT_flat = xT_all[:, :, :, :].rearrange("p t k c -> p (t k c)")
        lBs = xT_flat[:, 12 * NX * P:12 * NX * P + 2 * KC * D].rearrange("p (s j n) -> p s j n", s=2, j=KC)
        bbB = xT_flat[:, 11 * NX * P:11 * NX * P + 2 * KC * P].rearrange("p (s j n) -> p s j n", s=2, j=KC)
        q_i = gel[:, 0, :].bitcast(I32)
        q_nib = gel[:, 1, :].bitcast(I32)
        zero16, scale16 = c16, cT16
        crow = gel[:, 0, :]
        L_st = xT[:, :, :, :].rearrange("p s k c -> p s (k c)")
        azv = az[:, :].rearrange("p (b k s w) -> p b k s w", b=2, k=KC, s=2)
        L_az = az[:, 0:4 * D].rearrange("p (b s n) -> p b s n", b=2, s=2)
        L_rows = [L_az[:, 0], L_az[:, 1], WT[:, 0, 0:2, :], WT[:, 0, 2:4, :]]
        zp = Wbs[:, 0, :, :].rearrange("p k d -> p (k d)").rearrange("p (t a r) -> p t a r", t=NT, r=R32).bitcast(F32)
        zT = Wbs[:, 1, :, :].rearrange("p k d -> p (k d)").rearrange("p (t c) -> p t c", t=NT)
        BD = gel[:, 0, :]
        zw = gel[:, 1, :].rearrange("p (t r) -> p t r", t=NT)
        rt = x1s[:, :, :].rearrange("p a (b n) -> p (a b) n", n=NT * NE)
        lrow = sb("lrow", [P, R32], F32)
        rowsel = sb("rowsel", [P, 2], F32)
        zlo = sb("zlo", [P, AZW], F32)
        zsum = sb("zsum", [P, AZW], F32)
        bm_raw = x1s[:, 0, :]
        f32r_row = x1s[:, 1, :].bitcast(F32R)
        onehot, b_raw = hs[0:NS, 0, 0:NB], hs[0:NS, 1, 0:HID]
        li_raw = hmf[0:NE, 0:R32]
        qz_i = x1s[:, 1, 0:D // 8].bitcast(I32)
        fAT = x1s[0:R32, 1, :].rearrange("r (j p) -> r j p", j=KC)

        ps = [ctx.enter_context(nc.psum_tensor(f"ps{i}", [P, D], F32)) for i in range(7)]
        ps_ct = ctx.enter_context(nc.psum_tensor("ps_ct", [P, 2 * D], F16))
        ps_hid, ps_c, ps_f, ps_x, ps_z = ps[0:2], ps[2], ps[3], ps[4], ps[5]
        ps_s = ps[6]

        z_banks = ps_x, ps_z

        def main_bank(u):
            return ps[(u + 2) % 4]

        names_dma = ["ids", "w2", "bsess_in", "W", "fA", "li", "q", "qz", "sc", "bias", "lA", "lB", "Wb", "bb",
                     "crow_in", "bz_in", "Bm", "lrow", "x0", "x1", "x2", "x3"]
        dma = {n: sem("dma_" + n) for n in names_dma}
        s_L_st = [sem("L_stored0"), sem("L_stored1")]
        s_const, s_ids, s_deq, s_setup_ps, s_setup_hi, s_setup_lo = (sem(n) for n in (
            "const_ready", "ids_ready", "dequant_done", "setup_psum", "setup_hi", "setup_lo"))
        s_lB_hi, s_lB_lo, s_Wb_hi, s_Wb_lo = (sem(n) for n in ("lB_hi", "lB_lo", "Wb_hi", "Wb_lo"))
        s_sp, s_sv = sem("small_psum"), sem("small_evac")
        s_chain = sem("dve_chain")
        s_bbB = sem("bbB_ready")
        s_bst = sem("Bmat_split")
        s_pool = sem("pool_chain")
        s_masks, s_zlo, s_zsum = sem("masks_ready"), sem("z_lo_copied"), sem("h_summed")
        s_lzp = sem("L_z_psum")
        s_gate = sem("gather_gate")
        s_wg = [sem("wsel_in0"), sem("wsel_in1")]
        s_lzd = [sem("lz_in0"), sem("lz_in1")]
        s_idxw, s_idxl, s_wbd, s_az = sem("idxw_ready"), sem("idxl_ready"), sem("wbd_ready"), sem("az_ready")
        s_hid, s_gelu, s_cond, s_mask, s_c16, s_ctp, s_cT, s_ffn, s_f16, s_b16, s_x1, s_xTp, s_hi, s_lo = (
            sem(n) for n in ("hid_psum", "gelu_done", "cond_psum", "tmask", "c16_ready", "ct_psum", "cT_ready",
                             "ffn_psum", "f16_ready", "f16_biased", "x1_ready", "x1T_psum", "x1T_hi", "x1T_lo"))
        s_hz, s_hm, s_hh, s_hs, s_hTp, s_hT, s_l48, s_zh = (
            sem(n) for n in ("hz_psum", "h_masked", "h_hi", "hs_ready", "hT_psum", "hT_ready", "z_psum", "z_ready"))
        s_x1st = [sem("x1_stored0"), sem("x1_stored1")]
        s_xTst = [sem("xT_stored0"), sem("xT_stored1")]
        s_rp, s_ra, s_rv = sem("routing_psum"), sem("routing_act"), sem("routing_dve")
        s_Gp, s_Ghi, s_Glo = sem("G_psum"), sem("G_hi"), sem("G_lo")
        s_li, s_lhd, s_lld = sem("L_idx"), [sem(f"L_hi_in{u}") for u in range(4)], [sem(f"L_lo_in{u}") for u in range(4)]
        s_xc, s_zc, s_zones, s_zph, s_zs, s_zTp, s_zTs, s_main, s_out_r = (
            sem(n) for n in ("xT_copied", "zT_copied", "zp_ones", "zp_hi", "zp_split", "zT_psum", "zT_ready", "main_psum", "out_ready"))
        s_out = sem("out_stored")
        block = ctx.enter_context(nc.Block())

        BSESS, LIT, D2, GZ, CZ, CROW = 1, 2, 3, 4, 5, 6
        R_MAX, R_SCALE, R_LOGITS, R_DIFF, R_W, R_WT = 1, 2, 3, 4, 5, 6

        class Step:

            def __init__(self, k, c):
                self.k, self.c = k, c

            def on(self, s):
                return not isinstance(self.k, int) or 0 <= self.c - s < NT

            def tile(self, s, plus=0):
                return 2 * self.k + (self.c - s + plus)

            def half(self, s, plus=0):
                return self.k + ((self.c - s) // 2 + plus)

            def par(self, s):
                return (self.c - s) % 2

            def past(self, s, back):
                return not isinstance(self.k, int) or self.c - s - back >= 0

        FIRST = DEPTH + 2
        LAST = NT - 1

        def run_phase_a(eng, body):
            for n in range(FIRST):
                body(Step(0, n))
            with eng.Fori(0, (LAST - FIRST) // 2) as k:
                body(Step(k, FIRST))
                body(Step(k, FIRST + 1))
            for n in range(LAST, NT + DEPTH):
                body(Step(0, n))

        def row(v):
            return v.rearrange("(a n) -> a n", a=1)

        @block.sync
        def _(sp):
            for i, ids in enumerate((sess_ids, seq_lens, lora_ids, chan_counts)):
                sp.dma_start(ids_i[:, i, :], row(ids).to_broadcast([P, NB])).then_inc(dma["ids"], 16)
            sp.dma_start(W_raw, W.rearrange("(m p) o -> p m o", p=P)).then_inc(dma["W"], 16)
            sp.dma_start(lA_raw, lora_A.rearrange("a r d -> (a r) d").rearrange("(m p) d -> p m d", p=P)).then_inc(dma["lA"], 16)
            sp.dma_start(lB_raw.rearrange("p a j r -> p a (j r)"),
                         lora_B.rearrange("a (p j) r -> p a (j r)", j=KC)).then_inc(dma["lB"], 16)
            sp.dma_start(x_all[:, 0:4, :], x_rows[0:4 * P, :].rearrange("(a p) t -> p a t", p=P)).then_inc(dma["x0"], 16)
            sp.wait_ge(s_setup_ps, KC)
            sp.dma_start(Wb_raw, Wb.rearrange("(p j) d -> p j d", j=KC)).then_inc(dma["Wb"], 16)
            sp.wait_ge(s_setup_ps, 2 * KC)
            sp.dma_start(x_all[:, 12:16, :], x_rows[12 * P:16 * P, :].rearrange("(a p) t -> p a t", p=P)).then_inc(dma["x3"], 16)
            sp.wait_ge(s_lB_lo, KC)
            sp.dma_start(x_all[:, 4:8, :], x_rows[4 * P:8 * P, :].rearrange("(a p) t -> p a t", p=P)).then_inc(dma["x1"], 16)
            sp.wait_ge(s_Wb_lo, KC)
            sp.dma_start(x_all[:, 8:12, :], x_rows[8 * P:12 * P, :].rearrange("(a p) t -> p a t", p=P)).then_inc(dma["x2"], 16)
            for m in range(KC):
                rows = slice(m * P, (m + 1) * P)
                if m == KC - 1:
                    sp.wait_ge(s_deq, 1)
                    sp.dma_start(crow, row(b).to_broadcast([P, D])).then_inc(dma["crow_in"], 16)
                sp.wait_ge(s_setup_lo, 2 * KC + m + 1)
                st = L_st[:, m % 2, :].bitcast(F32)
                sp.dma_start(L_z_dram[rows, :], st[:, 2 * D:2 * D + 2 * ZW]).then_inc(s_L_st[m % 2], 16)
                sp.dma_start(L_hi_dram[rows, :], st[:, 0:D]).then_inc(s_L_st[m % 2], 16)
                sp.dma_start(L_lo_dram[rows, :], st[:, D:2 * D]).then_inc(s_L_st[m % 2], 16)

            def stores(n):
                if n.on(2):
                    sp.wait_ge(s_x1, n.tile(2, 1))
                    sp.dma_start(x_all[:, n.tile(2), :], x1s[:, n.par(2), :]).then_inc(s_x1st[n.par(2)], 16)
                if n.on(3):
                    sp.wait_ge(s_hT, n.tile(3, 1))
                    sp.dma_start(xT_all[:, n.tile(3), :, :].bitcast(F32), xT[:, n.par(3), :, :].bitcast(F32)).then_inc(s_xTst[n.par(3)], 16)
            run_phase_a(sp, stores)

            with sp.Fori(0, NT) as t:
                sp.wait_ge(s_out_r, t + 1)
                sp.dma_start(out_rows[bass.ts(t, P), :], x_all[:, t, :]).then_inc(s_out, 16)
            sp.wait_ge(s_out, 16 * NT)

        @block.gpsimd
        def _(pool):
            count = [0]

            def link(ins):
                count[0] += 1
                ins.then_inc(s_pool, 1)
                pool.wait_ge(s_pool, count[0])

            def band(ap, pattern, width, mult=1, base=0):
                link(nc.gpsimd.affine_select(out=ap, in_=ap, compare_op=ALU.is_ge, fill=0.0, base=base,
                                             pattern=pattern, channel_multiplier=mult))
                link(nc.gpsimd.affine_select(out=ap, in_=ap, compare_op=ALU.is_ge, fill=0.0, base=width - 1 - base,
                                             pattern=[[-s, c] for s, c in pattern], channel_multiplier=-mult))

            link(nc.gpsimd.memset(ident[:, :], 0.0))
            nc.gpsimd.affine_select(out=ident[:, :], in_=ident[:, :], compare_op=ALU.not_equal, fill=1.0, base=0,
                                    pattern=[[-1, P]], channel_multiplier=1).then_inc(s_const, 1)
            nc.gpsimd.iota(pid_i[:, 0:1], pattern=[[0, 1]], base=0, channel_multiplier=1)
            nc.gpsimd.memset(m16[:, :, :], 1.0)
            link(nc.gpsimd.memset(m32[:, :], 1.0))
            band(m32[:, :], [[-C, BT]], C)
            band(m16[:, :, :], [[-P // 2, 2], [-RK, BT]], RK)
            nc.gpsimd.memset(hmask[:, :, :], 1.0)
            nc.gpsimd.memset(blk[:, :, :], 1.0)
            nc.gpsimd.memset(ones2[:, :], 1.0)
            nc.gpsimd.iota(iota16[:, :], pattern=[[1, D]], base=0, channel_multiplier=0,
                           allow_small_or_imprecise_dtypes=True)
            link(nc.gpsimd.memset(W2bd[:, :, :], 0.0))
            band(hmask[:, :, :], [[-C, BT], [0, RK]], C)
            band(blk[:, :, :], [[-NE, NT], [0, NE]], NE)
            link(nc.gpsimd.memset(rowsel[:, :], 1.0))
            band(rowsel[:, :], [[-1, 2]], 1, base=-3 * R32)
            pool.sem_inc(s_masks, 1)

            def pool_lo(dst, src, hi, got, done):
                pool.wait_ge(*got)
                nc.gpsimd.tensor_tensor(dst, src, hi.bitcast(F32), ALU.subtract).then_inc(done, 1)

            for j in range(KC):
                pool_lo(Wbs[:, 1, j, :], Wb_raw[:, j, :], Wbs[:, 0, j, :], (s_Wb_hi, j + 1), s_Wb_lo)
            for j in range(KC):
                pool_lo(lBs[:, 1, j, :].rearrange("p (a r) -> p a r", r=RK), lB_raw[:, :, j, :],
                        lBs[:, 0, j, :].rearrange("p (a r) -> p a r", r=RK), (s_lB_hi, j + 1), s_lB_lo)

            def gather_w(n, s):
                t, par = n.tile(s), n.par(s)
                if n.past(s, 2):
                    pool.wait_ge(s_wg[par], 16 * n.half(s))
                    pool.wait_ge(s_wbd, n.tile(s, -1))
                nc.gpsimd.tensor_copy(idxw[:, par:par + 1], idx_w[:, bass.ds(t, 1)]).then_inc(s_idxw, 1)
                pool.wait_ge(s_idxw, n.tile(s, 1))
                pool.sem_inc(s_gate, 1)
                nc.gpsimd.indirect_dma_start(
                    wsel[:, par, :], None, W_sess.rearrange("s c h -> (s c) h"),
                    bass.IndirectOffsetOnAxis(idxw[:, par:par + 1], 0)).then_inc(s_wg[par], 16)

            def make_wbd(n, s):
                t, par = n.tile(s), n.par(s)
                pool.wait_ge(s_wg[par], 16 * n.half(s, 1))
                if n.past(s, 2):
                    pool.wait_ge(s_hid, 2 * n.tile(s, -1))
                nc.gpsimd.tensor_tensor(
                    wbd[:, par, :, :], wsel[:, par, :].unsqueeze(1).to_broadcast([P, BT, HID]),
                    mch[:, t, :].unsqueeze(2).to_broadcast([P, BT, HID]), ALU.mult).then_inc(s_wbd, 1)

            def gather_a(n, s):
                t, par = n.tile(s), n.par(s)
                if n.past(s, 2):
                    pool.wait_ge(s_hz, n.tile(s, -1))
                for j in range(BT):
                    a = pool.value_load(ids_i[0:1, 2, bass.ds(4 * t + j, 1)], min_val=0, max_val=NA - 1)
                    last = nc.gpsimd.tensor_copy(
                        azv[:, par, :, :, RK * j:RK * j + RK],
                        ATG[:, :, :, bass.ds(a * RK, RK)].rearrange("p s k w -> p k s w"))
                    if j < BT - 1:
                        last.then_inc(s_pool, 1)
                last.then_inc(s_az, 1)

            def gather_lz(n, s):
                t, par = n.tile(s), n.par(s)
                if n.past(s, 2):
                    pool.wait_ge(s_lzd[par], 16 * n.half(s))
                    pool.wait_ge(s_l48, n.tile(s, -1))
                nc.gpsimd.tensor_copy(idxl[:, par:par + 1], idx_l[:, bass.ds(t, 1)]).then_inc(s_idxl, 1)
                pool.wait_ge(s_idxl, n.tile(s, 1))
                pool.sem_inc(s_gate, 1)
                nc.gpsimd.indirect_dma_start(
                    lz[:, par, :].bitcast(F32), None, L_z_dram,
                    bass.IndirectOffsetOnAxis(idxl[:, par:par + 1], 0)).then_inc(s_lzd[par], 16)

            pool.wait_ge(s_ids, 1)
            gather_w(Step(0, 0), 0)
            make_wbd(Step(0, 0), 0)

            def gathers(n):
                if n.on(-1):
                    gather_w(n, -1)
                if isinstance(n.k, int) and n.c == 2:
                    pool.wait_ge(s_setup_lo, 2 * KC)
                    pool.wait_ge(s_sv, GZ)
                    for m in range(2):
                        pool.wait_ge(s_L_st[m], 16 * 3 * 2)
                if n.on(2):
                    gather_lz(n, 2)
                    gather_a(n, 2)
                if n.on(-1):
                    make_wbd(n, -1)
            run_phase_a(pool, gathers)

            for par in range(2):
                pool.wait_ge(s_lzd[par], 16 * NT // 2)
            pool.wait_ge(s_hz, NT)

            def gather_L(t, u, reader=None):
                if reader is not None:
                    pool.wait_ge(s_main, reader)
                nc.gpsimd.tensor_copy(idxl[:, u:u + 1], idx_l[:, bass.ds(t, 1)]).then_inc(s_li, 1)
                pool.wait_ge(s_li, t + 1)
                pool.sem_inc(s_gate, 1)
                nc.gpsimd.indirect_dma_start(L_rows[u][:, 0, :].bitcast(F32), None, L_hi_dram,
                                             bass.IndirectOffsetOnAxis(idxl[:, u:u + 1], 0)).then_inc(s_lhd[u], 16)
                nc.gpsimd.indirect_dma_start(L_rows[u][0:RH, 1, :].bitcast(F32), None, L_lo_dram,
                                             bass.IndirectOffsetOnAxis(idxl[0:RH, u:u + 1], 0)).then_inc(s_lld[u], 16)

            gather_L(0, 0)
            gather_L(1, 1)
            pool.wait_ge(s_Gp, KC)
            nc.gpsimd.memset(zp[:, :, 3, 2:R32], 0.0).then_inc(s_zones, 1)
            nc.gpsimd.memset(zp[:, :, 3, 0:2], 1.0).then_inc(s_zones, 1)
            gather_L(2, 2)
            gather_L(3, 3)
            with pool.Fori(1, NT // 4) as k:
                for u in range(4):
                    gather_L(4 * k + u, u, reader=4 * k + (u - 3))

        @block.scalar
        def _(act):
            def copy(dst, src):
                return nc.scalar.activation(dst, src, ACT.Copy)

            act.dma_start(fA[:, :, :], A.rearrange("(p j) r -> p j r", j=KC)).then_inc(dma["fA"], 16)
            act.dma_start(li_raw, LiMEs).then_inc(dma["li"], 16)
            act.dma_start(b_raw, b_sess).then_inc(dma["bsess_in"], 16)
            act.dma_start(bb_raw[:, :], bb.rearrange("(p j) -> p j", j=KC)).then_inc(dma["bb"], 16)
            act.dma_start(q_i, qweight.unsqueeze(0).to_broadcast([2, D // 8, D])).then_inc(dma["q"], 16)
            for h in range(2):
                half = slice(64 * h, 64 * h + 64)
                act.dma_start(qz_i[half, :],
                              qzeros.unsqueeze(1).to_broadcast([KC, P // 8, D // 8])).then_inc(dma["qz"], 16)
                act.dma_start(scale16[half, :],
                              scales.unsqueeze(1).to_broadcast([KC, P // 8, D])).then_inc(dma["sc"], 16)
            act.wait_ge(s_masks, 1)
            for h in range(2):
                act.dma_start(W2bd[HID * h:HID * h + HID, h, :], W2).then_inc(dma["w2"], 16)
            act.dma_start(b2col[:, :],
                          b2.rearrange("(n a) -> n a", a=1).unsqueeze(0).to_broadcast([BT, C, 1])).then_inc(dma["w2"], 16)
            act.dma_start(bias16[:, :], row(bias16_in).to_broadcast([P, D])).then_inc(dma["bias"], 16)
            act.dma_start(bm_raw, Bmat.unsqueeze(0).to_broadcast([BT, R32, D])).then_inc(dma["Bm"], 16)
            act.dma_start(bz[:, :], row(b)[:, 0:NE].to_broadcast([P, NE])).then_inc(dma["bz_in"], 16)
            act.dma_start(lrow[:, :], LiMEs.unsqueeze(0).to_broadcast([P // NE, NE, R32])).then_inc(dma["lrow"], 16)

            def setup_hi(k, dst, src):
                act.wait_ge(s_setup_ps, k + 1)
                copy(dst, src).then_inc(s_setup_hi, 1)

            for j in range(KC):
                setup_hi(j, WT[:, 0, j, :], ps[j % 4][:, :])
            act.wait_ge(dma["lB"], 16)
            for j in range(KC):
                copy(lBs[:, 0, j, :].rearrange("p (a r) -> p a r", r=RK), lB_raw[:, :, j, :]).then_inc(s_lB_hi, 1)
            for j in range(KC):
                setup_hi(KC + j, ATG[:, 0, j, :], ps[j % 4][:, :])
            act.wait_ge(dma["Wb"], 16)
            for j in range(KC):
                copy(Wbs[:, 0, j, :], Wb_raw[:, j, :]).then_inc(s_Wb_hi, 1)
            for m in range(KC):
                if m >= 2:
                    act.wait_ge(s_L_st[m % 2], 48)
                act.wait_ge(s_setup_ps, 2 * KC + m + 1)
                copy(L_st[:, m % 2, 0:D], ps[m % 4][:, :]).then_inc(s_setup_hi, 1)

            def gelu(n, p):
                act.wait_ge(s_hid, 2 * n.tile(0) + p + 1)
                if isinstance(n.k, int) and n.c == 0 and p == 0:
                    act.wait_ge(s_bst, 1)
                    act.wait_ge(s_sv, BSESS)
                if n.past(0, 1):
                    act.wait_ge(s_cond, n.tile(0))
                nc.scalar.activation(gel[:, p, :], ps_hid[p][:, :], ACT.Gelu,
                                     bias=bsess[:, bass.ds(2 * n.tile(0) + p, 1)]).then_inc(s_gelu, 1)

            def stages(n):
                if n.on(2):
                    act.wait_ge(s_ffn, n.tile(2, 1))
                    if n.past(2, 1):
                        act.wait_ge(s_x1, n.tile(2))
                    copy(f16[:, :], ps_f[:, :]).then_inc(s_f16, 1)
                if n.on(3):
                    act.wait_ge(s_hz, n.tile(3, 1))
                    if n.past(3, 1):
                        act.wait_ge(s_zsum, n.tile(3))
                    copy(zlo[:, :], ps_z[:, AZW:2 * AZW]).then_inc(s_zlo, 1)
                if n.on(0):
                    gelu(n, 0)
                if n.on(2):
                    act.wait_ge(s_xTp, n.tile(2, 1))
                    if isinstance(n.k, int) and n.c == 2:
                        for m in range(2):
                            act.wait_ge(s_L_st[m], 48 * KC // 2)
                    if n.past(2, 2):
                        act.wait_ge(s_xTst[n.par(2)], 16 * n.half(2))
                        act.wait_ge(s_l48, n.tile(2, -1))
                    copy(xT[:, n.par(2), 0:KC, :].rearrange("p k c -> p (k c)"), ps_x[:, :]).then_inc(s_hi, 1)
                if n.on(3):
                    act.wait_ge(s_hTp, n.tile(3, 1))
                    copy(xT[:, n.par(3), NX - 1, :], ps_s[:, 0:P]).then_inc(s_hT, 1)
                if n.on(0):
                    gelu(n, 1)
            run_phase_a(act, stages)

            act.wait_ge(s_rv, R_LOGITS)
            nc.scalar.activation(rt[:, 1, :], rt[:, 0, :], ACT.Exp).then_inc(s_ra, 1)
            for k in range(2):
                act.wait_ge(s_Gp, k + 1)
                if k == 0:
                    act.wait_ge(s_az, NT)
                copy(ATG[:, 0, k, :], ps[k % 2][:, :]).then_inc(s_Ghi, 1)
            act.wait_ge(s_rv, R_DIFF)
            nc.scalar.activation(rt[:, 3, :], rt[:, 4, :], ACT.Exp, scale=-2.0).then_inc(s_ra, 1)
            for k in range(2, KC):
                act.wait_ge(s_Gp, k + 1)
                copy(ATG[:, 0, k, :], ps[k % 2][:, :]).then_inc(s_Ghi, 1)
            for q in range(4):
                act.wait_ge(s_zTp, q + 1)
                copy(zT[:, 4 * q:4 * q + 4, :].rearrange("p t c -> p (t c)"), z_banks[q % 2][:, :]).then_inc(s_zTs, 1)
            act.wait_ge(s_zTs, 4)

            def fetch(t, u, reader=None):
                if reader is not None:
                    act.wait_ge(s_main, reader)
                copy(xT[:, u % 2, :, :], xT_all[:, bass.ds(t, 1), :, :].rearrange("p t k c -> p (t k) c").bitcast(F32)).then_inc(s_xc, 1)
                copy(zTu[:, u % 2, :], zT[:, t, :].bitcast(F32)).then_inc(s_zc, 1)

            fetch(4, 0)
            fetch(5, 1)
            with act.Fori(1, NT // 4 - 1) as k:
                for u in range(4):
                    fetch(4 * k + (u + 2), u, reader=4 * k + (u + 1))
            for t in range(NT - 2, NT):
                fetch(t, t, reader=t - 1)

        @block.vector
        def _(dve):
            count = [0]

            def link(ins):
                count[0] += 1
                ins.then_inc(s_chain, 1)
                dve.wait_ge(s_chain, count[0])

            def tt(o, a, bb_, op):
                return nc.vector.tensor_tensor(o, a, bb_, op)

            def ts_(o, a, s1, s2, op0, op1=None):
                return nc.vector.tensor_scalar(o, a, s1, s2, op0, op1) if op1 is not None else \
                    nc.vector.tensor_scalar(o, a, s1, None, op0)

            def stt(o, a, s, c, op0, op1):
                return nc.vector.scalar_tensor_tensor(out=o, in0=a, scalar=s, in1=c, op0=op0, op1=op1)

            def lo_of(dst, src, hi):
                return tt(dst, src, hi.bitcast(F32), ALU.subtract)

            dve.wait_ge(s_masks, 1)
            nc.vector.tensor_copy(ident16[:, :], ident[:, :]).then_inc(s_const, 1)
            link(ts_(pid_i[:, 1:2], pid_i[:, 0:1], C - 1, None, ALU.bitwise_and))
            link(ts_(pid_i[:, 2:3], pid_i[:, 0:1], RK - 1, None, ALU.bitwise_and))
            link(ts_(pid_i[:, 3:4], pid_i[:, 0:1], 1, None, ALU.bitwise_and))
            link(nc.vector.tensor_copy(pid_f[:, :], pid_i[:, :]))
            link(nc.vector.tensor_copy(oddp[:, :], pid_f[:, 3:4]))
            link(tt(m16[:, 0, :], m16[:, 0, :], m16[:, 1, :], ALU.add))
            dve.wait_ge(dma["ids"], 64)
            link(nc.vector.tensor_copy(ids_f[:, :, :], ids_i[:, :, :]))
            for i, m in enumerate((m32, m32, m16[:, 0, :], m32)):
                ids = ids_f[:, i, :].rearrange("p (t j) -> p t j", j=BT)
                link(ts_(sel[:, i, :], ids[:, :, 0], m[:, 0:1], None, ALU.mult))
                for j in range(1, BT):
                    link(stt(sel[:, i, :], ids[:, :, j], m[:, j:j + 1], sel[:, i, :], ALU.mult, ALU.add))
            link(ts_(sel[:, 4, :], sel[:, 0, :], float(C), pid_f[:, 1:2], ALU.mult, ALU.add))
            link(nc.vector.tensor_copy(idx_w[:, :], sel[:, 4, :]))
            link(ts_(sel[:, 4, :], sel[:, 2, :], float(RK), pid_f[:, 2:3], ALU.mult, ALU.add))
            link(nc.vector.tensor_copy(idx_l[:, :], sel[:, 4, :]))
            link(ts_(sel[:, 4, :], sel[:, 3, :], pid_f[:, 1:2], None, ALU.is_gt))
            tt(mch[:, :, :], sel[:, 4, :].unsqueeze(2).to_broadcast([P, NT, BT]),
               m32[:, :].unsqueeze(1).to_broadcast([P, NT, BT]), ALU.mult).then_inc(s_ids, 1)
            ts_(onehot[:, :], ids_f[0:NS, 0, :], pid_f[0:NS, 0:1], None, ALU.is_equal).then_inc(s_ids, 1)

            def setup_lo(k, dst, src, hi, eng_sem=s_setup_lo):
                dve.wait_ge(s_setup_hi, k + 1)
                lo_of(dst, src, hi).then_inc(eng_sem, 1)

            for j in range(KC):
                setup_lo(j, WT[:, 1, j, :], ps[j % 4][:, :], WT[:, 0, j, :])

            for j in range(KC):
                setup_lo(KC + j, ATG[:, 1, j, :], ps[j % 4][:, :], ATG[:, 0, j, :])
            dve.wait_ge(dma["qz"], 32)
            qzi = mask16[:, 0:2 * (D // 8)].bitcast(I32)
            for e in range(8):
                link(ts_(qzi, qz_i[:, :], 4 * e, 15, ALU.logical_shift_right, ALU.bitwise_and))
                link(nc.vector.tensor_copy(zero16[:, :].rearrange("p (m e) -> p m e", e=8)[:, :, e], qzi))
            dve.wait_ge(dma["q"], 16)
            link(ts_(q_i[64:P, :], q_i[64:P, :], 4, None, ALU.logical_shift_right))
            dve.wait_ge(s_sp, 1)
            nc.vector.tensor_copy(bsess[:, :], ps_s[:, 0:2 * NT]).then_inc(s_sv, 1)
            dve.wait_ge(s_sp, 2)
            link(nc.vector.tensor_copy(liT[:, :], ps_z[0:R32, 0:NE]))
            nc.vector.tensor_copy(fAT[:, :, :].rearrange("r j p -> r (j p)"), ps_s[0:R32, :]).then_inc(s_sv, 1)
            for s in range(2):
                nc.vector.tensor_copy(Rz[:, s, :, 0:NE], WT[:, s, :, 0:NE].bitcast(F32))
                nc.vector.memset(Rz[:, s, :, NZ:ZW].bitcast(F32), 0.0)
            link(nc.vector.tensor_copy(Rz[:, 0, :, 2 * NE:NZ], fA[:, :, :]))
            link(lo_of(Rz[:, 1, :, 2 * NE:NZ], fA[:, :, :], Rz[:, 0, :, 2 * NE:NZ]))
            dve.wait_ge(s_sp, 3)
            d2 = ps_s[:, 0:KC * NE].rearrange("p (j e) -> p j e", e=NE)
            link(nc.vector.tensor_copy(Rz[:, 0, :, NE:2 * NE], d2))
            lo_of(Rz[:, 1, :, NE:2 * NE], d2, Rz[:, 0, :, NE:2 * NE]).then_inc(s_sv, 1)
            dve.wait_ge(dma["bb"], 16)
            bbw = bb_raw[:, :].unsqueeze(2).to_broadcast([P, KC, P])
            link(nc.vector.tensor_copy(bbB[:, 0, :, :], bbw))
            tt(bbB[:, 1, :, :], bbw, bbB[:, 0, :, :].bitcast(F32), ALU.subtract).then_inc(s_bbB, 1)
            dve.wait_ge(s_sp, GZ)
            gz = ps_s[:, 0:KC * ZW].rearrange("p (k w) -> p k w", w=ZW)
            for par in range(2):
                link(nc.vector.tensor_copy(azv[:, par, :, 0, RH:AZW], gz))
                g = lo_of(azv[:, par, :, 1, RH:AZW], gz, azv[:, par, :, 0, RH:AZW])
                if par == 0:
                    link(g)
                else:
                    g.then_inc(s_sv, 1)
            dve.wait_ge(s_sv, GZ)
            dve.wait_ge(s_lzp, 1)
            for m in range(KC):
                dve.wait_ge(s_setup_hi, 2 * KC + m + 1)
                lo_of(L_st[:, m % 2, D:2 * D], ps[m % 4][:, :], L_st[:, m % 2, 0:D]).then_inc(s_chain, 1)
                count[0] += 1
                lzp = ps_x[:, m * ZW:m * ZW + ZW]
                link(nc.vector.tensor_copy(L_st[:, m % 2, 2 * D:2 * D + ZW], lzp))
                lo_of(L_st[:, m % 2, 2 * D + ZW:2 * D + 2 * ZW], lzp,
                      L_st[:, m % 2, 2 * D:2 * D + ZW]).then_inc(s_setup_lo, 1)
                if m == 0:
                    dve.wait_ge(dma["sc"], 32)
                link(ts_(q_nib, q_i, 8 * m, 15, ALU.logical_shift_right, ALU.bitwise_and))
                link(tt(f16[:, :], q_nib, zero16[:, :], ALU.subtract))
                w = tt(W16[:, m, :], f16[:, :], scale16[:, :], ALU.mult)
                if m < KC - 1:
                    link(w)
                else:
                    w.then_inc(s_deq, 1)
            dve.wait_ge(dma["Bm"], 16)
            link(ts_(bm_raw[:, :], bm_raw[:, :], 0.5, None, ALU.mult))
            link(nc.vector.tensor_copy(Bstk[:, :], bm_raw[:, :]))
            link(lo_of(Bstk[P // 2:P, :], bm_raw[P // 2:P, :], Bstk[P // 2:P, :]))
            dve.wait_ge(s_sp, CZ)
            dve.wait_ge(dma["bz_in"], 16)
            link(nc.vector.tensor_copy(cz[:, :], ps_s[:, 0:NZ]))
            tt(cz[:, 0:NE], cz[:, 0:NE], bz[:, :], ALU.add).then_inc(s_sv, 1)
            dve.wait_ge(s_sp, CROW)
            dve.wait_ge(dma["crow_in"], 16)
            tt(crow, crow, ps_f[:, :], ALU.add).then_inc(s_sv, 1)
            dve.wait_ge(s_sv, CROW)
            last = slice(3 * R32, P)
            link(nc.vector.tensor_copy(f32r_row[last, :], crow[last, :]))
            link(lo_of(crow[last, :], crow[last, :], f32r_row[last, :]))
            link(ts_(crow[last, :], crow[last, :], rowsel[last, 1:2], None, ALU.mult))
            stt(Bstk[last, :], f32r_row[last, :].bitcast(F32), rowsel[last, 0:1], crow[last, :],
                ALU.mult, ALU.add).then_inc(s_bst, 1)
            dve.wait_ge(dma["w2"], 16 * 3)
            dve.wait_ge(dma["bias"], 16)

            def stages(n):
                if n.on(2):
                    dve.wait_ge(s_f16, n.tile(2, 1))
                    tt(f16[:, :], f16[:, :], bias16[:, :], ALU.add).then_inc(s_b16, 1)
                if n.on(3):
                    if n.past(3, 1):
                        dve.wait_ge(s_zh, n.tile(3))
                    dve.wait_ge(s_zlo, n.tile(3, 1))
                    tt(zsum[:, :], ps_z[:, 0:AZW], zlo[:, :], ALU.add).then_inc(s_zsum, 1)
                if n.on(2):
                    t, par = n.tile(2), n.par(2)
                    dve.wait_ge(s_b16, n.tile(2, 1))
                    if n.past(2, 2):
                        dve.wait_ge(s_x1st[par], 16 * n.half(2))
                        dve.wait_ge(s_xTp, n.tile(2, -1))
                    tt(x1s[:, par, :], x_all[:, t, :], f16[:, :], ALU.add).then_inc(s_x1, 1)
                if n.on(3):
                    dve.wait_ge(s_zsum, n.tile(3, 1))
                    tt(hmf[:, :], zsum[:, 0:RH], hmask[:, :, :].rearrange("p j r -> p (j r)"), ALU.mult).then_inc(s_hm, 1)
                if n.on(1):
                    t = n.tile(1)
                    dve.wait_ge(s_mask, n.tile(1, 1))
                    dve.wait_ge(s_cond, n.tile(1, 1))
                    if n.past(1, 1):
                        dve.wait_ge(s_ctp, t)
                    stt(c16[:, :].rearrange("p (e w) -> p w e", e=8), ps_c[:, :].rearrange("p (w e) -> p w e", e=8),
                        b2col[:, :], mask16[:, :].rearrange("p (w e) -> p w e", e=8), ALU.add, ALU.mult).then_inc(s_c16, 1)
                if n.on(3):
                    dve.wait_ge(s_hm, n.tile(3, 1))
                    if n.past(3, 1):
                        dve.wait_ge(s_hTp, n.tile(3))
                    nc.vector.tensor_copy(hs[:, 0, 0:RH].bitcast(F32R), hmf[:, :]).then_inc(s_hh, 1)
                    dve.wait_ge(s_hh, n.tile(3, 1))
                    tt(hs[:, 0, RH:2 * RH], hmf[:, :], hs[:, 0, 0:RH], ALU.subtract).then_inc(s_hs, 1)
                if n.on(1):
                    t = n.tile(1)
                    dve.wait_ge(s_ctp, n.tile(1, 1))
                    if n.past(1, 1):
                        dve.wait_ge(s_ffn, t)
                    nc.vector.tensor_copy(cT16[:, :], ps_ct[:, 0:D]).then_inc(s_cT, 1)
                if n.on(0):
                    if n.past(0, 1):
                        dve.wait_ge(s_c16, n.tile(0))
                    ts_(mask16[:, :], iota16[:, :], sel[:, 1, bass.ds(n.tile(0), 1)], None, ALU.is_lt).then_inc(s_mask, 1)
                if n.on(2):
                    par = n.par(2)
                    dve.wait_ge(s_hi, n.tile(2, 1))
                    lo_of(xT[:, par, KC:2 * KC, :].rearrange("p k c -> p (k c)"), ps_x[:, :],
                          xT[:, par, 0:KC, :].rearrange("p k c -> p (k c)")).then_inc(s_lo, 1)
                if n.on(3):
                    dve.wait_ge(s_l48, n.tile(3, 1))
                    tt(zall[:, n.tile(3), :], zsum[:, RH:RH + NZ], ps_s[:, P:P + NZ], ALU.add).then_inc(s_zh, 1)
            run_phase_a(dve, stages)

            dve.wait_ge(s_zh, NT)
            link(tt(zall[:, :, :], zall[:, :, :], cz[:, :].unsqueeze(1).to_broadcast([P, NT, NZ]), ALU.add))
            for par in range(2):
                dve.wait_ge(s_x1st[par], 16 * NT // 2)
            steps = [0]

            def signal(ins):
                steps[0] += 1
                ins.then_inc(s_rv, 1)
                dve.wait_ge(s_rv, steps[0])

            ne3 = [P, NT, NE]

            def v(i):
                return rt[:, i, :].rearrange("p (t e) -> p t e", e=NE)

            def col(i):
                return rt[:, 7, i * NT:(i + 1) * NT]

            def bc(ap):
                return ap.unsqueeze(2).to_broadcast(ne3)

            Hs, dl = zall[:, :, 0:NE], zall[:, :, NE:2 * NE]
            for i, src in enumerate((Hs, dl)):
                link(ts_(v(i), src, oddp[:, 0:1], None, ALU.mult))
            link(nc.vector.tensor_reduce(small[:, 0:1], v(0), AX.XY, ALU.max, apply_absolute_value=True))
            signal(nc.vector.tensor_reduce(small[:, 1:2], v(1), AX.XY, ALU.max, apply_absolute_value=True))
            dve.wait_ge(s_rp, 1)
            link(nc.vector.tensor_reduce(small[0:2, 2:3], ps_s[0:2, 0:P], AX.X, ALU.max))
            link(ts_(small[0:2, 3:4], small[0:2, 2:3], EPS, None, ALU.max))
            link(nc.vector.reciprocal(small[0:2, 4:5], small[0:2, 3:4]))
            signal(ts_(small[0:2, 6:8], ident[0:2, 0:2], small[0:2, 4:5], 0.5, ALU.mult, ALU.mult))
            dve.wait_ge(s_rp, 2)
            link(nc.vector.tensor_copy(small[:, 8:10], ps_s[:, 0:2]))
            link(ts_(v(0), Hs, small[:, 8:9], None, ALU.mult))
            link(stt(v(0), dl, small[:, 9:10], v(0), ALU.mult, ALU.add))
            link(nc.vector.tensor_reduce(col(0), v(0), AX.X, ALU.max))
            signal(tt(v(0), v(0), bc(col(0)), ALU.subtract))
            dve.wait_ge(s_ra, 1)
            link(nc.vector.tensor_reduce(col(1), v(1), AX.X, ALU.add))
            link(nc.vector.reciprocal(col(2), col(1)))
            link(tt(v(2), v(1), bc(col(2)), ALU.mult))
            link(nc.vector.tensor_reduce(col(3), v(2), AX.X, ALU.max))
            link(tt(v(5), v(2), bc(col(3)), ALU.is_equal))
            link(nc.vector.tensor_reduce(col(4), v(5), AX.X, ALU.add))
            link(stt(v(6), v(5), -2.0, v(2), ALU.mult, ALU.add))
            link(nc.vector.tensor_reduce(col(5), v(6), AX.X, ALU.max))
            link(stt(col(6), col(4), 2.0, col(3), ALU.is_ge, ALU.mult))
            link(tt(col(7), col(5), col(6), ALU.max))
            signal(tt(v(4), v(2), bc(col(7)), ALU.subtract))
            for k in range(2):
                dve.wait_ge(s_Ghi, k + 1)
                lo_of(ATG[:, 1, k, :], ps[k % 2][:, :], ATG[:, 0, k, :]).then_inc(s_Glo, 1)
            dve.wait_ge(dma["lrow"], 16)
            link(tt(BD.rearrange("p (t r) -> p t r", t=NT), blk[:, :, 0:1].to_broadcast([P, NT, R32]),
                    lrow[:, :].unsqueeze(1).to_broadcast([P, NT, R32]), ALU.mult))
            dve.wait_ge(s_ra, 2)
            link(ts_(v(3), v(3), 1.0, None, ALU.add))
            link(nc.vector.reciprocal(v(4), v(3)))
            link(tt(v(2), v(2), v(4), ALU.mult))
            link(nc.vector.tensor_reduce(col(0), v(2), AX.X, ALU.add))
            link(ts_(col(1), col(0), WEPS, None, ALU.add))
            link(nc.vector.reciprocal(col(2), col(1)))
            signal(tt(v(2), v(2), bc(col(2)), ALU.mult))
            for k in range(2, KC):
                dve.wait_ge(s_Ghi, k + 1)
                lo_of(ATG[:, 1, k, :], ps[k % 2][:, :], ATG[:, 0, k, :]).then_inc(s_Glo, 1)
            dve.wait_ge(s_rp, 3)
            signal(nc.vector.tensor_copy(rt[:, 5, :].rearrange("p (n a) -> p n a", a=2),
                                         ps_s[:, 0:P].rearrange("p (n a) -> p n a", a=2)[:, :, 1:2].to_broadcast([P, P // 2, 2])))
            dve.wait_ge(s_rp, 4)
            link(tt(zw, zall[:, :, 2 * NE:NZ], ps_z[:, :].rearrange("p (t r) -> p t r", t=NT), ALU.mult))
            dve.wait_ge(s_Gp, KC)
            for q in range(4):
                tiles = slice(4 * q, 4 * q + 4)
                z4 = zw[:, tiles, :].unsqueeze(2)
                nc.vector.tensor_copy(zp[:, tiles, 0:3:2, :].bitcast(F32R), z4.to_broadcast([P, 4, 2, R32])).then_inc(s_zph, 1)
                dve.wait_ge(s_zph, q + 1)
                tt(zp[:, tiles, 1:2, :].bitcast(F32R), z4, zp[:, tiles, 0:1, :], ALU.subtract).then_inc(s_zs, 1)

            def finish(t, u):
                dve.wait_ge(s_main, t + 1)
                tt(x_all[:, t, :], x_all[:, t, :], main_bank(u)[:, :], ALU.add).then_inc(s_out_r, 1)

            with dve.Fori(0, NT // 4) as k:
                for u in range(4):
                    finish(4 * k + u, u)

        @block.tensor
        def _(pe):
            mm = nc.tensor.matmul

            def split_product(dst, lhs, rhs, start=True, stop=True):
                n = 0
                for j in range(KC):
                    for a, c in ((0, 0), (0, 1), (1, 0)):
                        last = mm(dst, lhs(a, j), rhs(c, j), start=start and n == 0, stop=stop and n == 3 * KC - 1)
                        n += 1
                return last

            pe.wait_ge(s_const, 1)
            pe.wait_ge(dma["W"], 16)
            for j in range(KC):
                for m in range(KC):
                    last = nc.tensor.transpose(ps[j][:, m * P:(m + 1) * P],
                                               W_raw[:, m, :].rearrange("p (c j) -> p j c", j=KC)[:, j, :], ident[:, :])
                last.then_inc(s_setup_ps, 1)
            pe.wait_ge(dma["lA"], 16)
            for k in range(KC):
                pe.wait_ge(s_setup_lo, k + 1)
                for m in range(KC):
                    last = nc.tensor.transpose(ps[k][:, m * P:(m + 1) * P], lA_raw[:, m, k * P:(k + 1) * P], ident[:, :])
                last.then_inc(s_setup_ps, 1)
            pe.wait_ge(s_ids, 2)
            pe.wait_ge(dma["bsess_in"], 16)
            oh = onehot[:, :].rearrange("s (n a) -> s a n", a=2)
            for a in range(2):
                last = mm(ps_s[HID * a:HID * a + HID, 0:2 * NT], b_raw[:, :], oh[:, a, :], start=True, stop=True)
            last.then_inc(s_sp, 1)
            pe.wait_ge(dma["li"], 16)
            pe.wait_ge(dma["fA"], 16)
            pe.wait_ge(s_sv, BSESS)
            nc.tensor.transpose(ps_z[0:R32, 0:NE], li_raw[:, :], ident[0:NE, 0:NE])
            for j in range(KC):
                last = nc.tensor.transpose(ps_s[0:R32, j * P:(j + 1) * P], fA[:, j, :], ident[:, :])
            last.then_inc(s_sp, 1)
            pe.wait_ge(s_sv, LIT)
            for j in range(KC):
                last = mm(ps_s[:, j * NE:(j + 1) * NE], fAT[:, j, :], liT[:, :], start=j == 0, stop=j == KC - 1,
                          skip_group_check=True)
            last.then_inc(s_sp, 1)
            pe.wait_ge(s_sv, D2)
            pe.wait_ge(s_Wb_lo, KC)
            for k in range(KC):
                last = split_product(ps_s[:, k * ZW:(k + 1) * ZW], lambda a, j: Wbs[:, a, j, k * P:(k + 1) * P],
                                     lambda a, j: Rz[:, a, j, :])
            last.then_inc(s_sp, 1)
            pe.wait_ge(s_lB_lo, KC)
            for m in range(KC):
                rows = slice(m * P, (m + 1) * P)
                last = split_product(ps_x[:, m * ZW:m * ZW + ZW], lambda a, j: lBs[:, a, j, rows], lambda a, j: Rz[:, a, j, :])
            last.then_inc(s_lzp, 1)
            for m in range(KC):
                pe.wait_ge(s_setup_lo, KC + m + 1)
                rows = slice(m * P, (m + 1) * P)
                last = split_product(ps[m % 4][:, :], lambda a, j: lBs[:, a, j, rows], lambda a, j: WT[:, a, j, :])
                last.then_inc(s_setup_ps, 1)
            pe.wait_ge(s_bbB, 1)
            pe.wait_ge(s_sv, GZ)
            last = split_product(ps_s[:, 0:ZW], lambda a, j: bbB[:, a, j, :], lambda a, j: Rz[:, a, j, :])
            last.then_inc(s_sp, 1)
            pe.wait_ge(s_setup_lo, 3 * KC)
            last = split_product(ps_f[:, :], lambda a, j: bbB[:, a, j, :], lambda a, j: WT[:, a, j, :])
            last.then_inc(s_sp, 1)
            pe.wait_ge(s_sv, CROW)
            pe.wait_ge(dma["w2"], 16 * 3)
            pe.wait_ge(dma["x0"], 16)
            pe.wait_ge(s_deq, 1)

            def hidden(n, p):
                t = n.tile(0)
                if p == 0:
                    pe.wait_ge(s_wbd, n.tile(0, 1))
                if n.past(0, 1):
                    pe.wait_ge(s_gelu, 2 * t + (p - 1))
                mm(ps_hid[p][:, :], wbd[:, n.par(0), 2 * p:2 * p + 2, :].rearrange("p a h -> p (a h)"),
                   x_all[:, t, :], start=True, stop=True).then_inc(s_hid, 1)

            def stages(n):
                if isinstance(n.k, int) and n.c == 3:
                    for g in ("x1", "x2", "x3"):
                        pe.wait_ge(dma[g], 16)
                if n.on(3):
                    t, par = n.tile(3), n.par(3)
                    pe.wait_ge(s_lo, n.tile(3, 1))
                    pe.wait_ge(s_az, n.tile(3, 1))
                    if n.past(3, 1):
                        pe.wait_ge(s_zsum, t)
                    for k in range(KC):
                        if k == KC - 1:
                            for kk in range(KC):
                                mm(ps_z[:, 0:AZW], xT[:, par, KC + kk, :], azv[:, par, kk, 0, :],
                                   start=False, stop=False, skip_group_check=True)
                        last = mm(ps_z[:, 0:2 * AZW], xT[:, par, k, :], azv[:, par, k, :, :].rearrange("p s w -> p (s w)"),
                                  start=k == 0, stop=k == KC - 1, skip_group_check=True)
                    last.then_inc(s_hz, 1)
                if n.on(1):
                    t = n.tile(1)
                    pe.wait_ge(s_gelu, 2 * t + 2)
                    if n.past(1, 1):
                        pe.wait_ge(s_c16, t)
                    for p in range(2):
                        last = mm(ps_c[2 * C * p:2 * C * p + 2 * C, :], W2bd[:, :, :].rearrange("p a s -> p (a s)"),
                                  gel[:, p, :], start=True, stop=True)
                    last.then_inc(s_cond, 1)
                if n.on(0):
                    hidden(n, 0)
                if n.on(2):
                    t, par = n.tile(2), n.par(2)
                    pe.wait_ge(s_x1, n.tile(2, 1))
                    if n.past(2, 1):
                        pe.wait_ge(s_lo, t)
                    for k in range(KC):
                        last = nc.tensor.transpose(ps_x[:, k * P:(k + 1) * P], x1s[:, par, k * P:(k + 1) * P], ident[:, :])
                    last.then_inc(s_xTp, 1)
                if n.on(1):
                    t = n.tile(1)
                    pe.wait_ge(s_c16, n.tile(1, 1))
                    if n.past(1, 1):
                        pe.wait_ge(s_cT, t)
                    for c in range(KC):
                        last = nc.tensor.transpose(ps_ct[:, c * P:(c + 1) * P], c16[:, c * P:(c + 1) * P], ident16[:, :])
                    last.then_inc(s_ctp, 1)
                if n.on(0):
                    hidden(n, 1)
                if n.on(3):
                    pe.wait_ge(s_hs, n.tile(3, 1))
                    if n.past(3, 1):
                        pe.wait_ge(s_zh, n.tile(3))
                    nc.tensor.transpose(ps_s[:, 0:P], hs[:, 0, :], ident[:, :]).then_inc(s_hTp, 1)
                if n.on(1):
                    t = n.tile(1)
                    pe.wait_ge(s_cT, n.tile(1, 1))
                    if n.past(1, 1):
                        pe.wait_ge(s_f16, t)
                    for c in range(KC):
                        last = mm(ps_f[:, :], cT16[:, c * P:(c + 1) * P], W16[:, c, :], start=c == 0, stop=c == KC - 1)
                    last.then_inc(s_ffn, 1)
                if n.on(3):
                    par = n.par(3)
                    pe.wait_ge(s_hT, n.tile(3, 1))
                    pe.wait_ge(s_lzd[par], 16 * n.half(3, 1))
                    for c in range(2):
                        last = mm(ps_s[:, P:P + ZW], xT[:, par, NX - 1, :], lz[:, par, c * ZW:(c + 1) * ZW],
                                  start=c == 0, stop=c == 1, skip_group_check=True)
                    last.then_inc(s_l48, 1)
            run_phase_a(pe, stages)

            def G_rows(k):
                if k >= 2:
                    pe.wait_ge(s_Glo, k - 1)
                split_product(ps[k % 2][:, :], lambda a, j: Wbs[:, a, j, k * P:(k + 1) * P],
                              lambda a, j: WT[:, a, j, :]).then_inc(s_Gp, 1)

            def main_x(u, operands, with_G=False):
                q = 0
                for j in range(KC):
                    if with_G:
                        pe.wait_ge(s_Glo, j + 1)
                    for a, c in ((0, 0), (0, 1), (1, 0)):
                        mm(main_bank(u)[:, :], operands[:, a * KC + j, :], ATG[:, c, j, :], start=q == 0, stop=False)
                        q += 1

            def main_rest(k, u, operands, zt):
                dst = main_bank(u)[:, :]
                pe.wait_ge(s_lhd[u], 16 * k + 16)
                mm(dst, operands[:, NX - 1, :], L_rows[u][:, 0, :], start=False, stop=False)
                pe.wait_ge(s_lld[u], 16 * k + 16)
                mm(dst, operands[0:RH, NX - 1, :], L_rows[u][0:RH, 1, :], start=False, stop=False)
                mm(dst, zt, Bstk[:, :], start=False, stop=True).then_inc(s_main, 1)

            G_rows(0)
            pe.wait_ge(s_rv, R_MAX)
            mm(ps_s[0:2, 0:P], small[:, 0:2], ident[:, :], start=True, stop=True).then_inc(s_rp, 1)
            pe.wait_ge(s_rv, R_SCALE)
            mm(ps_s[:, 0:2], ones2[:, :], small[0:2, 6:8], start=True, stop=True).then_inc(s_rp, 1)
            for k in range(1, KC):
                G_rows(k)
            for par in range(2):
                pe.wait_ge(s_xTst[par], 16 * NT // 2)
            main_x(0, xT_all[:, 0], with_G=True)
            pe.wait_ge(s_rv, R_W)
            nc.tensor.transpose(ps_s[:, 0:P], rt[:, 2, :], ident[:, :]).then_inc(s_rp, 1)
            main_x(1, xT_all[:, 1])
            pe.wait_ge(s_rv, R_WT)
            mm(ps_z[:, :], rt[:, 5, :], BD, start=True, stop=True).then_inc(s_rp, 1)
            main_x(2, xT_all[:, 2])
            main_x(3, xT_all[:, 3])
            pe.wait_ge(s_zones, 2)
            for q in range(4):
                pe.wait_ge(s_zs, q + 1)
                if q >= 2:
                    pe.wait_ge(s_zTs, q - 1)
                for i in range(4):
                    last = nc.tensor.transpose(z_banks[q % 2][:, i * P:(i + 1) * P],
                                               zp[:, 4 * q + i, :, :].rearrange("p a r -> p (a r)"), ident[:, :])
                last.then_inc(s_zTp, 1)
            pe.wait_ge(s_bst, 1)
            for u in range(4):
                if u == 0:
                    pe.wait_ge(s_zTs, 4)
                main_rest(0, u, xT_all[:, u], zT[:, u, :])
            with pe.Fori(1, NT // 4) as k:
                for u in range(4):
                    pe.wait_ge(s_out_r, 4 * k + (u - 3))
                    pe.wait_ge(s_xc, 4 * k + (u - 3))
                    main_x(u, xT[:, u % 2])
                    pe.wait_ge(s_zc, 4 * k + (u - 3))
                    main_rest(k, u, xT[:, u % 2], zTu[:, u % 2, :])


INPUTS = ['x', 'itok_B_0_7', 'itok_B_2182_4065', 'itok_B_6_15', '_lenS',
          'L0_cond_W_sess', 'L0_cond_b_sess', 'L0_cond_W2', 'L0_cond_b2',
          'L0_ffn_qweight', 'L0_ffn_qzeros', 'L0_ffn_scales', 'L0_ffn_bias',
          'L1_cond_base_weight', 'L1_cond_base_bias', 'L1_cond_lora_A_w', 'L1_cond_lora_B_w',
          'L1_ffn_W', 'L1_ffn_b', 'L1_ffn_A', 'L1_ffn_Bmat', 'L1_ffn_LiMEs']


def kernel(**inputs):
    import numpy as np
    import concourse.bacc as bacc
    from concourse.bass_utils import run_bass_kernel_spmd as run

    nc = bacc.Bacc("TRN2", target_bir_lowering=False, num_devices=1)
    arrays, args = {}, []
    for name in INPUTS:
        a = np.ascontiguousarray(inputs[name])
        arrays["in_" + name] = a
        args.append(nc.dram_tensor("in_" + name, a.shape, mybir.dt.from_np(a.dtype), kind="ExternalInput").ap())
    args.append(nc.dram_tensor("out_0", inputs["x"].shape, mybir.dt.float32, kind="ExternalOutput").ap())
    adaln_ffn_program(nc, *args)
    return run(nc, [arrays], core_ids=[0]).results[0]["out_0"]
```

```python
from contextlib import ExitStack

import concourse.bass as bass
from concourse import mybir

F32 = mybir.dt.float32
F32R = mybir.dt.float32r
F16 = mybir.dt.float16
I32 = mybir.dt.int32
ALU = mybir.AluOpType
ACT = mybir.ActivationFunctionType
AX = mybir.AxisListType

P = 128


def adaln_ffn_program(nc, x, sess_ids, seq_lens, lora_ids, chan_counts, W_sess, b_sess, W2, b2,
                      qweight, qzeros, scales, bias16_in, Wb, bb, lora_A, lora_B, W, b, A, Bmat, LiMEs, out):
    NB, C, D = x.shape
    NT = NB * C // P
    BT = P // C
    NS, _, HID = W_sess.shape
    NA, RK, _ = lora_A.shape
    KC = D // P
    R32, NE = A.shape[1], LiMEs.shape[0]
    RH = BT * RK
    NZ = 2 * NE + R32
    ZW = 64
    AZW = RH + ZW
    NX = 2 * KC + 1
    EPS, WEPS = 1e-6, 1e-9
    DEPTH = 3

    x_rows = x.rearrange("b c t -> (b c) t")
    out_rows = out.rearrange("b c t -> (b c) t")
    L_hi_dram = nc.dram_tensor("L_hi_dram", [NA * RK, D], F32).ap()
    L_lo_dram = nc.dram_tensor("L_lo_dram", [NA * RK, D], F32).ap()
    L_z_dram = nc.dram_tensor("L_z_dram", [NA * RK, 2 * ZW], F32).ap()

    with ExitStack() as ctx:
        def sb(name, shape, dt):
            return ctx.enter_context(nc.sbuf_tensor(name, shape, dt))

        def sem(name):
            return ctx.enter_context(nc.semaphore(name))

        x_all = sb("x_all", [P, NT, D], F32)
        xT_all = sb("xT_all", [P, NT, NX, P], F32R)
        ATG = sb("ATG", [P, 2, KC, D], F32R)
        WT = sb("WT", [P, 2, KC, D], F32R)
        Wbs = sb("Wbs", [P, 2, KC, D], F32R)
        xT = sb("xT", [P, 2, NX, P], F32R)
        az = sb("az", [P, 2 * KC * 2 * AZW], F32R)
        gel = sb("gel", [P, 2, D], F32)
        x1s = sb("x1s", [P, 2, D], F32)
        wide = sb("wide", [P, D], F32)
        zlo = sb("zlo", [P, AZW], F32)
        W16 = sb("W16", [P, KC, D], F16)
        c16 = sb("c16", [P, D], F16)
        cT16 = sb("cT16", [P, D], F16)
        f16 = sb("f16", [P, D], F16)
        mask16 = sb("mask16", [P, D], F16)
        iota16 = sb("iota16", [P, D], F16)
        bias16 = sb("bias16", [P, D], F16)
        wsel = sb("wsel", [P, 2, HID], F32)
        wbd = sb("wbd", [P, 2, BT, HID], F32)
        lz = sb("lz", [P, 2, 2 * ZW], F32R)
        cz = sb("cz", [P, NZ], F32)
        zall = sb("zall", [P, NT, NZ], F32)
        Bstk = sb("Bstk", [P, D], F32R)
        Rz = sb("Rz", [P, 2, KC, ZW], F32R)
        ident = sb("ident", [P, P], F32)
        ident16 = sb("ident16", [P, P], F16)
        ids_i = sb("ids_i", [P, 4, NB], I32)
        ids_f = sb("ids_f", [P, 4, NB], F32)
        m32 = sb("m32", [P, BT], F32)
        m16 = sb("m16", [P, 2, BT], F32)
        m4 = sb("m4", [P, 4, BT], F32)
        hmask = sb("hmask", [P, BT, RK], F32)
        blk = sb("blk", [P, NT, NE], F32)
        sel = sb("sel", [P, 5, NT], F32)
        idx_w = sb("idx_w", [P, NT], I32)
        idx_l = sb("idx_l", [P, NT], I32)
        idxw = sb("idxw", [P, 2], I32)
        idxl = sb("idxl", [P, 4], I32)
        pid_i = sb("pid_i", [P, 4], I32)
        pid_f = sb("pid_f", [P, 4], F32)
        mch = sb("mch", [P, NT, BT], F32)
        bsess = sb("bsess", [P, NT * 2], F32)
        W2bd = sb("W2bd", [P, 2, C], F32)
        b2col = sb("b2col", [P, 1], F32)
        fA = sb("fA", [P, KC, R32], F32)
        liT = sb("liT", [R32, NE], F32)
        bb_raw = sb("bb_raw", [P, KC], F32)
        bz = sb("bz", [P, NE], F32)
        hmf = sb("hmf", [P, RH], F32)
        hs = sb("hs", [P, 2, P], F32)
        small = sb("small", [P, 16], F32)
        oddp = sb("oddp", [P, 1], F32)

        W_raw = gel, x1s
        Wb_raw = x_all[:, 4:8, :]
        lA_raw = x_all[:, 8:12, :]
        lB_raw = x_all[:, 12:16, :].rearrange("p s (a j r) -> p (s a) j r", j=KC, r=RK)
        xT_flat = xT_all[:, :, :, :].rearrange("p t k c -> p (t k c)")
        lBs = xT_flat[:, 12 * NX * P:12 * NX * P + 2 * KC * D].rearrange("p (s j n) -> p s j n", s=2, j=KC)
        bbB = xT_flat[:, 11 * NX * P:11 * NX * P + 2 * KC * P].rearrange("p (s j n) -> p s j n", s=2, j=KC)
        early = xT_flat[:, 4 * NX * P:4 * NX * P + 6 * D].rearrange("p (i n) -> p i n", i=6)
        q_i, q_nib = wide[:, :].bitcast(I32), [x1s[:, i, :].bitcast(I32) for i in range(2)]
        f32r_row = early[:, 5, :]
        bm_raw, crow = wide[:, :], wide[:, :]
        zall_flat = zall[:, :, :].rearrange("p t c -> p (t c)")
        sel_terms = zall_flat[:, 0:4 * NB].rearrange("p (i t j) -> p i t j", i=4, j=BT)
        fAT = zall_flat[0:R32, 4 * NB:4 * NB + D].rearrange("r (j p) -> r j p", j=KC)
        qz_i = zlo[:, 0:D // 8].bitcast(I32)
        qz_nib = x1s[:, 1, :].bitcast(I32).rearrange("p (e m) -> p e m", e=8)
        L_st = early[:, 0:4, :].rearrange("p (m s) n -> p m s n", m=2)
        Lz_st = early[:, 4, :].rearrange("p (m s w) -> p m s w", m=KC, s=2)
        zero16, scale16 = c16, cT16
        G_zT, L_zT = x1s[0:ZW, 0, :], x1s[0:ZW, 1, :]
        azv = az[:, :].rearrange("p (b k s w) -> p b k s w", b=2, k=KC, s=2)
        L_az = az[:, 0:4 * D].rearrange("p (b s n) -> p b s n", b=2, s=2)
        L_rows = [L_az[:, 0], L_az[:, 1], WT[:, 0, 0:2, :], WT[:, 0, 2:4, :]]
        zp = Wbs[:, 0, :, :].rearrange("p k d -> p (k d)").rearrange("p (t a r) -> p t a r", t=NT, r=R32).bitcast(F32)
        zT = Wbs[:, 1, :, :].rearrange("p k d -> p (k d)").rearrange("p (t c) -> p t c", t=NT)
        BD = gel[:, 0, :]
        zw = gel[:, 1, :].rearrange("p (t r) -> p t r", t=NT)
        rt = x1s[:, :, :].rearrange("p a (b n) -> p (a b) n", n=NT * NE)
        lrow = sb("lrow", [P, R32], F32)
        rowsel = sb("rowsel", [P, 2], F32)
        zsum = sb("zsum", [P, AZW], F32)
        ones2 = hs[0:2, 1, :]
        zTu = lz
        onehot, b_raw = hs[0:NS, 0, 0:NB], hs[0:NS, 1, 0:HID]
        li_raw = hmf[0:NE, 0:R32]

        ps = [ctx.enter_context(nc.psum_tensor(f"ps{i}", [P, D], F32)) for i in range(7)]
        ps_ct = ctx.enter_context(nc.psum_tensor("ps_ct", [P, 2 * D], F16))
        ps_hid, ps_c, ps_f, ps_x, ps_z = ps[0:2], ps[2], ps[3], ps[4], ps[5]
        ps_s = ps[6]

        A_bank = ps_c, ps_f, ps_x, ps_z
        L_bank = ps_s, ps_x, ps_s, ps_s
        G_bank = main_bank = ps[0:4]
        z_banks = ps_x, ps_z

        names_dma = ["ids", "w2", "bsess_in", "W0", "W1", "fA", "li", "q", "qz", "sc", "bias", "lA", "lB", "Wb", "bb",
                     "crow_in", "bz_in", "Bm", "lrow", "x0", "x1", "x2", "x3"]
        dma = {n: sem("dma_" + n) for n in names_dma}
        s_L_st = [sem("L_stored0"), sem("L_stored1")]
        s_Bm_split = sem("Bm_split")
        s_Lz, s_Lz_st = sem("L_z_ready"), sem("L_z_stored")
        s_const, s_ids, s_deq, s_setup_ps, s_setup_hi, s_setup_lo = (sem(n) for n in (
            "const_ready", "ids_ready", "dequant_done", "setup_psum", "setup_hi", "setup_lo"))
        s_lB_hi, s_lB_lo, s_Wb_hi, s_Wb_lo = (sem(n) for n in ("lB_hi", "lB_lo", "Wb_hi", "Wb_lo"))
        s_sp, s_sv = sem("small_psum"), sem("small_evac")
        s_chain = sem("dve_chain")
        s_bbB = sem("bbB_ready")
        s_bst = sem("Bmat_split")
        s_pool = sem("pool_chain")
        s_masks, s_zlo, s_zsum = sem("masks_ready"), sem("z_lo_copied"), sem("h_summed")
        s_lzp, s_lzT = sem("L_z_psum"), sem("L_z_T_copied")
        s_gate = sem("gather_gate")
        s_wg = [sem("wsel_in0"), sem("wsel_in1")]
        s_lzd = [sem("lz_in0"), sem("lz_in1")]
        s_idxw, s_idxl, s_wbd, s_az = sem("idxw_ready"), sem("idxl_ready"), sem("wbd_ready"), sem("az_ready")
        s_hid, s_gelu, s_cond, s_mask, s_c16, s_ctp, s_cT, s_ffn, s_f16, s_b16, s_x1, s_xTp, s_hi, s_lo = (
            sem(n) for n in ("hid_psum", "gelu_done", "cond_psum", "tmask", "c16_ready", "ct_psum", "cT_ready",
                             "ffn_psum", "f16_ready", "f16_biased", "x1_ready", "x1T_psum", "x1T_hi", "x1T_lo"))
        s_hz, s_hm, s_hh, s_hs, s_hTp, s_hT, s_l48, s_zh = (
            sem(n) for n in ("hz_psum", "h_masked", "h_hi", "hs_ready", "hT_psum", "hT_ready", "z_psum", "z_ready"))
        s_x1st = [sem("x1_stored0"), sem("x1_stored1")]
        s_xTst = [sem("xT_stored0"), sem("xT_stored1")]
        s_rp, s_ra, s_rv = sem("routing_psum"), sem("routing_act"), sem("routing_dve")
        s_Gp, s_Ghi, s_Glo = sem("G_psum"), sem("G_hi"), sem("G_lo")
        s_li, s_lhd, s_lld = sem("L_idx"), [sem(f"L_hi_in{u}") for u in range(4)], [sem(f"L_lo_in{u}") for u in range(4)]
        s_xc, s_zc, s_zones, s_zph, s_zs, s_zTp, s_zTs, s_main, s_out_r = (
            sem(n) for n in ("xT_copied", "zT_copied", "zp_ones", "zp_hi", "zp_split", "zT_psum", "zT_ready", "main_psum", "out_ready"))
        s_out = sem("out_stored")
        block = ctx.enter_context(nc.Block())

        BSESS, LIT, D2, GZT, GZ, CZ, CROW = 1, 2, 3, 4, 5, 6, 7
        R_MAX, R_SCALE, R_LOGITS, R_DIFF, R_W, R_WT = 1, 2, 3, 4, 5, 6

        class Step:

            def __init__(self, k, c):
                self.k, self.c = k, c

            def on(self, s):
                return not isinstance(self.k, int) or 0 <= self.c - s < NT

            def tile(self, s, plus=0):
                return 2 * self.k + (self.c - s + plus)

            def half(self, s, plus=0):
                return self.k + ((self.c - s) // 2 + plus)

            def par(self, s):
                return (self.c - s) % 2

            def past(self, s, back):
                return not isinstance(self.k, int) or self.c - s - back >= 0

        FIRST = DEPTH + 2
        LAST = NT - 1

        def run_phase_a(eng, body, after=()):
            after = dict(after)
            for n in range(FIRST):
                body(Step(0, n))
                if n in after:
                    after[n]()
            with eng.Fori(0, (LAST - FIRST) // 2) as k:
                body(Step(k, FIRST))
                body(Step(k, FIRST + 1))
            for n in range(LAST, NT + DEPTH):
                body(Step(0, n))

        def row(v):
            return v.rearrange("(a n) -> a n", a=1)

        @block.sync
        def _(sp):
            def load_x(g):
                sp.dma_start(x_all[:, 4 * g:4 * g + 4, :],
                             x_rows[4 * g * P:4 * (g + 1) * P, :].rearrange("(a p) t -> p a t", p=P)).then_inc(dma[f"x{g}"], 16)

            def load_W(i):
                sp.dma_start(W_raw[i][:, :, :],
                             W[2 * i * P:2 * (i + 1) * P, :].rearrange("(m p) o -> p m o", p=P)).then_inc(dma[f"W{i}"], 16)

            load_W(0)
            for i, ids in ((0, sess_ids), (2, lora_ids)):
                sp.dma_start(ids_i[:, i, :], row(ids).to_broadcast([P, NB])).then_inc(dma["ids"], 16)
            load_W(1)
            sp.dma_start(b_raw, b_sess).then_inc(dma["bsess_in"], 16)
            load_x(0)
            sp.dma_start(Wb_raw, Wb.rearrange("(p j) d -> p j d", j=KC)).then_inc(dma["Wb"], 16)
            sp.dma_start(q_i, qweight.unsqueeze(0).to_broadcast([2, D // 8, D])).then_inc(dma["q"], 16)
            for h in range(2):
                half = slice(64 * h, 64 * h + 64)
                sp.dma_start(qz_i[half, :],
                             qzeros.unsqueeze(1).to_broadcast([KC, P // 8, D // 8])).then_inc(dma["qz"], 16)
                sp.dma_start(scale16[half, :],
                             scales.unsqueeze(1).to_broadcast([KC, P // 8, D])).then_inc(dma["sc"], 16)
            sp.wait_ge(s_idxw, 2)
            sp.dma_start(lA_raw, lora_A.rearrange("a r d -> (a r) d").rearrange("(m p) d -> p m d", p=P)).then_inc(dma["lA"], 16)
            sp.dma_start(bias16[:, :], row(bias16_in).to_broadcast([P, D])).then_inc(dma["bias"], 16)
            sp.dma_start(bb_raw[:, :], bb.rearrange("(p j) -> p j", j=KC)).then_inc(dma["bb"], 16)
            sp.dma_start(lB_raw.rearrange("p a j r -> p a (j r)"),
                         lora_B.rearrange("a (p j) r -> p a (j r)", j=KC)).then_inc(dma["lB"], 16)
            sp.dma_start(bz[:, :], row(b)[:, 0:NE].to_broadcast([P, NE])).then_inc(dma["bz_in"], 16)
            sp.dma_start(lrow[:, :], LiMEs.unsqueeze(0).to_broadcast([P // NE, NE, R32])).then_inc(dma["lrow"], 16)
            sp.wait_ge(s_Wb_lo, KC)
            load_x(1)
            sp.wait_ge(s_setup_ps, 2 * KC)
            load_x(2)
            sp.wait_ge(s_lB_lo, KC)
            load_x(3)

            sp.wait_ge(s_deq, 1)
            sp.dma_start(bm_raw, Bmat.unsqueeze(0).to_broadcast([BT, R32, D])).then_inc(dma["Bm"], 16)

            def stores(n):
                if n.on(2):
                    sp.wait_ge(s_x1, n.tile(2, 1))
                    sp.dma_start(x_all[:, n.tile(2), :], x1s[:, n.par(2), :]).then_inc(s_x1st[n.par(2)], 16)
                if n.on(3):
                    sp.wait_ge(s_hT, n.tile(3, 1))
                    sp.dma_start(xT_all[:, n.tile(3), :, :].bitcast(F32), xT[:, n.par(3), :, :].bitcast(F32)).then_inc(s_xTst[n.par(3)], 16)

            def store_L_z():
                sp.wait_ge(s_Lz, 1)
                sp.dma_start(L_z_dram.rearrange("(m p) w -> p m w", p=P),
                             Lz_st.rearrange("p m s w -> p m (s w)").bitcast(F32)).then_inc(s_Lz_st, 16)

            def store_L(m):
                rows = slice(m * P, (m + 1) * P)
                sp.wait_ge(s_setup_lo, 2 * KC + m + 1)
                sp.dma_start(L_hi_dram[rows, :], L_st[:, m % 2, 0, :].bitcast(F32)).then_inc(s_L_st[m % 2], 16)
                sp.dma_start(L_lo_dram[rows, :], L_st[:, m % 2, 1, :].bitcast(F32)).then_inc(s_L_st[m % 2], 16)

            def store_last_L():
                store_L(3)
                sp.wait_ge(s_bst, 1)
                for m in range(2):
                    sp.wait_ge(s_L_st[m], 32 * KC // 2)

            def two_L():
                store_L_z()
                store_L(0)
                store_L(1)
                sp.wait_ge(s_Bm_split, 1)
                sp.dma_start(crow, row(b).to_broadcast([P, D])).then_inc(dma["crow_in"], 16)

            run_phase_a(sp, stores, {2: two_L, 3: lambda: store_L(2),
                                     4: store_last_L})

            with sp.Fori(0, NT) as t:
                sp.wait_ge(s_out_r, t + 1)
                sp.dma_start(out_rows[bass.ts(t, P), :], x_all[:, t, :]).then_inc(s_out, 16)
            sp.wait_ge(s_out, 16 * NT)

        @block.gpsimd
        def _(pool):
            count = [0]

            def link(ins):
                count[0] += 1
                ins.then_inc(s_pool, 1)
                pool.wait_ge(s_pool, count[0])

            def band(ap, pattern, width, mult=1, base=0):
                link(nc.gpsimd.affine_select(out=ap, in_=ap, compare_op=ALU.is_ge, fill=0.0, base=base,
                                             pattern=pattern, channel_multiplier=mult))
                link(nc.gpsimd.affine_select(out=ap, in_=ap, compare_op=ALU.is_ge, fill=0.0, base=width - 1 - base,
                                             pattern=[[-s, c] for s, c in pattern], channel_multiplier=-mult))

            link(nc.gpsimd.memset(ident[:, :], 0.0))
            nc.gpsimd.affine_select(out=ident[:, :], in_=ident[:, :], compare_op=ALU.not_equal, fill=1.0, base=0,
                                    pattern=[[-1, P]], channel_multiplier=1).then_inc(s_const, 1)
            nc.gpsimd.iota(pid_i[:, 0:1], pattern=[[0, 1]], base=0, channel_multiplier=1)
            nc.gpsimd.memset(m16[:, :, :], 1.0)
            link(nc.gpsimd.memset(m32[:, :], 1.0))
            band(m32[:, :], [[-C, BT]], C)
            band(m16[:, :, :], [[-P // 2, 2], [-RK, BT]], RK)
            pool.sem_inc(s_masks, 1)
            nc.gpsimd.iota(iota16[:, :], pattern=[[1, D]], base=0, channel_multiplier=0,
                           allow_small_or_imprecise_dtypes=True)
            link(nc.gpsimd.memset(W2bd[:, :, :], 0.0))
            pool.sem_inc(s_masks, 1)

            def late_masks():
                nc.gpsimd.memset(hmask[:, :, :], 1.0)
                nc.gpsimd.memset(blk[:, :, :], 1.0)
                pool.wait_ge(s_sp, BSESS)
                nc.gpsimd.memset(ones2, 1.0)
                link(nc.gpsimd.memset(rowsel[:, :], 1.0))
                band(hmask[:, :, :], [[-C, BT], [0, RK]], C)
                band(blk[:, :, :], [[-NE, NT], [0, NE]], NE)
                band(rowsel[:, :], [[-1, 2]], 1, base=-3 * R32)
                pool.sem_inc(s_masks, 1)

            def pool_lo(dst, src, hi, got, done):
                pool.wait_ge(*got)
                nc.gpsimd.tensor_tensor(dst, src, hi.bitcast(F32), ALU.subtract).then_inc(done, 1)

            def split_Wb():
                for j in range(KC):
                    pool_lo(Wbs[:, 1, j, :], Wb_raw[:, j, :], Wbs[:, 0, j, :], (s_Wb_hi, j + 1), s_Wb_lo)

            def split_lB():
                for j in range(KC):
                    pool_lo(lBs[:, 1, j, :].rearrange("p (a r) -> p a r", r=RK), lB_raw[:, :, j, :],
                            lBs[:, 0, j, :].rearrange("p (a r) -> p a r", r=RK), (s_lB_hi, j + 1), s_lB_lo)

            def gather_w(n, s):
                t, par = n.tile(s), n.par(s)
                if n.past(s, 2):
                    pool.wait_ge(s_wg[par], 16 * n.half(s))
                    pool.wait_ge(s_wbd, n.tile(s, -1))
                nc.gpsimd.tensor_copy(idxw[:, par:par + 1], idx_w[:, bass.ds(t, 1)]).then_inc(s_idxw, 1)
                pool.wait_ge(s_idxw, n.tile(s, 1))
                pool.sem_inc(s_gate, 1)
                nc.gpsimd.indirect_dma_start(
                    wsel[:, par, :], None, W_sess.rearrange("s c h -> (s c) h"),
                    bass.IndirectOffsetOnAxis(idxw[:, par:par + 1], 0)).then_inc(s_wg[par], 16)

            def make_wbd(n, s):
                t, par = n.tile(s), n.par(s)
                pool.wait_ge(s_wg[par], 16 * n.half(s, 1))
                if n.past(s, 2):
                    pool.wait_ge(s_hid, 2 * n.tile(s, -1))
                nc.gpsimd.tensor_tensor(
                    wbd[:, par, :, :], wsel[:, par, :].unsqueeze(1).to_broadcast([P, BT, HID]),
                    mch[:, t, :].unsqueeze(2).to_broadcast([P, BT, HID]), ALU.mult).then_inc(s_wbd, 1)

            def gather_a(n, s):
                t, par = n.tile(s), n.par(s)
                if n.past(s, 2):
                    pool.wait_ge(s_hz, n.tile(s, -1))
                for j in range(BT):
                    a = pool.value_load(ids_i[0:1, 2, bass.ds(4 * t + j, 1)], min_val=0, max_val=NA - 1)
                    last = nc.gpsimd.tensor_copy(
                        azv[:, par, :, :, RK * j:RK * j + RK],
                        ATG[:, :, :, bass.ds(a * RK, RK)].rearrange("p s k w -> p k s w"))
                    if j < BT - 1:
                        last.then_inc(s_pool, 1)
                last.then_inc(s_az, 1)

            def gather_lz(n, s):
                t, par = n.tile(s), n.par(s)
                if n.past(s, 2):
                    pool.wait_ge(s_lzd[par], 16 * n.half(s))
                    pool.wait_ge(s_l48, n.tile(s, -1))
                nc.gpsimd.tensor_copy(idxl[:, par:par + 1], idx_l[:, bass.ds(t, 1)]).then_inc(s_idxl, 1)
                pool.wait_ge(s_idxl, n.tile(s, 1))
                pool.sem_inc(s_gate, 1)
                nc.gpsimd.indirect_dma_start(
                    lz[:, par, :].bitcast(F32), None, L_z_dram,
                    bass.IndirectOffsetOnAxis(idxl[:, par:par + 1], 0)).then_inc(s_lzd[par], 16)

            pool.wait_ge(s_ids, 1)
            gather_w(Step(0, 0), 0)
            gather_w(Step(0, 1), 0)
            make_wbd(Step(0, 0), 0)
            split_Wb()
            make_wbd(Step(0, 1), 0)
            late_masks()
            gather_w(Step(0, 2), 0)
            split_lB()
            make_wbd(Step(0, 2), 0)

            def gathers(n):
                if isinstance(n.k, int) and n.c <= 1:
                    return
                if n.on(-1):
                    gather_w(n, -1)
                first_az = isinstance(n.k, int) and n.c == 2
                if first_az:
                    make_wbd(n, -1)
                    pool.wait_ge(s_setup_lo, 2 * KC)
                    gather_a(n, 2)
                    pool.wait_ge(s_Lz_st, 16)
                if n.on(2):
                    gather_lz(n, 2)
                if not first_az:
                    if n.on(2):
                        gather_a(n, 2)
                    if n.on(-1):
                        make_wbd(n, -1)
            run_phase_a(pool, gathers)

            for par in range(2):
                pool.wait_ge(s_lzd[par], 16 * NT // 2)
            pool.wait_ge(s_hz, NT)
            for m in range(2):
                pool.wait_ge(s_L_st[m], 32 * KC // 2)

            def gather_L(t, u, reader=None):
                if reader is not None:
                    pool.wait_ge(s_main, reader)
                nc.gpsimd.tensor_copy(idxl[:, u:u + 1], idx_l[:, bass.ds(t, 1)]).then_inc(s_li, 1)
                pool.wait_ge(s_li, t + 1)
                pool.sem_inc(s_gate, 1)
                nc.gpsimd.indirect_dma_start(L_rows[u][:, 0, :].bitcast(F32), None, L_hi_dram,
                                             bass.IndirectOffsetOnAxis(idxl[:, u:u + 1], 0)).then_inc(s_lhd[u], 16)
                nc.gpsimd.indirect_dma_start(L_rows[u][0:RH, 1, :].bitcast(F32), None, L_lo_dram,
                                             bass.IndirectOffsetOnAxis(idxl[0:RH, u:u + 1], 0)).then_inc(s_lld[u], 16)

            gather_L(0, 0)
            gather_L(1, 1)
            pool.wait_ge(s_Gp, KC)
            nc.gpsimd.memset(zp[:, :, 3, 2:R32], 0.0).then_inc(s_zones, 1)
            nc.gpsimd.memset(zp[:, :, 3, 0:2], 1.0).then_inc(s_zones, 1)
            gather_L(2, 2)
            gather_L(3, 3)
            with pool.Fori(1, NT // 4) as k:
                for u in range(4):
                    gather_L(4 * k + u, u, reader=4 * k + (u - 3))

        @block.scalar
        def _(act):
            def copy(dst, src):
                return nc.scalar.activation(dst, src, ACT.Copy)

            for i, ids in ((1, seq_lens), (3, chan_counts)):
                act.dma_start(ids_i[:, i, :], row(ids).to_broadcast([P, NB])).then_inc(dma["ids"], 16)
            act.dma_start(li_raw, LiMEs).then_inc(dma["li"], 16)
            act.dma_start(fA[:, :, :], A.rearrange("(p j) r -> p j r", j=KC)).then_inc(dma["fA"], 16)
            act.wait_ge(s_masks, 2)
            for h in range(2):
                act.dma_start(W2bd[HID * h:HID * h + HID, h, :], W2).then_inc(dma["w2"], 16)
            act.dma_start(b2col[:, :],
                          b2.rearrange("(n a) -> n a", a=1).unsqueeze(0).to_broadcast([BT, C, 1])).then_inc(dma["w2"], 16)

            def setup_hi(k, dst, src):
                act.wait_ge(s_setup_ps, k + 1)
                copy(dst, src).then_inc(s_setup_hi, 1)

            for j in range(KC):
                setup_hi(j, WT[:, 0, j, :], ps[j % 4][:, :])
            act.wait_ge(dma["Wb"], 16)
            for j in range(KC):
                copy(Wbs[:, 0, j, :], Wb_raw[:, j, :]).then_inc(s_Wb_hi, 1)
            def split_adapters():
                for j in range(KC):
                    setup_hi(KC + j, ATG[:, 0, j, :], A_bank[j][:, :])
                act.wait_ge(dma["lB"], 16)
                for j in range(KC):
                    copy(lBs[:, 0, j, :].rearrange("p (a r) -> p a r", r=RK), lB_raw[:, :, j, :]).then_inc(s_lB_hi, 1)

            def split_L(m):
                if m >= 2:
                    act.wait_ge(s_L_st[m % 2], 32)
                setup_hi(2 * KC + m, L_st[:, m % 2, 0, :], L_bank[m][:, :])

            def G_hi(k):
                act.wait_ge(s_Gp, k + 1)
                act.wait_ge(s_az, NT)
                copy(ATG[:, 0, k, :], G_bank[k][:, :]).then_inc(s_Ghi, 1)

            def gelu(n, p):
                act.wait_ge(s_hid, 2 * n.tile(0) + p + 1)
                if isinstance(n.k, int) and n.c == 0 and p == 0:
                    act.wait_ge(s_sv, BSESS)
                if n.past(0, 1):
                    act.wait_ge(s_cond, n.tile(0))
                nc.scalar.activation(gel[:, p, :], ps_hid[p][:, :], ACT.Gelu,
                                     bias=bsess[:, bass.ds(2 * n.tile(0) + p, 1)]).then_inc(s_gelu, 1)

            def stages(n):
                if n.on(2):
                    act.wait_ge(s_ffn, n.tile(2, 1))
                    if n.past(2, 1):
                        act.wait_ge(s_x1, n.tile(2))
                    copy(f16[:, :], ps_f[:, :]).then_inc(s_f16, 1)
                if n.on(3):
                    act.wait_ge(s_hz, n.tile(3, 1))
                    if n.past(3, 1):
                        act.wait_ge(s_zsum, n.tile(3))
                    copy(zlo[:, :], ps_z[:, AZW:2 * AZW]).then_inc(s_zlo, 1)
                if n.on(0):
                    gelu(n, 0)
                if n.on(2):
                    act.wait_ge(s_xTp, n.tile(2, 1))
                    if n.past(2, 2):
                        act.wait_ge(s_xTst[n.par(2)], 16 * n.half(2))
                        act.wait_ge(s_l48, n.tile(2, -1))
                    copy(xT[:, n.par(2), 0:KC, :].rearrange("p k c -> p (k c)"), ps_x[:, :]).then_inc(s_hi, 1)
                if isinstance(n.k, int) and n.c == NT + 2:
                    G_hi(0)
                    G_hi(1)
                if n.on(3):
                    act.wait_ge(s_hTp, n.tile(3, 1))
                    copy(xT[:, n.par(3), NX - 1, :], ps_s[:, 0:P]).then_inc(s_hT, 1)
                if n.on(0):
                    gelu(n, 1)
            run_phase_a(act, stages, {0: split_adapters, 2: lambda: (split_L(0), split_L(1)), 3: lambda: split_L(2),
                                      4: lambda: split_L(3)})

            G_hi(2)
            G_hi(3)
            act.wait_ge(s_rv, R_LOGITS)
            nc.scalar.activation(rt[:, 1, :], rt[:, 0, :], ACT.Exp).then_inc(s_ra, 1)
            act.wait_ge(s_rv, R_DIFF)
            nc.scalar.activation(rt[:, 3, :], rt[:, 4, :], ACT.Exp, scale=-2.0).then_inc(s_ra, 1)
            def fetch_x(t, u, reader=None):
                if reader is not None:
                    act.wait_ge(s_main, reader)
                copy(xT[:, u % 2, :, :], xT_all[:, bass.ds(t, 1), :, :].rearrange("p t k c -> p (t k) c").bitcast(F32)).then_inc(s_xc, 1)

            def fetch_z(t, u):
                copy(zTu[:, u % 2, :], zT[:, t, :].bitcast(F32)).then_inc(s_zc, 1)

            for par in range(2):
                act.wait_ge(s_xTst[par], 16 * NT // 2)
            fetch_x(4, 0)
            fetch_x(5, 1)
            for q in range(4):
                act.wait_ge(s_zTp, q + 1)
                copy(zT[:, 4 * q:4 * q + 4, :].rearrange("p t c -> p (t c)"), z_banks[q % 2][:, :]).then_inc(s_zTs, 1)
            act.wait_ge(s_zTs, 4)
            fetch_z(4, 0)
            fetch_z(5, 1)
            with act.Fori(1, NT // 4 - 1) as k:
                for u in range(4):
                    fetch_x(4 * k + (u + 2), u, reader=4 * k + (u + 1))
                    fetch_z(4 * k + (u + 2), u)
            for t in range(NT - 2, NT):
                fetch_x(t, t, reader=t - 1)
                fetch_z(t, t)

        @block.vector
        def _(dve):
            count = [0]

            def link(ins):
                count[0] += 1
                ins.then_inc(s_chain, 1)
                dve.wait_ge(s_chain, count[0])

            def tt(o, a, bb_, op):
                return nc.vector.tensor_tensor(o, a, bb_, op)

            def ts_(o, a, s1, s2, op0, op1=None):
                return nc.vector.tensor_scalar(o, a, s1, s2, op0, op1) if op1 is not None else \
                    nc.vector.tensor_scalar(o, a, s1, None, op0)

            def stt(o, a, s, c, op0, op1):
                return nc.vector.scalar_tensor_tensor(out=o, in0=a, scalar=s, in1=c, op0=op0, op1=op1)

            def lo_of(dst, src, hi):
                return tt(dst, src, hi.bitcast(F32), ALU.subtract)

            dve.wait_ge(s_masks, 1)
            nc.vector.tensor_copy(ident16[:, :], ident[:, :]).then_inc(s_const, 1)
            link(ts_(pid_i[:, 1:2], pid_i[:, 0:1], C - 1, None, ALU.bitwise_and))
            link(ts_(pid_i[:, 2:3], pid_i[:, 0:1], RK - 1, None, ALU.bitwise_and))
            link(ts_(pid_i[:, 3:4], pid_i[:, 0:1], 1, None, ALU.bitwise_and))
            link(nc.vector.tensor_copy(pid_f[:, :], pid_i[:, :]))
            link(nc.vector.tensor_copy(oddp[:, :], pid_f[:, 3:4]))
            link(nc.vector.tensor_copy(m4[:, :, :], m32[:, :].unsqueeze(1).to_broadcast([P, 4, BT])))
            link(tt(m4[:, 2, :], m16[:, 0, :], m16[:, 1, :], ALU.add))
            dve.wait_ge(dma["ids"], 64)
            link(nc.vector.tensor_copy(ids_f[:, :, :], ids_i[:, :, :]))
            link(tt(sel_terms, ids_f[:, :, :].rearrange("p i (t j) -> p i t j", j=BT),
                    m4[:, :, :].unsqueeze(2).to_broadcast([P, 4, NT, BT]), ALU.mult))
            link(nc.vector.tensor_reduce(sel[:, 0:4, :], sel_terms, AX.X, ALU.add))
            link(ts_(sel[:, 4, :], sel[:, 0, :], float(C), pid_f[:, 1:2], ALU.mult, ALU.add))
            link(nc.vector.tensor_copy(idx_w[:, :], sel[:, 4, :]))
            link(ts_(sel[:, 4, :], sel[:, 2, :], float(RK), pid_f[:, 2:3], ALU.mult, ALU.add))
            link(nc.vector.tensor_copy(idx_l[:, :], sel[:, 4, :]))
            link(ts_(sel[:, 4, :], sel[:, 3, :], pid_f[:, 1:2], None, ALU.is_gt))
            tt(mch[:, :, :], sel[:, 4, :].unsqueeze(2).to_broadcast([P, NT, BT]),
               m32[:, :].unsqueeze(1).to_broadcast([P, NT, BT]), ALU.mult).then_inc(s_ids, 1)
            ts_(onehot[:, :], ids_f[0:NS, 0, :], pid_f[0:NS, 0:1], None, ALU.is_equal).then_inc(s_ids, 1)

            def setup_lo(k, dst, src, hi, eng_sem=s_setup_lo):
                dve.wait_ge(s_setup_hi, k + 1)
                lo_of(dst, src, hi).then_inc(eng_sem, 1)

            dve.wait_ge(s_sp, 1)
            nc.vector.tensor_copy(bsess[:, :], ps_s[:, 0:2 * NT]).then_inc(s_sv, 1)
            for j in range(KC):
                setup_lo(j, WT[:, 1, j, :], ps[j % 4][:, :], WT[:, 0, j, :])

            dve.wait_ge(s_sp, 2)
            link(nc.vector.tensor_copy(liT[:, :], ps_z[0:R32, 0:NE]))
            nc.vector.tensor_copy(fAT[:, :, :].rearrange("r j p -> r (j p)"), ps_s[0:R32, :]).then_inc(s_sv, 1)
            for part in range(2):
                nc.vector.tensor_copy(Rz[:, part, :, 0:NE], WT[:, part, :, 0:NE].bitcast(F32))
                nc.vector.memset(Rz[:, part, :, NZ:ZW].bitcast(F32), 0.0)
            link(nc.vector.tensor_copy(Rz[:, 0, :, 2 * NE:NZ], fA[:, :, :]))
            link(lo_of(Rz[:, 1, :, 2 * NE:NZ], fA[:, :, :], Rz[:, 0, :, 2 * NE:NZ]))
            dve.wait_ge(dma["qz"], 32)
            for e in range(8):
                last = ts_(qz_nib[:, e, :], qz_i[:, :], 4 * e, 15, ALU.logical_shift_right, ALU.bitwise_and)
            link(last)
            nc.vector.tensor_copy(zero16[:, :].rearrange("p (m e) -> p e m", e=8), qz_nib)
            dve.wait_ge(dma["q"], 16)
            link(ts_(q_i[64:P, :], q_i[64:P, :], 4, None, ALU.logical_shift_right))
            dve.wait_ge(s_sp, 3)
            d2 = ps_s[:, 0:KC * NE].rearrange("p (j e) -> p j e", e=NE)
            link(nc.vector.tensor_copy(Rz[:, 0, :, NE:2 * NE], d2))
            lo_of(Rz[:, 1, :, NE:2 * NE], d2, Rz[:, 0, :, NE:2 * NE]).then_inc(s_sv, 1)
            dve.wait_ge(dma["sc"], 32)
            link(ts_(q_nib[0], q_i, 0, 15, ALU.logical_shift_right, ALU.bitwise_and))
            for c in range(KC):
                link(tt(f16[:, :], q_nib[c % 2], zero16[:, :], ALU.subtract))
                if c < KC - 1:
                    ts_(q_nib[(c + 1) % 2], q_i, 8 * (c + 1), 15, ALU.logical_shift_right, ALU.bitwise_and)
                w = tt(W16[:, c, :], f16[:, :], scale16[:, :], ALU.mult)
                if c < KC - 1:
                    link(w)
                else:
                    w.then_inc(s_deq, 1)
            def lora_and_G_z():
                for j in range(KC):
                    setup_lo(KC + j, ATG[:, 1, j, :], A_bank[j][:, :], ATG[:, 0, j, :])
                dve.wait_ge(s_sp, GZT)
                nc.vector.tensor_copy(G_zT, ps_s[0:ZW, :]).then_inc(s_sv, 1)

            def G_z_and_L_z():
                dve.wait_ge(s_sp, GZ)
                gz = ps_s[:, 0:KC * ZW].rearrange("p (k w) -> p k w", w=ZW)
                for par in range(2):
                    link(nc.vector.tensor_copy(azv[:, par, :, 0, RH:AZW], gz))
                    g = lo_of(azv[:, par, :, 1, RH:AZW], gz, azv[:, par, :, 0, RH:AZW])
                    if par == 0:
                        link(g)
                    else:
                        g.then_inc(s_sv, 1)

                dve.wait_ge(dma["bb"], 16)
                bbw = bb_raw[:, :].unsqueeze(2).to_broadcast([P, KC, P])
                link(nc.vector.tensor_copy(bbB[:, 0, :, :], bbw))
                tt(bbB[:, 1, :, :], bbw, bbB[:, 0, :, :].bitcast(F32), ALU.subtract).then_inc(s_bbB, 1)
                dve.wait_ge(s_lzp, 1)
                nc.vector.tensor_copy(L_zT, ps_z[0:ZW, :]).then_inc(s_lzT, 1)

            def L_z():
                dve.wait_ge(s_lzp, 2)
                lzp = ps_z[:, 0:KC * ZW].rearrange("p (m w) -> p m w", w=ZW)
                link(nc.vector.tensor_copy(Lz_st[:, :, 0, :], lzp))
                lo_of(Lz_st[:, :, 1, :], lzp, Lz_st[:, :, 0, :]).then_inc(s_Lz, 1)

            def split_L(m):
                if m >= 2:
                    dve.wait_ge(s_L_st[m % 2], 32)
                setup_lo(2 * KC + m, L_st[:, m % 2, 1, :], L_bank[m][:, :], L_st[:, m % 2, 0, :])

            def two_L():
                L_z()
                split_L(0)
                dve.wait_ge(s_sp, CZ)
                dve.wait_ge(dma["bz_in"], 16)
                link(nc.vector.tensor_copy(cz[:, :], ps_z[:, 0:NZ]))
                tt(cz[:, 0:NE], cz[:, 0:NE], bz[:, :], ALU.add).then_inc(s_sv, 1)
                dve.wait_ge(dma["Bm"], 16)
                link(ts_(bm_raw[:, :], bm_raw[:, :], 0.5, None, ALU.mult))
                link(nc.vector.tensor_copy(Bstk[:, :], bm_raw[:, :]))
                lo_of(Bstk[P // 2:P, :], bm_raw[P // 2:P, :], Bstk[P // 2:P, :]).then_inc(s_Bm_split, 1)
                split_L(1)

            def constant_row_and_L():
                dve.wait_ge(s_sp, CROW)
                dve.wait_ge(dma["crow_in"], 16)
                tt(crow, crow, ps_z[:, :], ALU.add).then_inc(s_sv, 1)
                split_L(2)

            def last_L():
                dve.wait_ge(s_sv, CROW)
                last = slice(3 * R32, P)
                link(nc.vector.tensor_copy(f32r_row[last, :], crow[last, :]))
                link(lo_of(crow[last, :], crow[last, :], f32r_row[last, :]))
                link(ts_(crow[last, :], crow[last, :], rowsel[last, 1:2], None, ALU.mult))
                stt(Bstk[last, :], f32r_row[last, :].bitcast(F32), rowsel[last, 0:1], crow[last, :],
                    ALU.mult, ALU.add).then_inc(s_bst, 1)
                split_L(3)

            dve.wait_ge(dma["w2"], 16 * 3)
            dve.wait_ge(dma["bias"], 16)
            dve.wait_ge(s_masks, 3)

            def G_lo(k):
                dve.wait_ge(s_Ghi, k + 1)
                lo_of(ATG[:, 1, k, :], G_bank[k][:, :], ATG[:, 0, k, :]).then_inc(s_Glo, 1)

            def stages(n):
                if n.on(2):
                    dve.wait_ge(s_f16, n.tile(2, 1))
                    tt(f16[:, :], f16[:, :], bias16[:, :], ALU.add).then_inc(s_b16, 1)
                if n.on(3):
                    if n.past(3, 1):
                        dve.wait_ge(s_zh, n.tile(3))
                    dve.wait_ge(s_zlo, n.tile(3, 1))
                    tt(zsum[:, :], ps_z[:, 0:AZW], zlo[:, :], ALU.add).then_inc(s_zsum, 1)
                if n.on(2):
                    t, par = n.tile(2), n.par(2)
                    dve.wait_ge(s_b16, n.tile(2, 1))
                    if n.past(2, 2):
                        dve.wait_ge(s_x1st[par], 16 * n.half(2))
                        dve.wait_ge(s_xTp, n.tile(2, -1))
                    tt(x1s[:, par, :], x_all[:, t, :], f16[:, :], ALU.add).then_inc(s_x1, 1)
                if n.on(3):
                    dve.wait_ge(s_zsum, n.tile(3, 1))
                    tt(hmf[:, :], zsum[:, 0:RH], hmask[:, :, :].rearrange("p j r -> p (j r)"), ALU.mult).then_inc(s_hm, 1)
                if n.on(1):
                    t = n.tile(1)
                    dve.wait_ge(s_mask, n.tile(1, 1))
                    dve.wait_ge(s_cond, n.tile(1, 1))
                    if n.past(1, 1):
                        dve.wait_ge(s_ctp, t)
                    stt(c16[:, :].rearrange("p (e w) -> p w e", e=8), ps_c[:, :].rearrange("p (w e) -> p w e", e=8),
                        b2col[:, :], mask16[:, :].rearrange("p (w e) -> p w e", e=8), ALU.add, ALU.mult).then_inc(s_c16, 1)
                if n.on(3):
                    dve.wait_ge(s_hm, n.tile(3, 1))
                    if n.past(3, 1):
                        dve.wait_ge(s_hTp, n.tile(3))
                    nc.vector.tensor_copy(hs[:, 0, 0:RH].bitcast(F32R), hmf[:, :]).then_inc(s_hh, 1)
                    dve.wait_ge(s_hh, n.tile(3, 1))
                    tt(hs[:, 0, RH:2 * RH], hmf[:, :], hs[:, 0, 0:RH], ALU.subtract).then_inc(s_hs, 1)
                if n.on(1):
                    t = n.tile(1)
                    dve.wait_ge(s_ctp, n.tile(1, 1))
                    if n.past(1, 1):
                        dve.wait_ge(s_ffn, t)
                    nc.vector.tensor_copy(cT16[:, :], ps_ct[:, 0:D]).then_inc(s_cT, 1)
                if n.on(0):
                    if n.past(0, 1):
                        dve.wait_ge(s_c16, n.tile(0))
                    ts_(mask16[:, :], iota16[:, :], sel[:, 1, bass.ds(n.tile(0), 1)], None, ALU.is_lt).then_inc(s_mask, 1)
                if n.on(2):
                    par = n.par(2)
                    dve.wait_ge(s_hi, n.tile(2, 1))
                    lo_of(xT[:, par, KC:2 * KC, :].rearrange("p k c -> p (k c)"), ps_x[:, :],
                          xT[:, par, 0:KC, :].rearrange("p k c -> p (k c)")).then_inc(s_lo, 1)
                if isinstance(n.k, int) and n.c == NT + 2:
                    G_lo(0)
                    G_lo(1)
                if n.on(3):
                    dve.wait_ge(s_l48, n.tile(3, 1))
                    tt(zall[:, n.tile(3), :], zsum[:, RH:RH + NZ], ps_s[:, P:P + NZ], ALU.add).then_inc(s_zh, 1)
            run_phase_a(dve, stages, {0: lora_and_G_z, 1: G_z_and_L_z, 2: two_L, 3: constant_row_and_L, 4: last_L})

            dve.wait_ge(s_zh, NT)
            link(tt(zall[:, :, 0:2 * NE], zall[:, :, 0:2 * NE], cz[:, 0:2 * NE].unsqueeze(1).to_broadcast([P, NT, 2 * NE]), ALU.add))
            for par in range(2):
                dve.wait_ge(s_x1st[par], 16 * NT // 2)
            steps = [0]

            def signal(ins):
                steps[0] += 1
                ins.then_inc(s_rv, 1)
                dve.wait_ge(s_rv, steps[0])

            ne3 = [P, NT, NE]

            def v(i):
                return rt[:, i, :].rearrange("p (t e) -> p t e", e=NE)

            def col(i):
                return rt[:, 7, i * NT:(i + 1) * NT]

            def bc(ap):
                return ap.unsqueeze(2).to_broadcast(ne3)

            Hs, dl = zall[:, :, 0:NE], zall[:, :, NE:2 * NE]
            link(nc.vector.tensor_reduce(small[:, 10:11], Hs, AX.XY, ALU.max, apply_absolute_value=True))
            link(nc.vector.tensor_reduce(small[:, 11:12], dl, AX.XY, ALU.max, apply_absolute_value=True))
            signal(ts_(small[:, 0:2], small[:, 10:12], oddp[:, 0:1], None, ALU.mult))
            G_lo(2)
            dve.wait_ge(s_rp, 1)
            link(nc.vector.tensor_reduce(small[0:2, 2:3], ps_s[0:2, 0:P], AX.X, ALU.max))
            link(ts_(small[0:2, 3:4], small[0:2, 2:3], EPS, None, ALU.max))
            link(nc.vector.reciprocal(small[0:2, 4:5], small[0:2, 3:4]))
            signal(ts_(small[0:2, 6:8], ident[0:2, 0:2], small[0:2, 4:5], 0.5, ALU.mult, ALU.mult))
            G_lo(3)
            dve.wait_ge(s_rp, 2)
            link(nc.vector.tensor_copy(small[:, 8:10], ps_s[:, 0:2]))
            link(ts_(v(0), Hs, small[:, 8:9], None, ALU.mult))
            link(stt(v(0), dl, small[:, 9:10], v(0), ALU.mult, ALU.add))
            link(nc.vector.tensor_reduce(col(0), v(0), AX.X, ALU.max))
            signal(tt(v(0), v(0), bc(col(0)), ALU.subtract))
            dve.wait_ge(s_ra, 1)
            link(nc.vector.tensor_reduce(col(1), v(1), AX.X, ALU.add))
            link(nc.vector.reciprocal(col(2), col(1)))
            link(tt(v(2), v(1), bc(col(2)), ALU.mult))
            link(nc.vector.tensor_reduce(col(3), v(2), AX.X, ALU.max))
            link(tt(v(5), v(2), bc(col(3)), ALU.is_equal))
            link(nc.vector.tensor_reduce(col(4), v(5), AX.X, ALU.add))
            link(stt(v(6), v(5), -2.0, v(2), ALU.mult, ALU.add))
            link(nc.vector.tensor_reduce(col(5), v(6), AX.X, ALU.max))
            link(stt(col(6), col(4), 2.0, col(3), ALU.is_ge, ALU.mult))
            link(tt(col(7), col(5), col(6), ALU.max))
            signal(tt(v(4), v(2), bc(col(7)), ALU.subtract))
            dve.wait_ge(dma["lrow"], 16)
            link(tt(BD.rearrange("p (t r) -> p t r", t=NT), blk[:, :, 0:1].to_broadcast([P, NT, R32]),
                    lrow[:, :].unsqueeze(1).to_broadcast([P, NT, R32]), ALU.mult))
            dve.wait_ge(s_ra, 2)
            link(ts_(v(3), v(3), 1.0, None, ALU.add))
            link(nc.vector.reciprocal(v(4), v(3)))
            link(tt(v(2), v(2), v(4), ALU.mult))
            link(nc.vector.tensor_reduce(col(0), v(2), AX.X, ALU.add))
            link(ts_(col(1), col(0), WEPS, None, ALU.add))
            link(nc.vector.reciprocal(col(2), col(1)))
            signal(tt(v(2), v(2), bc(col(2)), ALU.mult))
            link(tt(zall[:, :, 2 * NE:NZ], zall[:, :, 2 * NE:NZ], cz[:, 2 * NE:NZ].unsqueeze(1).to_broadcast([P, NT, R32]), ALU.add))
            dve.wait_ge(s_rp, 3)
            signal(nc.vector.tensor_copy(rt[:, 5, :].rearrange("p (n a) -> p n a", a=2),
                                         ps_s[:, 0:P].rearrange("p (n a) -> p n a", a=2)[:, :, 1:2].to_broadcast([P, P // 2, 2])))
            dve.wait_ge(s_rp, 4)
            link(tt(zw, zall[:, :, 2 * NE:NZ], ps_z[:, :].rearrange("p (t r) -> p t r", t=NT), ALU.mult))
            dve.wait_ge(s_Gp, KC)
            for q in range(4):
                tiles = slice(4 * q, 4 * q + 4)
                z4 = zw[:, tiles, :].unsqueeze(2)
                nc.vector.tensor_copy(zp[:, tiles, 0:3:2, :].bitcast(F32R), z4.to_broadcast([P, 4, 2, R32])).then_inc(s_zph, 1)
                dve.wait_ge(s_zph, q + 1)
                tt(zp[:, tiles, 1:2, :].bitcast(F32R), z4, zp[:, tiles, 0:1, :], ALU.subtract).then_inc(s_zs, 1)

            def finish(t, u):
                dve.wait_ge(s_main, t + 1)
                tt(x_all[:, t, :], x_all[:, t, :], main_bank[u][:, :], ALU.add).then_inc(s_out_r, 1)

            with dve.Fori(0, NT // 4) as k:
                for u in range(4):
                    finish(4 * k + u, u)

        @block.tensor
        def _(pe):
            mm = nc.tensor.matmul

            def split_product(dst, lhs, rhs, start=True, stop=True):
                n = 0
                for j in range(KC):
                    for a, c in ((0, 0), (0, 1), (1, 0)):
                        last = mm(dst, lhs(a, j), rhs(c, j), start=start and n == 0, stop=stop and n == 3 * KC - 1)
                        n += 1
                return last

            pe.wait_ge(s_const, 1)
            for i in range(2):
                pe.wait_ge(dma[f"W{i}"], 16)
                for j in range(KC):
                    for m in range(2 * i, 2 * i + 2):
                        last = nc.tensor.transpose(ps[j][:, m * P:(m + 1) * P],
                                                   W_raw[i][:, m % 2, :].rearrange("p (c j) -> p j c", j=KC)[:, j, :], ident[:, :])
                    if i == 1:
                        last.then_inc(s_setup_ps, 1)
            pe.wait_ge(s_ids, 2)
            pe.wait_ge(dma["bsess_in"], 16)
            oh = onehot[:, :].rearrange("s (n a) -> s a n", a=2)
            for a in range(2):
                last = mm(ps_s[HID * a:HID * a + HID, 0:2 * NT], b_raw[:, :], oh[:, a, :], start=True, stop=True)
            last.then_inc(s_sp, 1)
            pe.wait_ge(dma["li"], 16)
            pe.wait_ge(dma["fA"], 16)
            pe.wait_ge(s_sv, BSESS)
            nc.tensor.transpose(ps_z[0:R32, 0:NE], li_raw[:, :], ident[0:NE, 0:NE])
            for j in range(KC):
                last = nc.tensor.transpose(ps_s[0:R32, j * P:(j + 1) * P], fA[:, j, :], ident[:, :])
            last.then_inc(s_sp, 1)
            pe.wait_ge(s_sv, LIT)
            for j in range(KC):
                last = mm(ps_s[:, j * NE:(j + 1) * NE], fAT[:, j, :], liT[:, :], start=j == 0, stop=j == KC - 1,
                          skip_group_check=True)
            last.then_inc(s_sp, 1)

            def lora_and_G_z():
                pe.wait_ge(dma["lA"], 16)
                pe.wait_ge(s_setup_lo, KC)
                for k in range(KC):
                    for m in range(KC):
                        last = nc.tensor.transpose(A_bank[k][:, m * P:(m + 1) * P], lA_raw[:, m, k * P:(k + 1) * P], ident[:, :])
                    last.then_inc(s_setup_ps, 1)
                pe.wait_ge(s_sv, D2)
                pe.wait_ge(s_Wb_lo, KC)
                split_product(ps_s[0:ZW, :], lambda a, j: Rz[:, a, j, :], lambda a, j: Wbs[:, a, j, :]).then_inc(s_sp, 1)

            def back(bank, src):
                for m in range(KC):
                    last = nc.tensor.transpose(bank[:, m * ZW:(m + 1) * ZW], src[:, m * P:(m + 1) * P], ident[0:ZW, 0:ZW])
                return last

            def L_z():
                pe.wait_ge(s_sv, GZT)
                back(ps_s, G_zT).then_inc(s_sp, 1)
                pe.wait_ge(s_lB_lo, KC)
                split_product(ps_z[0:ZW, :], lambda a, j: Rz[:, a, j, :], lambda a, j: lBs[:, a, j, :]).then_inc(s_lzp, 1)

            def L(m):
                rows = slice(m * P, (m + 1) * P)
                split_product(L_bank[m][:, :], lambda a, j: lBs[:, a, j, rows],
                              lambda a, j: WT[:, a, j, :]).then_inc(s_setup_ps, 1)

            def two_L():
                pe.wait_ge(s_lzT, 1)
                back(ps_z, L_zT).then_inc(s_lzp, 1)
                pe.wait_ge(s_sv, GZ)
                L(0)
                pe.wait_ge(s_bbB, 1)
                pe.wait_ge(s_Lz, 1)
                split_product(ps_z[:, 0:ZW], lambda a, j: bbB[:, a, j, :], lambda a, j: Rz[:, a, j, :]).then_inc(s_sp, 1)
                pe.wait_ge(s_lo, 1)
                L(1)
                pe.wait_ge(s_sv, CZ)

            def constant_row_and_L():
                pe.wait_ge(s_zsum, 1)
                split_product(ps_z[:, :], lambda a, j: bbB[:, a, j, :], lambda a, j: WT[:, a, j, :]).then_inc(s_sp, 1)
                pe.wait_ge(s_zh, 1)
                L(2)
                pe.wait_ge(s_sv, CROW)

            def last_L():
                pe.wait_ge(s_zh, 2)
                L(3)

            pe.wait_ge(dma["x0"], 16)

            def hidden(n, p):
                t = n.tile(0)
                if p == 0:
                    pe.wait_ge(s_wbd, n.tile(0, 1))
                if n.past(0, 1):
                    pe.wait_ge(s_gelu, 2 * t + (p - 1))
                mm(ps_hid[p][:, :], wbd[:, n.par(0), 2 * p:2 * p + 2, :].rearrange("p a h -> p (a h)"),
                   x_all[:, t, :], start=True, stop=True).then_inc(s_hid, 1)

            def G_part(n, at, k, parts):
                if isinstance(n.k, int) and n.c == at:
                    for j in parts:
                        for a, c in ((0, 0), (0, 1), (1, 0)):
                            last = mm(G_bank[k][:, :], Wbs[:, a, j, k * P:(k + 1) * P], WT[:, c, j, :],
                                      start=j == 0 and a == c, stop=j == KC - 1 and a == 1)
                    if KC - 1 in parts:
                        last.then_inc(s_Gp, 1)

            def stages(n):
                if isinstance(n.k, int) and n.c == NT:
                    pe.wait_ge(s_gelu, 2 * NT)
                if isinstance(n.k, int) and n.c == NT + 2:
                    pe.wait_ge(s_c16, NT)
                if isinstance(n.k, int) and n.c == 1:
                    pe.wait_ge(dma["w2"], 16 * 3)
                    pe.wait_ge(s_const, 2)
                    pe.wait_ge(s_deq, 1)
                if isinstance(n.k, int) and n.c == 4:
                    for g in ("x1", "x2", "x3"):
                        pe.wait_ge(dma[g], 16)
                if n.on(3):
                    t, par = n.tile(3), n.par(3)
                    pe.wait_ge(s_lo, n.tile(3, 1))
                    pe.wait_ge(s_az, n.tile(3, 1))
                    if n.past(3, 1):
                        pe.wait_ge(s_zsum, t)
                    for k in range(KC):
                        if k == KC - 1:
                            for kk in range(KC):
                                mm(ps_z[:, 0:AZW], xT[:, par, KC + kk, :], azv[:, par, kk, 0, :],
                                   start=False, stop=False, skip_group_check=True)
                        last = mm(ps_z[:, 0:2 * AZW], xT[:, par, k, :], azv[:, par, k, :, :].rearrange("p s w -> p (s w)"),
                                  start=k == 0, stop=k == KC - 1, skip_group_check=True)
                    last.then_inc(s_hz, 1)
                if n.on(1):
                    t = n.tile(1)
                    pe.wait_ge(s_gelu, 2 * t + 2)
                    if n.past(1, 1):
                        pe.wait_ge(s_c16, t)
                    else:
                        pe.wait_ge(s_setup_lo, KC + 1)
                    for p in range(2):
                        last = mm(ps_c[2 * C * p:2 * C * p + 2 * C, :], W2bd[:, :, :].rearrange("p a s -> p (a s)"),
                                  gel[:, p, :], start=True, stop=True)
                    last.then_inc(s_cond, 1)
                if n.on(0):
                    hidden(n, 0)
                G_part(n, NT, 0, (0,))
                G_part(n, NT + 1, 1, (0, 1, 2))
                if n.on(2):
                    t, par = n.tile(2), n.par(2)
                    pe.wait_ge(s_x1, n.tile(2, 1))
                    if n.past(2, 1):
                        pe.wait_ge(s_lo, t)
                    if isinstance(n.k, int) and n.c == 3:
                        pe.wait_ge(s_setup_lo, 2 * KC + 2)
                    for k in range(KC):
                        last = nc.tensor.transpose(ps_x[:, k * P:(k + 1) * P], x1s[:, par, k * P:(k + 1) * P], ident[:, :])
                    last.then_inc(s_xTp, 1)
                G_part(n, NT, 0, (1,))
                if n.on(1):
                    t = n.tile(1)
                    pe.wait_ge(s_c16, n.tile(1, 1))
                    if n.past(1, 1):
                        pe.wait_ge(s_cT, t)
                    for c in range(KC):
                        last = nc.tensor.transpose(ps_ct[:, c * P:(c + 1) * P], c16[:, c * P:(c + 1) * P], ident16[:, :])
                    last.then_inc(s_ctp, 1)
                if n.on(0):
                    hidden(n, 1)
                G_part(n, NT, 0, (2,))
                G_part(n, NT + 2, 2, (0, 1, 2))
                if n.on(3):
                    pe.wait_ge(s_hs, n.tile(3, 1))
                    if n.past(3, 1):
                        pe.wait_ge(s_zh, n.tile(3))
                        pe.wait_ge(s_setup_lo, 3 * KC - 1 if isinstance(n.k, int) and n.c == 4 else 3 * KC)
                    nc.tensor.transpose(ps_s[:, 0:P], hs[:, 0, :], ident[:, :]).then_inc(s_hTp, 1)
                G_part(n, NT, 0, (3,))
                G_part(n, NT + 1, 1, (3,))
                G_part(n, NT + 2, 2, (3,))
                if n.on(1):
                    t = n.tile(1)
                    pe.wait_ge(s_cT, n.tile(1, 1))
                    if n.past(1, 1):
                        pe.wait_ge(s_f16, t)
                    else:
                        pe.wait_ge(s_setup_lo, 2 * KC)
                    for c in range(KC):
                        last = mm(ps_f[:, :], cT16[:, c * P:(c + 1) * P], W16[:, c, :], start=c == 0, stop=c == KC - 1)
                    last.then_inc(s_ffn, 1)
                if n.on(3):
                    par = n.par(3)
                    pe.wait_ge(s_hT, n.tile(3, 1))
                    pe.wait_ge(s_lzd[par], 16 * n.half(3, 1))
                    for c in range(2):
                        last = mm(ps_s[:, P:P + ZW], xT[:, par, NX - 1, :], lz[:, par, c * ZW:(c + 1) * ZW],
                                  start=c == 0, stop=c == 1, skip_group_check=True)
                    last.then_inc(s_l48, 1)
            run_phase_a(pe, stages, {0: lora_and_G_z, 1: L_z, 2: two_L, 3: constant_row_and_L, 4: last_L})

            def main_x(u, operands, chunks=range(KC), wait_G=False):
                for j in chunks:
                    if wait_G:
                        pe.wait_ge(s_Glo, j + 1)
                    for a, c in ((0, 0), (0, 1), (1, 0)):
                        mm(main_bank[u][:, :], operands[:, a * KC + j, :], ATG[:, c, j, :],
                           start=j == 0 and a == c, stop=False)

            def main_L(k, u, operands):
                dst = main_bank[u][:, :]
                pe.wait_ge(s_lhd[u], 16 * k + 16)
                mm(dst, operands[:, NX - 1, :], L_rows[u][:, 0, :], start=False, stop=False)
                pe.wait_ge(s_lld[u], 16 * k + 16)
                mm(dst, operands[0:RH, NX - 1, :], L_rows[u][0:RH, 1, :], start=False, stop=False)

            def main_z(u, zt):
                mm(main_bank[u][:, :], zt, Bstk[:, :], start=False, stop=True).then_inc(s_main, 1)

            pe.wait_ge(s_f16, NT)
            G_part(Step(0, 0), 0, 3, range(KC))
            pe.wait_ge(s_rv, R_MAX)
            mm(ps_s[0:2, 0:P], small[:, 0:2], ident[:, :], start=True, stop=True).then_inc(s_rp, 1)
            for par in range(2):
                pe.wait_ge(s_xTst[par], 16 * 2)
            main_x(0, xT_all[:, 0], (0,), wait_G=True)
            pe.wait_ge(s_rv, R_SCALE)
            mm(ps_s[:, 0:2], ones2, small[0:2, 6:8], start=True, stop=True).then_inc(s_rp, 1)
            main_x(0, xT_all[:, 0], range(1, KC), wait_G=True)
            for u in range(1, 4):
                main_x(u, xT_all[:, u])
            pe.wait_ge(s_rv, R_W)
            nc.tensor.transpose(ps_s[:, 0:P], rt[:, 2, :], ident[:, :]).then_inc(s_rp, 1)
            pe.wait_ge(s_rv, R_WT)
            mm(ps_z[:, :], rt[:, 5, :], BD, start=True, stop=True).then_inc(s_rp, 1)
            for u in range(4):
                main_L(0, u, xT_all[:, u])
            pe.wait_ge(s_zones, 2)

            def z_transposes(q):
                pe.wait_ge(s_zs, q + 1)
                if q >= 2:
                    pe.wait_ge(s_zTs, q - 1)
                for i in range(4):
                    last = nc.tensor.transpose(z_banks[q % 2][:, i * P:(i + 1) * P],
                                               zp[:, 4 * q + i, :, :].rearrange("p a r -> p (a r)"), ident[:, :])
                last.then_inc(s_zTp, 1)

            z_transposes(0)
            z_transposes(1)
            z_transposes(2)
            pe.wait_ge(s_bst, 1)
            for u in range(4):
                main_z(u, zT[:, u, :])
            z_transposes(3)
            with pe.Fori(1, NT // 4) as k:
                for u in range(4):
                    pe.wait_ge(s_out_r, 4 * k + (u - 3))
                    pe.wait_ge(s_xc, 4 * k + (u - 3))
                    main_x(u, xT[:, u % 2])
                    main_L(k, u, xT[:, u % 2])
                    pe.wait_ge(s_zc, 4 * k + (u - 3))
                    main_z(u, zTu[:, u % 2, :])


INPUTS = ['x', 'itok_B_0_7', 'itok_B_2182_4065', 'itok_B_6_15', '_lenS',
          'L0_cond_W_sess', 'L0_cond_b_sess', 'L0_cond_W2', 'L0_cond_b2',
          'L0_ffn_qweight', 'L0_ffn_qzeros', 'L0_ffn_scales', 'L0_ffn_bias',
          'L1_cond_base_weight', 'L1_cond_base_bias', 'L1_cond_lora_A_w', 'L1_cond_lora_B_w',
          'L1_ffn_W', 'L1_ffn_b', 'L1_ffn_A', 'L1_ffn_Bmat', 'L1_ffn_LiMEs']


def kernel(**inputs):
    import numpy as np
    import concourse.bacc as bacc
    from concourse.bass_utils import run_bass_kernel_spmd as run

    nc = bacc.Bacc("TRN2", target_bir_lowering=False, num_devices=1)
    arrays, args = {}, []
    for name in INPUTS:
        a = np.ascontiguousarray(inputs[name])
        arrays["in_" + name] = a
        args.append(nc.dram_tensor("in_" + name, a.shape, mybir.dt.from_np(a.dtype), kind="ExternalInput").ap())
    args.append(nc.dram_tensor("out_0", inputs["x"].shape, mybir.dt.float32, kind="ExternalOutput").ap())
    adaln_ffn_program(nc, *args)
    return run(nc, [arrays], core_ids=[0]).results[0]["out_0"]
```
